# Optimizing a Trainium2 kernel written in Bass

```python
import numpy as np
import jax
import jax.numpy as jnp

def _softmax(x, axis=-1):
    return jax.nn.softmax(x, axis=axis)

def _gelu(x):
    return jax.nn.gelu(x, approximate=True)

def _silu(x):
    return jax.nn.silu(x)

def _sigmoid(x):
    return jax.nn.sigmoid(x)

def _layernorm(x, axis=-1, eps=1e-05):
    m = jnp.mean(x, axis=axis, keepdims=True)
    v = jnp.var(x, axis=axis, keepdims=True)
    return (x - m) / jnp.sqrt(v + eps)

def _scatter_add(tgt, idx, src, axis=0):
    return tgt.at[idx].add(src)

def _segment_sum(src, seg, n):
    return jax.ops.segment_sum(src, seg, n)
kernel_name = 'mk_gnn_ffn_d4_gnn_r32_1a2a48'

def setup_inputs(seed: int=0):
    np.random.seed(seed)
    _w = jnp.asarray

    def _rec_inputs():
        import jax
        import jax.numpy as jnp
        _gk = jax.random.key(seed)
        x = -0.0002117 + 1 * jax.random.normal(jax.random.fold_in(_gk, 1), (3125, 256), jnp.float32)
        src = jax.random.randint(jax.random.fold_in(_gk, 2), (50000,), 0, 3125, jnp.int32)
        dst = jax.random.randint(jax.random.fold_in(_gk, 3), (50000,), 0, 3125, jnp.int32)
        _o = jnp.argsort(dst, stable=True)
        src = src[_o]
        dst = dst[_o]
        edge_weight = jax.random.uniform(jax.random.fold_in(_gk, 13), (50000,), jnp.float32, 0.0, 1)
        edge_weight1 = 0.000486536 + 0.999406 * jax.random.normal(jax.random.fold_in(_gk, 14), (50000, 1), jnp.float32)
        return (x, src, dst, edge_weight, edge_weight1)
    x, src, dst, edge_weight, edge_weight1 = _rec_inputs()

    def _L0_gnn_setup():
        import jax, jax.numpy as jnp
        import numpy as np
        N_NODES = 3125
        N_EDGES = 100000
        D_IN = 256
        D_OUT = 256
        key = jax.random.key(seed)
        k_x, k_w, k_v, k_r, k_c = jax.random.split(key, 5)
        x = jax.random.normal(k_x, (N_NODES, D_IN), dtype=jnp.float32)
        W = jax.random.normal(k_w, (D_OUT, D_IN), dtype=jnp.float32) * (1.0 / np.sqrt(D_IN))
        edge_vals = jax.random.uniform(k_v, (N_EDGES,), dtype=jnp.float32)
        edge_row = jax.random.randint(k_r, (N_EDGES,), 0, N_NODES, dtype=jnp.int32)
        edge_col = jax.random.randint(k_c, (N_EDGES,), 0, N_NODES, dtype=jnp.int32)
        return {'x': x, 'W': W, 'edge_vals': edge_vals, 'edge_row': edge_row, 'edge_col': edge_col}
    _L0_gnn_all = _L0_gnn_setup()
    _L0_gnn_in = {k: v for k, v in _L0_gnn_all.items() if k in ('W',)}
    del _L0_gnn_all

    def _L0_ffn_setup():
        import jax, jax.numpy as jnp
        import numpy as np
        E = 8
        K = 2
        D = 256
        H = 512
        DOUT = 256
        EPS = 1e-05
        key = jax.random.key(seed)
        ks = jax.random.split(key, 9)
        s = 0.02
        return {'x': jax.random.normal(ks[0], (4, 256, D), jnp.float32), 'gamma': 1.0 + 0.05 * jax.random.normal(ks[1], (D,), jnp.float32), 'beta': 0.05 * jax.random.normal(ks[2], (D,), jnp.float32), 'Wr': 0.01 * jax.random.normal(ks[3], (D, E), jnp.float32), 'br': jnp.zeros((E,), jnp.float32), 'W1': s * jax.random.normal(ks[4], (E, D, H), jnp.float32), 'b1': s * jax.random.normal(ks[5], (E, H), jnp.float32), 'W2': s * jax.random.normal(ks[6], (E, H, DOUT), jnp.float32), 'b2': s * jax.random.normal(ks[7], (E, DOUT), jnp.float32)}
    _L0_ffn_all = _L0_ffn_setup()
    _L0_ffn_in = {k: v for k, v in _L0_ffn_all.items() if k in ('gamma', 'beta', 'Wr', 'br', 'W1', 'b1', 'W2', 'b2')}
    del _L0_ffn_all

    def _L1_gnn_setup():
        import jax, jax.numpy as jnp
        import numpy as np
        N = 3125
        E = 50000
        IN_DIM = 256
        OUT_DIM = 32
        H = 8
        EPS = 1e-05
        key = jax.random.key(seed)
        k1, k2, k3, k4, k5 = jax.random.split(key, 5)
        h = jax.random.normal(k1, (N, IN_DIM), jnp.float32)
        W = jax.random.normal(k2, (H, OUT_DIM, IN_DIM), jnp.float32) / np.sqrt(IN_DIM)
        gamma = jnp.ones((H, OUT_DIM), jnp.float32)
        beta = jnp.zeros((H, OUT_DIM), jnp.float32)
        src = jax.random.randint(k3, (E,), 0, N, jnp.int32)
        dst = jax.random.randint(k4, (E,), 0, N, jnp.int32)
        e = jax.random.normal(k5, (E, 1), jnp.float32)
        return {'h': h, 'W': W, 'gamma': gamma, 'beta': beta, 'src': src, 'dst': dst, 'e': e}
    _L1_gnn_all = _L1_gnn_setup()
    _L1_gnn_in = {k: v for k, v in _L1_gnn_all.items() if k in ('W', 'gamma', 'beta')}
    del _L1_gnn_all

    def _L1_ffn_setup():
        import math
        import jax, jax.numpy as jnp
        import numpy as np
        CAPACITY_FACTOR = 1.25
        TOP_K = 2
        LN_EPS = 1e-05

        def _layer_norm(x, gamma, beta):
            mu = jnp.mean(x, axis=-1, keepdims=True)
            var = jnp.var(x, axis=-1, keepdims=True)
            return (x - mu) * jax.lax.rsqrt(var + LN_EPS) * gamma + beta
        key = jax.random.key(seed)
        ks = jax.random.split(key, 4)
        B, S, D, F, E = (8, 128, 256, 512, 8)
        x = jax.random.normal(ks[0], (B, S, D), dtype=jnp.float32)
        Wr = jax.random.normal(ks[1], (D, E), dtype=jnp.float32) / np.sqrt(D)
        br = jnp.zeros((E,), jnp.float32)
        W1 = jax.random.normal(ks[2], (E, D, F), dtype=jnp.float32) / np.sqrt(D)
        b1 = jnp.zeros((E, F), jnp.float32)
        W2 = jax.random.normal(ks[3], (E, F, D), dtype=jnp.float32) / np.sqrt(F)
        b2 = jnp.zeros((E, D), jnp.float32)
        gamma = jnp.ones((D,), jnp.float32)
        beta = jnp.zeros((D,), jnp.float32)
        return {'x': x, 'Wr': Wr, 'br': br, 'W1': W1, 'b1': b1, 'W2': W2, 'b2': b2, 'gamma': gamma, 'beta': beta}
    _L1_ffn_all = _L1_ffn_setup()
    _L1_ffn_in = {k: v for k, v in _L1_ffn_all.items() if k in ('Wr', 'br', 'W1', 'b1', 'W2', 'b2', 'gamma', 'beta')}
    del _L1_ffn_all

    def _L2_gnn_setup():
        import jax, jax.numpy as jnp
        import numpy as np
        N_NODES = 50000
        N_EDGES = 15625
        EPS = 1e-05

        def gcn_conv(x, W, b, src, dst, n):
            h = x @ W
            deg = jax.ops.segment_sum(jnp.ones(src.shape[0], h.dtype), dst, num_segments=n) + 1.0
            dinv = deg ** (-0.5)
            coef = dinv[src] * dinv[dst]
            agg = jax.ops.segment_sum(h[src] * coef[:, None], dst, num_segments=n)
            agg = agg + h * (dinv * dinv)[:, None]
            return agg + b

        def layer_norm(x, gamma, beta):
            m = jnp.mean(x, axis=-1, keepdims=True)
            v = jnp.mean(jnp.square(x - m), axis=-1, keepdims=True)
            return (x - m) * jax.lax.rsqrt(v + EPS) * gamma + beta
        key = jax.random.key(seed)
        ks = jax.random.split(key, 8)
        x = jax.random.normal(ks[0], (N_NODES, 256), dtype=jnp.float32)
        edge_index = jax.random.randint(ks[1], (2, N_EDGES), 0, N_NODES, dtype=jnp.int64)

        def lin(k, i, o):
            return jax.random.normal(k, (i, o), dtype=jnp.float32) * (1.0 / np.sqrt(i))
        W1 = lin(ks[2], 256, 1024)
        W2 = lin(ks[3], 1024, 512)
        W3 = lin(ks[4], 512, 256)
        return {'x': x, 'edge_index': edge_index, 'W1': W1, 'b1': jnp.zeros((1024,), jnp.float32), 'g1': jnp.ones((1024,), jnp.float32), 'beta1': jnp.zeros((1024,), jnp.float32), 'W2': W2, 'b2': jnp.zeros((512,), jnp.float32), 'g2': jnp.ones((512,), jnp.float32), 'beta2': jnp.zeros((512,), jnp.float32), 'W3': W3, 'b3': jnp.zeros((256,), jnp.float32), 'g3': jnp.ones((256,), jnp.float32), 'beta3': jnp.zeros((256,), jnp.float32)}
    _L2_gnn_all = _L2_gnn_setup()
    _L2_gnn_in = {k: v for k, v in _L2_gnn_all.items() if k in ('W1', 'b1', 'g1', 'beta1', 'W2', 'b2', 'g2', 'beta2', 'W3', 'b3', 'g3', 'beta3')}
    del _L2_gnn_all

    def _L2_ffn_setup():
        import jax, jax.numpy as jnp
        import numpy as np
        D_MODEL = 256
        EXPERT_DIM = 512
        NUM_EXPERTS = 8
        TOP_K = 2
        SEQ_LEN = 64
        BATCH = 2
        key = jax.random.key(seed)
        ks = jax.random.split(key, 8)
        s = 0.02
        x = jax.random.normal(ks[0], (SEQ_LEN, BATCH, D_MODEL), dtype=jnp.float32)
        Wg = jax.random.normal(ks[1], (D_MODEL, NUM_EXPERTS), dtype=jnp.float32) * s
        bg = jax.random.normal(ks[2], (NUM_EXPERTS,), dtype=jnp.float32) * s
        bias = jnp.zeros((NUM_EXPERTS,), dtype=jnp.float32)
        W1 = jax.random.normal(ks[3], (NUM_EXPERTS, D_MODEL, EXPERT_DIM), dtype=jnp.float32) * s
        b1 = jax.random.normal(ks[4], (NUM_EXPERTS, EXPERT_DIM), dtype=jnp.float32) * s
        W2 = jax.random.normal(ks[5], (NUM_EXPERTS, EXPERT_DIM, D_MODEL), dtype=jnp.float32) * s
        b2 = jax.random.normal(ks[6], (NUM_EXPERTS, D_MODEL), dtype=jnp.float32) * s
        return {'x': x, 'Wg': Wg, 'bg': bg, 'bias': bias, 'W1': W1, 'b1': b1, 'W2': W2, 'b2': b2}
    _L2_ffn_all = _L2_ffn_setup()
    _L2_ffn_in = {k: v for k, v in _L2_ffn_all.items() if k in ('Wg', 'bg', 'bias', 'W1', 'b1', 'W2', 'b2')}
    del _L2_ffn_all

    def _L3_gnn_setup():
        import jax, jax.numpy as jnp
        import numpy as np
        N_NODES = 3125
        N_EDGES = 100000
        IN_FEATS = 256
        OUT_FEATS = 256
        key = jax.random.key(seed)
        k1, k2, k3, k4 = jax.random.split(key, 4)
        x = jax.random.normal(k1, (N_NODES, IN_FEATS), dtype=jnp.float32)
        edge_index = jax.random.randint(k2, (2, N_EDGES), 0, N_NODES, dtype=jnp.int64)
        bound = 1.0 / np.sqrt(2 * IN_FEATS)
        W = jax.random.uniform(k3, (OUT_FEATS, 2 * IN_FEATS), minval=-bound, maxval=bound, dtype=jnp.float32)
        b = jax.random.uniform(k4, (OUT_FEATS,), minval=-bound, maxval=bound, dtype=jnp.float32)
        return {'x': x, 'edge_index': edge_index, 'W': W, 'b': b}
    _L3_gnn_all = _L3_gnn_setup()
    _L3_gnn_in = {k: v for k, v in _L3_gnn_all.items() if k in ('W', 'b')}
    del _L3_gnn_all

    def _L3_ffn_setup():
        import jax, jax.numpy as jnp
        import numpy as np
        NUM_EXPERTS = 8
        TOP_K = 2
        B, S, D = (8, 256, 256)

        def _moe(tokens, router_w, w1, b1, w2, b2):
            N = tokens.shape[0]
            E = router_w.shape[0]
            logits = tokens.astype(jnp.float32) @ router_w.astype(jnp.float32).T
            probs = jax.nn.softmax(logits, axis=-1)
            rw, re = jax.lax.top_k(probs, TOP_K)
            if TOP_K > 1:
                rw = rw / jnp.maximum(rw.sum(-1, keepdims=True), 1e-12)
            rw = rw.astype(tokens.dtype)
            combine = jnp.zeros((N, E), tokens.dtype).at[jnp.arange(N)[:, None], re].set(rw)
            out = tokens
            for e in range(E):
                h = jax.nn.gelu(tokens @ w1[e] + b1[e], approximate=False)
                y = h @ w2[e] + b2[e]
                out = out + combine[:, e:e + 1] * y
            return out
        key = jax.random.key(seed)
        ks = jax.random.split(key, 4)
        scale = 1.0 / np.sqrt(D).astype(np.float32)
        return {'input_embeddings': jax.random.normal(ks[0], (B, S, D), jnp.float32), 'router_w': jax.random.normal(ks[1], (NUM_EXPERTS, D), jnp.float32) * scale, 'w1': jax.random.normal(ks[2], (NUM_EXPERTS, D, D), jnp.float32) * scale, 'b1': jnp.zeros((NUM_EXPERTS, D), jnp.float32), 'w2': jax.random.normal(ks[3], (NUM_EXPERTS, D, D), jnp.float32) * scale, 'b2': jnp.zeros((NUM_EXPERTS, D), jnp.float32)}
    _L3_ffn_all = _L3_ffn_setup()
    _L3_ffn_in = {k: v for k, v in _L3_ffn_all.items() if k in ('router_w', 'w1', 'b1', 'w2', 'b2')}
    del _L3_ffn_all
    return {'x': x, 'src': src, 'dst': dst, 'edge_weight': edge_weight, 'edge_weight1': edge_weight1, 'L0_gnn_W': _L0_gnn_in['W'], 'L0_ffn_gamma': _L0_ffn_in['gamma'], 'L0_ffn_beta': _L0_ffn_in['beta'], 'L0_ffn_Wr': _L0_ffn_in['Wr'], 'L0_ffn_br': _L0_ffn_in['br'], 'L0_ffn_W1': _L0_ffn_in['W1'], 'L0_ffn_b1': _L0_ffn_in['b1'], 'L0_ffn_W2': _L0_ffn_in['W2'], 'L0_ffn_b2': _L0_ffn_in['b2'], 'L1_gnn_W': _L1_gnn_in['W'], 'L1_gnn_gamma': _L1_gnn_in['gamma'], 'L1_gnn_beta': _L1_gnn_in['beta'], 'L1_ffn_Wr': _L1_ffn_in['Wr'], 'L1_ffn_br': _L1_ffn_in['br'], 'L1_ffn_W1': _L1_ffn_in['W1'], 'L1_ffn_b1': _L1_ffn_in['b1'], 'L1_ffn_W2': _L1_ffn_in['W2'], 'L1_ffn_b2': _L1_ffn_in['b2'], 'L1_ffn_gamma': _L1_ffn_in['gamma'], 'L1_ffn_beta': _L1_ffn_in['beta'], 'L2_gnn_W1': _L2_gnn_in['W1'], 'L2_gnn_b1': _L2_gnn_in['b1'], 'L2_gnn_g1': _L2_gnn_in['g1'], 'L2_gnn_beta1': _L2_gnn_in['beta1'], 'L2_gnn_W2': _L2_gnn_in['W2'], 'L2_gnn_b2': _L2_gnn_in['b2'], 'L2_gnn_g2': _L2_gnn_in['g2'], 'L2_gnn_beta2': _L2_gnn_in['beta2'], 'L2_gnn_W3': _L2_gnn_in['W3'], 'L2_gnn_b3': _L2_gnn_in['b3'], 'L2_gnn_g3': _L2_gnn_in['g3'], 'L2_gnn_beta3': _L2_gnn_in['beta3'], 'L2_ffn_Wg': _L2_ffn_in['Wg'], 'L2_ffn_bg': _L2_ffn_in['bg'], 'L2_ffn_bias': _L2_ffn_in['bias'], 'L2_ffn_W1': _L2_ffn_in['W1'], 'L2_ffn_b1': _L2_ffn_in['b1'], 'L2_ffn_W2': _L2_ffn_in['W2'], 'L2_ffn_b2': _L2_ffn_in['b2'], 'L3_gnn_W': _L3_gnn_in['W'], 'L3_gnn_b': _L3_gnn_in['b'], 'L3_ffn_router_w': _L3_ffn_in['router_w'], 'L3_ffn_w1': _L3_ffn_in['w1'], 'L3_ffn_b1': _L3_ffn_in['b1'], 'L3_ffn_w2': _L3_ffn_in['w2'], 'L3_ffn_b2': _L3_ffn_in['b2']}

def reference(x, src, dst, edge_weight, edge_weight1, L0_gnn_W, L0_ffn_gamma, L0_ffn_beta, L0_ffn_Wr, L0_ffn_br, L0_ffn_W1, L0_ffn_b1, L0_ffn_W2, L0_ffn_b2, L1_gnn_W, L1_gnn_gamma, L1_gnn_beta, L1_ffn_Wr, L1_ffn_br, L1_ffn_W1, L1_ffn_b1, L1_ffn_W2, L1_ffn_b2, L1_ffn_gamma, L1_ffn_beta, L2_gnn_W1, L2_gnn_b1, L2_gnn_g1, L2_gnn_beta1, L2_gnn_W2, L2_gnn_b2, L2_gnn_g2, L2_gnn_beta2, L2_gnn_W3, L2_gnn_b3, L2_gnn_g3, L2_gnn_beta3, L2_ffn_Wg, L2_ffn_bg, L2_ffn_bias, L2_ffn_W1, L2_ffn_b1, L2_ffn_W2, L2_ffn_b2, L3_gnn_W, L3_gnn_b, L3_ffn_router_w, L3_ffn_w1, L3_ffn_b1, L3_ffn_w2, L3_ffn_b2):
    import jax
    import jax.numpy as jnp

    def _L0_gnn_ref(x, W, edge_vals, edge_row, edge_col):
        import jax, jax.numpy as jnp
        import numpy as np
        N_NODES = 3125
        N_EDGES = 100000
        D_IN = 256
        D_OUT = 256
        h = x @ W.T
        msgs = edge_vals[:, None] * h[edge_col]
        out = jax.ops.segment_sum(msgs, edge_row, num_segments=N_NODES)
        return out

    def _L0_ffn_ref(x, gamma, beta, Wr, br, W1, b1, W2, b2):
        import jax, jax.numpy as jnp
        import numpy as np
        E = 8
        K = 2
        D = 256
        H = 512
        DOUT = 256
        EPS = 1e-05
        mu = jnp.mean(x, axis=-1, keepdims=True)
        var = jnp.mean(jnp.square(x - mu), axis=-1, keepdims=True)
        xn = (x - mu) * jax.lax.rsqrt(var + EPS) * gamma + beta
        logits = jnp.einsum('bsd,de->bse', xn, Wr) + br
        top_vals, top_idx = jax.lax.top_k(logits, K)
        w = jax.nn.softmax(top_vals, axis=-1)
        w_full = jnp.einsum('bsk,bske->bse', w, jax.nn.one_hot(top_idx, E, dtype=w.dtype))
        y = jnp.zeros(x.shape[:-1] + (DOUT,), x.dtype)
        for e in range(E):
            h = jax.nn.gelu(jnp.einsum('bsd,dh->bsh', xn, W1[e]) + b1[e], approximate=False)
            y_e = jnp.einsum('bsh,hd->bsd', h, W2[e]) + b2[e]
            y = y + y_e * w_full[..., e, None]
        return y

    def _L1_gnn_ref(h, W, gamma, beta, src, dst, e):
        import jax, jax.numpy as jnp
        import numpy as np
        N = 3125
        E = 50000
        IN_DIM = 256
        OUT_DIM = 32
        H = 8
        EPS = 1e-05
        z = jnp.einsum('nd,hod->nho', h, W)
        msg = z[src]
        agg = jax.ops.segment_sum(msg, dst, num_segments=N)
        mean = jnp.mean(agg, axis=0)
        var = jnp.var(agg, axis=0)
        hn = (agg - mean) * jax.lax.rsqrt(var + EPS) * gamma + beta
        hn = jax.nn.elu(hn)
        out = hn.reshape(N, H * OUT_DIM)
        return h + out

    def _L1_ffn_ref(x, Wr, br, W1, b1, W2, b2, gamma, beta):
        import math
        import jax, jax.numpy as jnp
        import numpy as np
        CAPACITY_FACTOR = 1.25
        TOP_K = 2
        LN_EPS = 1e-05

        def _layer_norm(x, gamma, beta):
            mu = jnp.mean(x, axis=-1, keepdims=True)
            var = jnp.var(x, axis=-1, keepdims=True)
            return (x - mu) * jax.lax.rsqrt(var + LN_EPS) * gamma + beta
        B, S, D = x.shape
        E = Wr.shape[1]
        N = B * S
        K = TOP_K
        logits = jnp.mean(x, axis=1) @ Wr + br
        routing_weights = jax.nn.softmax(logits, axis=-1)
        capacity = float(math.ceil(N * CAPACITY_FACTOR / E))
        expected_loads = routing_weights.sum(axis=0) * (N / B)
        scale = jnp.where(expected_loads > capacity, capacity / expected_loads, 1.0)
        routing_weights = jax.nn.softmax(routing_weights * scale, axis=-1)
        rw_tok = jnp.broadcast_to(routing_weights[:, None, :], (B, S, E)).reshape(N, E)
        top_w, top_i = jax.lax.top_k(rw_tok, K)
        top_w = jax.nn.softmax(top_w, axis=-1)
        xf = x.reshape(N, D)
        h = jax.nn.gelu(jnp.einsum('nd,edf->enf', xf, W1) + b1[:, None, :], approximate=False)
        y = jnp.einsum('enf,efd->end', h, W2) + b2[:, None, :]
        w_dense = jnp.zeros((N, E), x.dtype).at[jnp.arange(N)[:, None], top_i].add(top_w)
        out = jnp.einsum('ne,end->nd', w_dense, y).reshape(B, S, D)
        out = _layer_norm(out + x, gamma, beta)
        return out

    def _L2_gnn_ref(x, edge_index, W1, b1, g1, beta1, W2, b2, g2, beta2, W3, b3, g3, beta3):
        import jax, jax.numpy as jnp
        import numpy as np
        N_NODES = 50000
        N_EDGES = 15625
        EPS = 1e-05

        def gcn_conv(x, W, b, src, dst, n):
            h = x @ W
            deg = jax.ops.segment_sum(jnp.ones(src.shape[0], h.dtype), dst, num_segments=n) + 1.0
            dinv = deg ** (-0.5)
            coef = dinv[src] * dinv[dst]
            agg = jax.ops.segment_sum(h[src] * coef[:, None], dst, num_segments=n)
            agg = agg + h * (dinv * dinv)[:, None]
            return agg + b

        def layer_norm(x, gamma, beta):
            m = jnp.mean(x, axis=-1, keepdims=True)
            v = jnp.mean(jnp.square(x - m), axis=-1, keepdims=True)
            return (x - m) * jax.lax.rsqrt(v + EPS) * gamma + beta
        src, dst = (edge_index[0], edge_index[1])
        n = x.shape[0]
        x1 = layer_norm(jax.nn.relu(gcn_conv(x, W1, b1, src, dst, n)), g1, beta1)
        x2 = layer_norm(jax.nn.relu(gcn_conv(x1, W2, b2, src, dst, n)), g2, beta2)
        x3 = layer_norm(jax.nn.relu(gcn_conv(x2, W3, b3, src, dst, n)), g3, beta3)
        return x3

    def _L2_ffn_ref(x, Wg, bg, bias, W1, b1, W2, b2):
        import jax, jax.numpy as jnp
        import numpy as np
        D_MODEL = 256
        EXPERT_DIM = 512
        NUM_EXPERTS = 8
        TOP_K = 2
        SEQ_LEN = 64
        BATCH = 2
        x_flat = x.reshape(-1, D_MODEL)
        gate_logits = x_flat @ Wg + bg + bias
        topk_vals, topk_idx = jax.lax.top_k(gate_logits, TOP_K)
        topk_w = jax.nn.softmax(topk_vals, axis=-1)
        combine = (jax.nn.one_hot(topk_idx, NUM_EXPERTS, dtype=x.dtype) * topk_w[..., None]).sum(axis=1)
        h = jax.nn.relu(jnp.einsum('td,edh->teh', x_flat, W1) + b1)
        y = jnp.einsum('teh,ehd->ted', h, W2) + b2
        out = jnp.einsum('ted,te->td', y, combine)
        return out.reshape(x.shape)

    def _L3_gnn_ref(x, edge_index, W, b):
        import jax, jax.numpy as jnp
        import numpy as np
        N_NODES = 3125
        N_EDGES = 100000
        IN_FEATS = 256
        OUT_FEATS = 256
        dst, src = (edge_index[0], edge_index[1])
        agg = jnp.zeros_like(x).at[dst].set(x[src])
        h = jnp.concatenate((x, agg), axis=-1)
        return h @ W.T + b

    def _L3_ffn_ref(input_embeddings, router_w, w1, b1, w2, b2):
        import jax, jax.numpy as jnp
        import numpy as np
        NUM_EXPERTS = 8
        TOP_K = 2
        B, S, D = (8, 256, 256)

        def _moe(tokens, router_w, w1, b1, w2, b2):
            N = tokens.shape[0]
            E = router_w.shape[0]
            logits = tokens.astype(jnp.float32) @ router_w.astype(jnp.float32).T
            probs = jax.nn.softmax(logits, axis=-1)
            rw, re = jax.lax.top_k(probs, TOP_K)
            if TOP_K > 1:
                rw = rw / jnp.maximum(rw.sum(-1, keepdims=True), 1e-12)
            rw = rw.astype(tokens.dtype)
            combine = jnp.zeros((N, E), tokens.dtype).at[jnp.arange(N)[:, None], re].set(rw)
            out = tokens
            for e in range(E):
                h = jax.nn.gelu(tokens @ w1[e] + b1[e], approximate=False)
                y = h @ w2[e] + b2[e]
                out = out + combine[:, e:e + 1] * y
            return out
        b, s, d = input_embeddings.shape
        tokens = input_embeddings.reshape(b * s, d)
        return _moe(tokens, router_w, w1, b1, w2, b2).reshape(b, s, d)
    edge_index = jnp.stack([src, dst])
    x = x + _L0_gnn_ref(_layernorm(x, axis=-1), L0_gnn_W, edge_weight, src, dst)
    x = x + _L0_ffn_ref(_layernorm(x, axis=-1)[None], L0_ffn_gamma, L0_ffn_beta, L0_ffn_Wr, L0_ffn_br, L0_ffn_W1, L0_ffn_b1, L0_ffn_W2, L0_ffn_b2)[0]
    x = x + _L1_gnn_ref(_layernorm(x, axis=-1), L1_gnn_W, L1_gnn_gamma, L1_gnn_beta, src, dst, edge_weight1)
    x = x + _L1_ffn_ref(_layernorm(x, axis=-1)[None], L1_ffn_Wr, L1_ffn_br, L1_ffn_W1, L1_ffn_b1, L1_ffn_W2, L1_ffn_b2, L1_ffn_gamma, L1_ffn_beta)[0]
    x = x + _L2_gnn_ref(_layernorm(x, axis=-1), edge_index, L2_gnn_W1, L2_gnn_b1, L2_gnn_g1, L2_gnn_beta1, L2_gnn_W2, L2_gnn_b2, L2_gnn_g2, L2_gnn_beta2, L2_gnn_W3, L2_gnn_b3, L2_gnn_g3, L2_gnn_beta3)
    x = x + _L2_ffn_ref(_layernorm(x, axis=-1)[None], L2_ffn_Wg, L2_ffn_bg, L2_ffn_bias, L2_ffn_W1, L2_ffn_b1, L2_ffn_W2, L2_ffn_b2)[0]
    x = x + _L3_gnn_ref(_layernorm(x, axis=-1), edge_index, L3_gnn_W, L3_gnn_b)
    x = x + _L3_ffn_ref(_layernorm(x, axis=-1)[None], L3_ffn_router_w, L3_ffn_w1, L3_ffn_b1, L3_ffn_w2, L3_ffn_b2)[0]
    return x

_drawn_inputs = setup_inputs


def setup_inputs(seed=0):
    import zlib

    import numpy as np

    out = dict(_drawn_inputs(seed))
    spreads = {'L0_ffn_br': (0.0, 0.327),
     'L1_gnn_gamma': (1.0, 0.2),
     'L1_gnn_beta': (0.0, 0.1),
     'L1_ffn_br': (0.0, 0.8),
     'L1_ffn_b1': (0.0, 0.35),
     'L1_ffn_b2': (0.0, 0.1),
     'L1_ffn_gamma': (1.0, 0.2),
     'L1_ffn_beta': (0.0, 0.1),
     'L2_gnn_b1': (0.0, 0.1),
     'L2_gnn_g1': (1.0, 0.2),
     'L2_gnn_beta1': (0.0, 0.1),
     'L2_gnn_b2': (0.0, 0.1),
     'L2_gnn_g2': (1.0, 0.2),
     'L2_gnn_beta2': (0.0, 0.1),
     'L2_gnn_b3': (0.0, 0.1),
     'L2_gnn_g3': (1.0, 0.2),
     'L2_gnn_beta3': (0.0, 0.342),
     'L2_ffn_bias': (0.0, 0.8),
     'L3_ffn_b1': (0.0, 0.8),
     'L3_ffn_b2': (0.0, 0.631)}
    factors = {'L0_ffn_gamma': 8.0,
     'L0_ffn_beta': 8.0,
     'L0_ffn_Wr': 3.41,
     'L0_ffn_b1': 8.0,
     'L0_ffn_b2': 5.669,
     'L2_ffn_Wg': 3.613,
     'L2_ffn_bg': 8.0,
     'L2_ffn_W1': 3.841,
     'L2_ffn_b1': 8.0,
     'L2_ffn_W2': 3.292,
     'L2_ffn_b2': 8.0,
     'L3_gnn_b': 8.0}
    for name, (base, spread) in spreads.items():
        noise = np.random.default_rng([zlib.crc32(name.encode()), seed]).standard_normal(out[name].shape)
        drawn = base * np.exp(spread * noise) if base else spread * noise
        out[name] = jnp.asarray(drawn.astype(out[name].dtype))
    for name, factor in factors.items():
        out[name] = (out[name] * factor).astype(out[name].dtype)
    return out
```

```python
from contextlib import ExitStack, contextmanager

import concourse.bass as bass
from concourse import mybir

F32 = mybir.dt.float32
I32 = mybir.dt.int32
ALU = mybir.AluOpType
ACT = mybir.ActivationFunctionType
AX_X = mybir.AxisListType.X

P = 128
NODES = 3125
EDGES = 50000
D = 256
TILES = -(-NODES // P)
LAST = NODES - (TILES - 1) * P
BATCH = 5
BATCHES = TILES // BATCH
EPS = 1e-5
EXPERTS = 8
LEAD = 64

PER_ROW = -(-EDGES // P)
FULL_ROWS = EDGES // PER_ROW
REST = EDGES - FULL_ROWS * PER_ROW
CHUNKS_NEEDED = (EDGES + TILES * (P - 1)) // P
RING = 8
HALF = RING // 2
CHUNKS = -(-CHUNKS_NEEDED // RING) * RING
SPILL = CHUNKS + 1
SCATTER_STEP = 23
SCATTER_PARTS = (12, 11)
assert PER_ROW % SCATTER_STEP == 0 and TILES % BATCH == 0


class Counter:

    def __init__(self, sem, lead=LEAD):
        self.sem, self.lead = sem, lead
        self.next = lead

    def reserve(self, n):
        base = self.next
        self.next += n
        return base


class Chain:

    def __init__(self, sem):
        self.sem, self.base, self.n = sem, 0, 0

    def mark(self, ins):
        ins.then_inc(self.sem, 1)
        self.n += 1

    def wait(self, eng):
        eng.wait_ge(self.sem, self.base + self.n)

    @contextmanager
    def loop(self, eng, trips, per_trip):
        start = self.base + self.n
        with eng.Fori(0, trips) as i:
            self.base, self.n = start + per_trip * i, 0
            yield i
            assert self.n == per_trip, (self.n, per_trip)
        self.base, self.n = start + per_trip * trips, 0


def tiles5(i, u):
    return bass.ds(i * BATCH + u, 1)


def before(i, u):
    return BATCH * i + (u - 1 if u >= 2 else (-1 if u == 1 else 0))


class Core:

    def __init__(self, nc, ctx, T, out):
        self.nc, self.T, self.out = nc, T, out
        self.ctx = ctx
        self.sems = []
        f = self.sbuf
        self.x = f("x_nodes", [P, TILES, D])
        self.big_a = f("big_a", [P, TILES * 2 * D])
        self.big_b = f("big_b", [P, TILES * 2 * D])
        self.w_area = f("w_area", [P, 7168])
        self.arena = f("arena", [P, 7168])
        self.vec = f("vectors", [P, 2304])
        self.iota = f("iota_row", [P, CHUNKS])
        self.ident = f("ident", [P, P])
        self.ones = f("ones", [P, P])
        self.earlier = self.vec[:, 0:P]
        self.mean = f("mean", [P, TILES])
        self.rstd = f("rstd", [P, TILES])
        self.logits = f("logits", [P, TILES, EXPERTS])[:, :, :]
        self.stat_tmp = f("stat_tmp", [P, 4, 64])
        self.gates = f("gates", [P, TILES, EXPERTS])
        self.cols = f("columns", [P, 64])
        self.dinv = f("dinv", [P, TILES])
        self.last_edge = f("last_edge", [P, TILES])
        self.bank = [ctx.enter_context(nc.psum_tensor(f"bank{b}", [P, 512], F32)) for b in range(8)]
        self.table = nc.dram_tensor("table", [TILES * P, D], F32, kind="Internal").ap()
        self.wide_table = nc.dram_tensor("wide_table", [TILES * P, 2 * D], F32, kind="Internal").ap()
        self.stat_in = f("stat_in", [P, BATCH * 12])
        self.batch_mean = f("batch_mean", [P, 2 * BATCH])
        self.engines = ("tensor", "vector", "scalar", "gpsimd", "sync")
        self.done = {e: ctx.enter_context(nc.semaphore(f"{e}_stages_done")) for e in self.engines}
        self.gate = {e: ctx.enter_context(nc.semaphore(f"{e}_gate")) for e in self.engines}
        self.v = Chain(ctx.enter_context(nc.semaphore("vector_steps")))
        self.a = Chain(ctx.enter_context(nc.semaphore("scalar_steps")))
        self.counters = {}
        self.loads = self.counter("loads_landed")
        self.store = self.counter("stores_landed")
        self.stages = []

    def sbuf(self, name, shape, dt=F32):
        return self.ctx.enter_context(self.nc.sbuf_tensor(name, shape, dt))

    def counter(self, name, lead=LEAD):
        if name not in self.counters:
            self.counters[name] = Counter(self.ctx.enter_context(self.nc.semaphore(name)), lead)
        return self.counters[name]

    def hold(self, eng, name, sem, value):
        eng.wait_ge(sem, value)
        eng.sem_inc(self.gate[name], 1)

    def enter(self, name, eng, n):
        if n > 0:
            for other in self.engines:
                if other != name:
                    eng.wait_ge(self.done[other], n)

    def leave(self, name, eng):
        if name == "sync":
            eng.sem_inc(self.done[name], 1)
        else:
            eng.drain().then_inc(self.done[name], 1)


class Stage:
    def tensor(self, pe):
        pass

    def vector(self, dve):
        pass

    def scalar(self, act):
        pass

    def gpsimd(self, pool):
        pass

    def sync(self, sp):
        pass


class Setup(Stage):

    def __init__(self, c):
        self.c = c
        self.int_row = c.big_b[:, 0:CHUNKS].bitcast(I32)
        self.made = c.counter("constants_made")
        self.m = self.made.reserve(6)
        self.l = c.loads.reserve(32)
        self.cleared = c.counter("cleared")
        self.z = self.cleared.reserve(1)

    def gpsimd(self, pool):
        c = self.c
        pool.iota(self.int_row, [[1, CHUNKS]], base=0, channel_multiplier=0).then_inc(self.made.sem, 1)
        pool.memset(c.ident[:, :], 0.0).then_inc(self.made.sem, 1)
        pool.memset(c.ones[:, :], 1.0).then_inc(self.made.sem, 1)
        pool.memset(c.earlier[:, :], 1.0).then_inc(self.made.sem, 1)
        pool.wait_ge(self.made.sem, self.m + 4)
        pool.affine_select(out=c.ident[:, :], in_=c.ident[:, :], compare_op=ALU.not_equal, fill=1.0,
                           base=0, pattern=[[-1, P]], channel_multiplier=1).then_inc(self.made.sem, 1)
        pool.affine_select(out=c.earlier[:, :], in_=c.earlier[:, :], compare_op=ALU.is_gt, fill=0.0,
                           base=0, pattern=[[1, P]], channel_multiplier=-1).then_inc(self.made.sem, 1)

    def vector(self, dve):
        c = self.c
        dve.memset(c.x[:, TILES - 1, :], 0.0).then_inc(self.cleared.sem, 1)
        dve.wait_ge(self.made.sem, self.m + 1)
        c.v.mark(dve.tensor_copy(c.iota[:, :], self.int_row))

    def sync(self, sp):
        c, whole = self.c, (TILES - 1) * P
        sp.dma_start(c.x[:, 0:TILES - 1, :], c.T["x"][0:whole, :].rearrange("(t p) d -> p t d", p=P)
                     ).then_inc(c.loads.sem, 16)
        sp.wait_ge(self.cleared.sem, self.z + 1)
        sp.dma_start(c.x[0:LAST, TILES - 1, :], c.T["x"][whole:NODES, :]).then_inc(c.loads.sem, 16)
        sp.wait_ge(c.loads.sem, self.l + 32)


class SortEdges(Stage):

    def __init__(self, c, name, key, other, weight):
        self.c, self.name = c, name
        self.key, self.other, self.weight = c.T[key], c.T[other], weight and c.T[weight]
        self.slots = c.nc.dram_tensor(f"{name}_slots", [P, SPILL * 4], F32, kind="Internal").ap()
        self.row = c.sbuf(f"{name}_row", [P, CHUNKS], I32)
        self.node = c.sbuf(f"{name}_node", [P, CHUNKS])
        self.value = weight and c.sbuf(f"{name}_weight", [P, CHUNKS])
        self.tile = c.sbuf(f"{name}_tile", [1, CHUNKS], I32)
        n = [0]

        def part(size):
            n[0] += size
            return c.big_b[:, n[0] - size:n[0]]

        self.key_i, self.other_i, self.low_i, self.high_i, self.id_i, self.slot_i = (
            part(PER_ROW).bitcast(I32) for _ in range(6))
        self.wt, self.high, self.mask, self.position, self.term, self.one = (part(PER_ROW) for _ in range(6))
        self.fill = part(SPILL * 4)
        self.rec = part(PER_ROW * 4)
        self.tile_all = part(CHUNKS)
        self.total, self.chunks, self.ends, self.start = (part(TILES) for _ in range(4))
        self.chunks_i = part(TILES).bitcast(I32)
        assert n[0] <= TILES * 2 * D
        self.scan = c.big_a[:, 0:TILES * PER_ROW]
        self.back = c.big_a[:, 0:CHUNKS * 4]
        self.ring = [c.arena[:, 0:SCATTER_PARTS[0] * 4], c.arena[:, 64:64 + SCATTER_PARTS[1] * 4]]
        self.ring_to = [c.arena[:, 128:128 + SCATTER_PARTS[0]].bitcast(I32),
                        c.arena[:, 160:160 + SCATTER_PARTS[1]].bitcast(I32)]
        self.steps = PER_ROW // SCATTER_STEP
        self.cleared = c.counter("cleared")
        self.z = self.cleared.reserve(1)
        self.ids = c.counter("edge_ids_made")
        self.i0 = self.ids.reserve(1)
        self.filled = c.counter("filling_ready")
        self.f0 = self.filled.reserve(1)
        self.l = c.loads.reserve(16 * (6 if weight else 4))
        self.counted = c.counter("bucket_counts_ready")
        self.k0 = self.counted.reserve(1)
        self.summed = c.counter("bucket_sums_ready")
        self.s0 = self.summed.reserve(1)
        self.slot_filled = c.counter("slots_filled")
        self.g0 = self.slot_filled.reserve(16)
        self.ring_ready = c.counter("scatter_ring_ready")
        self.r0 = self.ring_ready.reserve(2 * self.steps)
        self.scattered = [c.counter(f"edges_scattered{h}", 0) for h in range(2)]
        self.e0 = [s.reserve(16 * self.steps * n) for s, n in zip(self.scattered, SCATTER_PARTS)]
        self.read_back = c.counter("slots_read_back")
        self.b0 = self.read_back.reserve(16)

    def sync(self, sp):
        c = self.c
        sp.wait_ge(self.cleared.sem, self.z + 1)
        pairs = [(self.key_i, self.key), (self.other_i, self.other)]
        if self.weight is not None:
            pairs.append((self.wt, self.weight))
        for to, src in pairs:
            sp.dma_start(to[0:FULL_ROWS, :], src[0:FULL_ROWS * PER_ROW].rearrange("(p j) -> p j", j=PER_ROW)
                         ).then_inc(c.loads.sem, 16)
            sp.dma_start(to[FULL_ROWS:FULL_ROWS + 1, 0:REST],
                         src[FULL_ROWS * PER_ROW:EDGES].rearrange("(p j) -> p j", p=1)).then_inc(c.loads.sem, 16)
        sp.wait_ge(self.filled.sem, self.f0 + 1)
        sp.dma_start(self.slots, self.fill).then_inc(self.slot_filled.sem, 16)
        for h, n in enumerate(SCATTER_PARTS):
            sp.wait_ge(self.scattered[h].sem, self.e0[h] + 16 * self.steps * n)
        sp.dma_start(self.back, self.slots[:, 0:CHUNKS * 4]).then_inc(self.read_back.sem, 16)
        sp.wait_ge(self.read_back.sem, self.b0 + 16)

    def gpsimd(self, pool):
        c = self.c
        pool.iota(self.id_i, [[1, PER_ROW]], base=0, channel_multiplier=PER_ROW).then_inc(self.ids.sem, 1)
        pool.wait_ge(self.slot_filled.sem, self.g0 + 16)
        target = self.slots.rearrange("p (c r) -> (p c) r", r=4)
        with pool.Fori(0, self.steps) as i:
            for h, n in enumerate(SCATTER_PARTS):
                c.hold(pool, "gpsimd", self.ring_ready.sem, self.r0 + 2 * i + h + 1)
                for k in range(n):
                    pool.indirect_dma_start(
                        target, bass.IndirectOffsetOnAxis(ap=self.ring_to[h][:, k:k + 1], axis=0),
                        self.ring[h][:, 4 * k:4 * k + 4], None).then_inc(self.scattered[h].sem, 16)

    def tensor(self, pe):
        c = self.c
        pe.wait_ge(self.counted.sem, self.k0 + 1)
        pe.matmul(c.bank[0][:, 0:TILES], c.earlier[:, :], self.total, start=True, stop=True)
        pe.matmul(c.bank[1][:, 0:TILES], c.ones[:, :], self.total, start=True, stop=True
                  ).then_inc(self.summed.sem, 1)

    def vector(self, dve):
        c, v = self.c, self.c.v
        rec = self.rec.rearrange("p (j r) -> p j r", r=4)
        rec_i = rec.bitcast(I32)
        v.mark(dve.memset(self.other_i, 0))
        v.mark(dve.memset(self.wt, 0.0))
        v.mark(dve.memset(self.one, 1.0))
        v.wait(dve)
        dve.memset(self.key_i, -1).then_inc(self.cleared.sem, 1)
        fill = self.fill.rearrange("p (c r) -> p c r", r=4)
        v.mark(dve.memset(self.fill, 0.0))
        v.wait(dve)
        dve.memset(fill[:, :, 1:2], -1.0).then_inc(self.filled.sem, 1)
        dve.wait_ge(self.ids.sem, self.i0 + 1)
        v.mark(dve.tensor_copy(self.term, self.id_i))
        v.wait(dve)
        v.mark(dve.tensor_scalar(self.mask, self.term, float(EDGES), None, ALU.is_ge))
        v.mark(dve.tensor_scalar(rec[:, :, 3], self.term, 1.0, None, ALU.add))
        v.wait(dve)
        v.mark(dve.scalar_tensor_tensor(out=self.position, in0=self.term, scalar=float(P * CHUNKS - EDGES),
                                        in1=self.mask, op0=ALU.add, op1=ALU.mult))
        dve.wait_ge(c.loads.sem, self.l + 16 * (6 if self.weight is not None else 4))
        v.mark(dve.tensor_scalar(self.high_i, self.key_i, 7, None, ALU.arith_shift_right))
        v.mark(dve.tensor_scalar(self.low_i, self.key_i, P - 1, None, ALU.bitwise_and))
        v.mark(dve.tensor_copy(rec_i[:, :, 0], self.other_i))
        v.mark(dve.tensor_copy(rec[:, :, 2], self.wt))
        v.wait(dve)
        v.mark(dve.tensor_copy(self.high, self.high_i))
        v.mark(dve.tensor_copy(rec[:, :, 1], self.low_i))
        v.wait(dve)
        with v.loop(dve, TILES, 2) as b:
            v.mark(dve.tensor_scalar(self.mask, self.high, c.iota[:, bass.ds(b, 1)], None, ALU.is_equal))
            v.wait(dve)
            v.mark(dve.tensor_tensor_scan(self.scan[:, bass.ds(b * PER_ROW, PER_ROW)], self.one, self.mask,
                                          0.0, ALU.mult, ALU.add))
            v.wait(dve)
        scan = self.scan.rearrange("p (b j) -> p b j", j=PER_ROW)
        dve.tensor_copy(self.total, scan[:, :, PER_ROW - 1]).then_inc(self.counted.sem, 1)
        dve.wait_ge(self.summed.sem, self.s0 + 1)
        v.mark(dve.tensor_scalar(self.chunks_i, c.bank[1][:, 0:TILES], float(P - 1), None, ALU.add))
        v.wait(dve)
        v.mark(dve.tensor_scalar(self.chunks_i, self.chunks_i, 7, None, ALU.arith_shift_right))
        v.wait(dve)
        v.mark(dve.tensor_copy(self.chunks, self.chunks_i))
        v.wait(dve)
        v.mark(dve.tensor_tensor_scan(self.ends, self.one[:, 0:TILES], self.chunks, 0.0, ALU.mult, ALU.add))
        v.wait(dve)
        v.mark(dve.tensor_tensor(self.ends, self.ends, self.chunks, ALU.subtract))
        v.wait(dve)
        v.mark(dve.tensor_scalar(self.start, self.ends, float(P), -1.0, ALU.mult, ALU.add))
        v.wait(dve)
        v.mark(dve.tensor_tensor(self.start, self.start, c.bank[0][:, 0:TILES], ALU.add))
        v.wait(dve)
        with v.loop(dve, TILES, 3) as b:
            v.mark(dve.tensor_scalar(self.mask, self.high, c.iota[:, bass.ds(b, 1)], None, ALU.is_equal))
            v.wait(dve)
            v.mark(dve.scalar_tensor_tensor(out=self.term, in0=self.scan[:, bass.ds(b * PER_ROW, PER_ROW)],
                                            scalar=self.start[:, bass.ds(b, 1)], in1=self.mask,
                                            op0=ALU.add, op1=ALU.mult))
            v.wait(dve)
            v.mark(dve.tensor_tensor(self.position, self.position, self.term, ALU.add))
            v.wait(dve)
        v.mark(dve.tensor_copy(self.slot_i, self.position))
        v.wait(dve)
        v.mark(dve.tensor_scalar(self.high_i, self.slot_i, 7, None, ALU.arith_shift_right))
        v.mark(dve.tensor_scalar(self.low_i, self.slot_i, P - 1, None, ALU.bitwise_and))
        v.wait(dve)
        v.mark(dve.tensor_copy(self.mask, self.high_i))
        v.mark(dve.tensor_copy(self.term, self.low_i))
        v.wait(dve)
        v.mark(dve.scalar_tensor_tensor(out=self.slot_i, in0=self.term, scalar=float(SPILL), in1=self.mask,
                                        op0=ALU.mult, op1=ALU.add))
        v.mark(dve.memset(self.tile_all, 0.0))
        v.wait(dve)
        with v.loop(dve, TILES - 1, 1) as b:
            v.mark(dve.scalar_tensor_tensor(out=self.tile_all, in0=c.iota[:, :], scalar=self.ends[:, bass.ds(b + 1, 1)],
                                            in1=self.tile_all, op0=ALU.is_ge, op1=ALU.add))
            v.wait(dve)
        v.mark(dve.tensor_copy(self.tile[:, :], self.tile_all[0:1, :]))
        at = [0, SCATTER_PARTS[0]]
        v.wait(dve)

        def fill_ring(i, h):
            n, j = SCATTER_PARTS[h], i * SCATTER_STEP + at[h]
            dve.tensor_copy(self.ring[h].rearrange("p (j r) -> p j r", r=4).bitcast(I32),
                            rec_i[:, bass.ds(j, n), :])
            dve.tensor_copy(self.ring_to[h], self.slot_i[:, bass.ds(j, n)]).then_inc(self.ring_ready.sem, 1)

        fill_ring(0, 0)
        fill_ring(0, 1)
        with dve.Fori(1, self.steps) as i:
            for h, n in enumerate(SCATTER_PARTS):
                dve.wait_ge(self.scattered[h].sem, self.e0[h] + 16 * n * i)
                fill_ring(i, h)
        dve.wait_ge(self.read_back.sem, self.b0 + 16)
        back = self.back.rearrange("p (c r) -> p c r", r=4)
        v.mark(dve.tensor_copy(self.row[:, :], back[:, :, 0].bitcast(I32)))
        v.mark(dve.tensor_copy(self.node[:, :], back[:, :, 1]))
        if self.value is not None:
            v.mark(dve.tensor_copy(self.value[:, :], back[:, :, 2]))
            v.mark(dve.tensor_copy(c.big_b[:, 0:CHUNKS], back[:, :, 3]))
        v.wait(dve)


class GatherAdd(Stage):

    def __init__(self, c, edges, width, degree=False):
        self.c, self.edges, self.width, self.degree = c, edges, width, degree
        self.total = width + degree
        self.trips = CHUNKS // RING
        self.sums = c.big_a[:, 0:TILES * self.total].rearrange("p (t d) -> p t d", d=self.total)
        self.rows = c.arena[:, 0:RING * 520].rearrange("p (k d) -> p k d", d=520)
        self.onehot = c.arena[:, RING * 520:RING * 520 + RING * P].rearrange("p (k d) -> p k d", d=P)
        self.ring = c.arena[:, 5500:5500 + RING].bitcast(I32)
        n = self.trips * RING
        self.index_ready = c.counter("gather_index_ready")
        self.i0 = self.index_ready.reserve(2 * self.trips)
        self.landed = [c.counter(f"chunk_landed{k}", 0) for k in range(RING)]
        self.l0 = [s.reserve(16 * self.trips) for s in self.landed]
        self.onehot_ready = c.counter("onehot_ready")
        self.o0 = self.onehot_ready.reserve(n)
        self.summed = c.counter("chunk_summed")
        self.s0 = self.summed.reserve(n)
        self.added = c.counter("chunk_added")
        self.a0 = self.added.reserve(n)
        self.cleared = c.counter("sums_cleared")
        self.z0 = self.cleared.reserve(2)

    def scalar(self, act):
        def fill(i, h):
            act.copy(self.ring[:, h * HALF:(h + 1) * HALF],
                     self.edges.row[:, bass.ds(i * RING + h * HALF, HALF)]).then_inc(self.index_ready.sem, 1)

        fill(0, 0)
        fill(0, 1)
        with act.Fori(1, self.trips) as i:
            for h in range(2):
                for k in range(h * HALF, (h + 1) * HALF):
                    act.wait_ge(self.landed[k].sem, self.l0[k] + 16 * i)
                fill(i, h)

    def gpsimd(self, pool):
        c = self.c
        with pool.Fori(0, self.trips) as i:
            for h in range(2):
                c.hold(pool, "gpsimd", self.index_ready.sem, self.i0 + 2 * i + h + 1)
                c.hold(pool, "gpsimd", self.summed.sem, self.s0 + RING * (i - 1) + (h + 1) * HALF)
                for k in range(h * HALF, (h + 1) * HALF):
                    pool.indirect_dma_start(self.rows[:, k, 0:self.width], None, c.table if self.width == D else c.wide_table,
                                            bass.IndirectOffsetOnAxis(ap=self.ring[:, k:k + 1], axis=0)
                                            ).then_inc(self.landed[k].sem, 16)

    def tensor(self, pe):
        c = self.c
        pe.wait_ge(self.cleared.sem, self.z0 + 2)
        with pe.Fori(0, self.trips) as i:
            for k in range(RING):
                pe.wait_ge(self.onehot_ready.sem, self.o0 + RING * i + k + 1)
                pe.wait_ge(self.landed[k].sem, self.l0[k] + 16 * (i + 1))
                pe.wait_ge(self.added.sem, self.a0 + RING * i + k - 3)
                pe.matmul(c.bank[k % 4][:, 0:self.total], self.onehot[:, k, :], self.rows[:, k, 0:self.total],
                          start=True, stop=True).then_inc(self.summed.sem, 1)

    def vector(self, dve):
        c, e = self.c, self.edges
        dve.memset(c.big_a[:, 0:TILES * self.total], 0.0).then_inc(self.cleared.sem, 1)
        dve.memset(self.rows[:, :, self.width:self.width + 1], 1.0).then_inc(self.cleared.sem, 1)
        dve.wait_ge(self.cleared.sem, self.z0 + 2)

        def select(i, k):
            dve.wait_ge(self.summed.sem, self.s0 + RING * (i - 1) + k + 1)
            at = bass.ds(RING * i + k, 1)
            if e.value is None:
                ins = dve.tensor_scalar(self.onehot[:, k, :], c.iota[:, 0:P], e.node[:, at], None, ALU.is_equal)
            else:
                ins = dve.tensor_scalar(self.onehot[:, k, :], c.iota[:, 0:P], e.node[:, at], e.value[:, at],
                                        ALU.is_equal, ALU.mult)
            ins.then_inc(self.onehot_ready.sem, 1)

        with dve.Fori(0, self.trips) as i:
            for k in range(HALF):
                select(i, k)
            for k in range(RING):
                tile = dve.value_load(e.tile[0:1, bass.ds(RING * i + k, 1)], min_val=0, max_val=TILES - 1)
                dve.wait_ge(self.summed.sem, self.s0 + RING * i + k + 1)
                dve.wait_ge(self.added.sem, self.a0 + RING * i + k)
                into = self.sums[:, bass.ds(tile, 1), :]
                part = c.bank[k % 4][:, 0:self.total].rearrange("p (a d) -> p a d", a=1)
                dve.tensor_tensor(into, into, part, ALU.add).then_inc(self.added.sem, 1)
                if k + HALF < RING:
                    select(i, k + HALF)


class LastEdge(Stage):

    def __init__(self, c, edges):
        self.c, self.edges = c, edges
        self.trips = CHUNKS // RING
        self.tagged = c.arena[:, 0:RING * P].rearrange("p (k d) -> p k d", d=P)
        self.best = c.arena[:, 1024:1024 + CHUNKS]
        self.masked = c.arena[:, 2048:2048 + CHUNKS]
        self.ids = c.big_b[:, 0:CHUNKS]
        self.tagged_ready = c.counter("tagged_ready")
        self.t0 = self.tagged_ready.reserve(2 * self.trips)
        self.turned = c.counter("tagged_turned")
        self.u0 = self.turned.reserve(2 * self.trips)
        self.taken = c.counter("tagged_taken")
        self.k0 = self.taken.reserve(2 * self.trips)

    def tensor(self, pe):
        c = self.c
        with pe.Fori(0, self.trips) as i:
            for h in range(2):
                pe.wait_ge(self.tagged_ready.sem, self.t0 + 2 * i + h + 1)
                pe.wait_ge(self.taken.sem, self.k0 + 2 * i + h - 1)
                for k in range(HALF):
                    ins = pe.transpose(c.bank[h][:, k * P:(k + 1) * P], self.tagged[:, h * HALF + k, :], c.ident[:, :])
                ins.then_inc(self.turned.sem, 1)

    def vector(self, dve):
        c, e, v = self.c, self.edges, self.c.v

        def tag(i, h):
            dve.wait_ge(self.turned.sem, self.u0 + 2 * i + h - 1)
            for k in range(HALF):
                at = bass.ds(RING * i + h * HALF + k, 1)
                ins = dve.tensor_scalar(self.tagged[:, h * HALF + k, :], c.iota[:, 0:P], e.node[:, at],
                                        self.ids[:, at], ALU.is_equal, ALU.mult)
            ins.then_inc(self.tagged_ready.sem, 1)

        with dve.Fori(0, self.trips) as i:
            tag(i, 0)
            tag(i, 1)
            for h in range(2):
                dve.wait_ge(self.turned.sem, self.u0 + 2 * i + h + 1)
                dve.tensor_reduce(self.best[:, bass.ds(RING * i + h * HALF, HALF)],
                                  c.bank[h][:, :].rearrange("p (k d) -> p k d", d=P), AX_X, ALU.max
                                  ).then_inc(self.taken.sem, 1)
        dve.wait_ge(self.taken.sem, self.k0 + 2 * self.trips)
        with v.loop(dve, TILES, 2) as t:
            v.mark(dve.scalar_tensor_tensor(out=self.masked, in0=e.tile_all, scalar=c.iota[:, bass.ds(t, 1)],
                                            in1=self.best, op0=ALU.is_equal, op1=ALU.mult))
            v.wait(dve)
            v.mark(dve.tensor_reduce(c.last_edge[:, bass.ds(t, 1)], self.masked, AX_X, ALU.max))
            v.wait(dve)


class RowStats(Stage):

    def __init__(self, c, src):
        self.c, self.src = c, src
        self.stats = c.arena[:, 0:TILES * 6]
        self.s = Statistics(c, TILES, 2, D)

    def vector(self, dve):
        c, v = self.c, self.c.v
        with v.loop(dve, TILES, 1) as t:
            v.mark(dve.bn_stats(self.stats.rearrange("p (t s) -> p t s", s=6)[:, bass.ds(t, 1), :],
                                self.src[:, bass.ds(t, 1), :]))
        v.wait(dve)
        self.s.vector(dve, self.stats.rearrange("p (t g s) -> p t g s", g=2, s=3), c.mean[:, :], c.rstd[:, :])

    def scalar(self, act):
        self.s.scalar(act)


class Statistics:

    def __init__(self, c, rows, groups, width, uses=1):
        self.c, self.rows, self.groups, self.width = c, rows, groups, width
        n = rows * groups
        self.dev = c.stat_tmp[:, 0, 0:n].rearrange("p (t g) -> p t g", g=groups)
        self.sq = c.stat_tmp[:, 1, 0:n].rearrange("p (t g) -> p t g", g=groups)
        self.var, self.std = c.stat_tmp[:, 2, 0:rows], c.stat_tmp[:, 3, 0:rows]
        self.var_ready = c.counter("variance_ready")
        self.v0 = self.var_ready.reserve(uses)
        self.std_ready = c.counter("deviation_ready")
        self.d0 = self.std_ready.reserve(uses)
        self.STEPS = 7

    def vector(self, dve, stats, mean, rstd, use=0):
        v = self.c.v
        shape = [P, self.rows, self.groups]
        per_group = float(self.width // self.groups)
        v.mark(dve.tensor_reduce(mean, stats[:, :, :, 1], AX_X, ALU.add))
        v.wait(dve)
        v.mark(dve.tensor_scalar(mean, mean, 1.0 / self.groups, None, ALU.mult))
        v.wait(dve)
        v.mark(dve.tensor_tensor(self.dev, stats[:, :, :, 1], mean.unsqueeze(2).broadcast_to(shape), ALU.subtract))
        v.wait(dve)
        v.mark(dve.scalar_tensor_tensor(out=self.sq, in0=self.dev, scalar=per_group, in1=self.dev,
                                        op0=ALU.mult, op1=ALU.mult))
        v.wait(dve)
        v.mark(dve.tensor_tensor(self.sq, self.sq, stats[:, :, :, 2], ALU.add))
        v.wait(dve)
        v.mark(dve.tensor_reduce(self.var, self.sq, AX_X, ALU.add))
        v.wait(dve)
        dve.tensor_scalar(self.var, self.var, 1.0 / self.width, EPS, ALU.mult, ALU.add
                          ).then_inc(self.var_ready.sem, 1)
        dve.wait_ge(self.std_ready.sem, self.d0 + use + 1)
        v.mark(dve.reciprocal(rstd, self.std))
        v.wait(dve)

    def scalar(self, act, use=0):
        act.wait_ge(self.var_ready.sem, self.v0 + use + 1)
        act.activation(self.std, self.var, ACT.Sqrt).then_inc(self.std_ready.sem, 1)


class Project(Stage):

    def __init__(self, c, K, N, weights, prepare, take, taker, affine=None, store=None, keep_columns=None,
                 tag="", steps=0, before_batch=None, rows=None, columns=None, first_bank=2):
        self.c, self.K, self.N, self.w = c, K, N, weights
        self.prepare, self.take, self.taker, self.affine, self.store = prepare, take, taker, affine, store
        self.keep, self.steps, self.before_batch, self.first_bank = keep_columns, steps, before_batch, first_bank
        self.blocks = K // P
        self.G = -(-self.blocks // 4)
        self.C = -(-N // 512)
        rows = c.arena[:, 0:BATCH * K] if rows is None else rows
        columns = c.arena[:, 5120:5120 + 2 * self.blocks * P] if columns is None else columns
        self.rows = rows.rearrange("p (u d) -> p u d", d=K)
        self.columns = columns.rearrange("p (s n) -> p s n", s=2)
        n = TILES
        self.row_ready = c.counter(tag + "rows_ready")
        self.r0 = self.row_ready.reserve(n)
        self.turned = c.counter(tag + "rows_turned")
        self.t0 = self.turned.reserve(n * self.G)
        self.column_ready = c.counter(tag + "columns_ready")
        self.c0 = self.column_ready.reserve(n * self.G)
        self.product = c.counter(tag + "product_ready")
        self.p0 = self.product.reserve(n)
        self.used = c.counter(tag + "product_used")
        self.u0 = self.used.reserve(n)
        self.kept = c.counter(tag + "columns_kept")
        self.k0 = self.kept.reserve(n if keep_columns is not None else 0)
        self.stored = c.store.reserve(16 * BATCHES if store is not None else 0)

    def banks(self, u):
        return [self.c.bank[self.first_bank + (u % 2) * self.C + j] for j in range(self.C)]

    def turn_bank(self, u, g):
        return self.c.bank[(u * self.G + g) % 2]

    def tensor_batch(self, pe, i):
        c = self.c

        def turn(i, u):
            pe.wait_ge(self.row_ready.sem, self.r0 + BATCH * i + u + 1)
            for g in range(self.G):
                copied = before(i, u) if self.G == 1 else 2 * (BATCH * i + u - 1) + g + 1
                pe.wait_ge(self.column_ready.sem, self.c0 + copied)
                for b in range(4 * g, min(4 * g + 4, self.blocks)):
                    ins = pe.transpose(self.turn_bank(u, g)[:, (b % 4) * P:(b % 4 + 1) * P],
                                       self.rows[:, u, b * P:(b + 1) * P], c.ident[:, :])
                ins.then_inc(self.turned.sem, 1)

        def multiply(i, u):
            pe.wait_ge(self.column_ready.sem, self.c0 + self.G * (BATCH * i + u + 1))
            pe.wait_ge(self.used.sem, self.u0 + before(i, u))
            for j, bank in enumerate(self.banks(u)):
                lo, hi = j * 512, min(j * 512 + 512, self.N)
                for b in range(self.blocks):
                    ins = pe.matmul(bank[:, 0:hi - lo], self.columns[:, u % 2, b * P:(b + 1) * P],
                                    self.w[:, b, lo:hi], start=b == 0, stop=b == self.blocks - 1)
            ins.then_inc(self.product.sem, 1)

        turn(i, 0)
        for u in range(BATCH):
            if u + 1 < BATCH:
                turn(i, u + 1)
            multiply(i, u)

    def tensor(self, pe):
        with pe.Fori(0, BATCHES) as i:
            self.tensor_batch(pe, i)

    def copy_columns(self, act, i, u):
        for g in range(self.G):
            act.wait_ge(self.turned.sem, self.t0 + self.G * (BATCH * i + u) + g + 1)
            if g == 0:
                act.wait_ge(self.product.sem, self.p0 + before(i, u))
                if self.keep is not None:
                    act.wait_ge(self.kept.sem, self.k0 + before(i, u))
            hi = min(4 * g + 4, self.blocks)
            bank = self.turn_bank(u, g)
            if self.affine is None:
                ins = act.copy(self.columns[:, u % 2, 4 * g * P:hi * P], bank[:, 0:(hi - 4 * g) * P])
            else:
                gain, shift = self.affine
                for b in range(4 * g, hi):
                    ins = act.activation(self.columns[:, u % 2, b * P:(b + 1) * P],
                                         bank[:, (b - 4 * g) * P:(b - 4 * g + 1) * P], ACT.Identity,
                                         bias=shift[:, b:b + 1], scale=gain[:, b:b + 1])
            ins.then_inc(self.column_ready.sem, 1)

    def take_one(self, eng, i, u):
        eng.wait_ge(self.product.sem, self.p0 + BATCH * i + u + 1)
        self.take(eng, i, u, self.banks(u)).then_inc(self.used.sem, 1)

    def scalar_batch(self, act, i):
        self.copy_columns(act, i, 0)
        for u in range(BATCH):
            if u + 1 < BATCH:
                self.copy_columns(act, i, u + 1)
            if self.taker == "scalar":
                self.take_one(act, i, u)

    def scalar(self, act):
        with act.Fori(0, BATCHES) as i:
            if self.before_batch is not None:
                self.before_batch.scalar(act, i)
            self.scalar_batch(act, i)

    def vector_batch(self, dve, i):
        if self.before_batch is not None:
            self.before_batch.vector(dve, i)
        for u in range(BATCH):
            dve.wait_ge(self.turned.sem, self.t0 + self.G * (BATCH * (i - 1) + u + 1))
            self.prepare(dve, i, u, self.rows[:, u, :]).then_inc(self.row_ready.sem, 1)
        for u in range(BATCH):
            if self.keep is not None:
                dve.wait_ge(self.column_ready.sem, self.c0 + self.G * (BATCH * i + u + 1))
                for b in range(self.blocks):
                    ins = dve.tensor_copy(self.keep[:, b, bass.ds((i * BATCH + u) * P, P)],
                                          self.columns[:, u % 2, b * P:(b + 1) * P])
                ins.then_inc(self.kept.sem, 1)
            if self.taker == "vector":
                self.take_one(dve, i, u)

    def vector(self, dve):
        with self.c.v.loop(dve, BATCHES, self.steps) as i:
            self.vector_batch(dve, i)

    def sync(self, sp):
        if self.store is None:
            return
        src, to = self.store
        with sp.Fori(0, BATCHES) as i:
            sp.wait_ge(self.used.sem, self.u0 + BATCH * (i + 1))
            sp.dma_start(to.rearrange("(t p) d -> p t d", p=P)[:, bass.ds(i * BATCH, BATCH), :],
                         src[:, bass.ds(i * BATCH, BATCH), :]).then_inc(self.c.store.sem, 16)
        sp.wait_ge(self.c.store.sem, self.stored + 16 * BATCHES)


class TurnWeights(Stage):

    def __init__(self, c, W, rows, K, vectors=()):
        self.c, self.W, self.parts, self.blocks, self.rows = c, W, rows // P, K // P, rows
        self.plain = c.arena[:, 0:self.parts * K].rearrange("p (r k) -> p r k", k=K)
        self.out = c.w_area[:, 0:self.blocks * rows].rearrange("p (b n) -> p b n", n=rows)
        self.vectors = vectors
        self.l0 = c.loads.reserve(16 * len(vectors))
        self.landed = c.counter("plain_weights_landed")
        self.n0 = self.landed.reserve(16)
        self.turned = c.counter("weights_turned")
        self.t0 = self.turned.reserve(self.blocks)

    def sync(self, sp):
        c = self.c
        sp.dma_start(self.plain, self.W.rearrange("(r p) k -> p r k", p=P)).then_inc(self.landed.sem, 16)
        for to, src in self.vectors:
            sp.dma_start(to, src).then_inc(c.loads.sem, 16)
        sp.wait_ge(self.landed.sem, self.n0 + 16)
        sp.wait_ge(c.loads.sem, self.l0 + 16 * len(self.vectors))

    def tensor(self, pe):
        pe.wait_ge(self.landed.sem, self.n0 + 16)
        for b in range(self.blocks):
            for r in range(self.parts):
                ins = pe.transpose(self.c.bank[b][:, r * P:(r + 1) * P], self.plain[:, r, b * P:(b + 1) * P],
                                   self.c.ident[:, :])
            ins.then_inc(self.turned.sem, 1)

    def scalar(self, act):
        for b in range(self.blocks):
            act.wait_ge(self.turned.sem, self.t0 + b + 1)
            act.copy(self.out[:, b, :], self.c.bank[b][:, 0:self.rows])


class Load(Stage):

    def __init__(self, c, pairs):
        self.c, self.pairs = c, pairs
        self.l0 = c.loads.reserve(16 * len(pairs))

    def sync(self, sp):
        for to, src in self.pairs:
            with self.c.nc.allow_non_contiguous_dma(reason="vectors of a few hundred elements"):
                sp.dma_start(to, src).then_inc(self.c.loads.sem, 16)
        sp.wait_ge(self.c.loads.sem, self.l0 + 16 * len(self.pairs))


def over(ap, width):
    return ap.unsqueeze(2).broadcast_to([ap.shape[0], ap.shape[1], width])


def along(ap, n):
    return ap.unsqueeze(1).broadcast_to([ap.shape[0], n, ap.shape[1]])


class Steps(Stage):

    def __init__(self, c, make):
        self.c, self.make = c, make

    def vector(self, dve):
        for ins in self.make(dve):
            self.c.v.mark(ins)
            self.c.v.wait(dve)


class StoreTable(Stage):

    def __init__(self, c, src):
        self.c, self.src = c, src
        self.s0 = c.store.reserve(16)

    def sync(self, sp):
        sp.dma_start(self.c.table.rearrange("(t p) d -> p t d", p=P), self.src).then_inc(self.c.store.sem, 16)
        sp.wait_ge(self.c.store.sem, self.s0 + 16)


class BatchNorm(Stage):

    def __init__(self, c, sums, gamma, beta):
        self.c, self.gamma, self.beta = c, gamma, beta
        self.sums = sums
        self.centred = c.big_b[:, 0:TILES * D].rearrange("p (t d) -> p t d", d=D)
        self.square = c.big_b[:, TILES * D:2 * TILES * D].rearrange("p (t d) -> p t d", d=D)
        self.mean, self.gain = c.arena[:, 0:D], c.arena[:, D:2 * D]
        self.ready = c.counter("columns_to_sum")
        self.r0 = self.ready.reserve(1)
        self.summed = c.counter("columns_summed")
        self.s0 = self.summed.reserve(2)
        self.asked = c.counter("norm_asked")
        self.q0 = self.asked.reserve(3)
        self.answered = c.counter("norm_answered")
        self.n0 = self.answered.reserve(3)

    def tensor(self, pe):
        c = self.c
        for n, what in enumerate((self.sums[:, :, 0:D], self.square)):
            if n == 1:
                pe.wait_ge(self.ready.sem, self.r0 + 1)
            out = c.bank[n][:, 0:D]
            pe.matmul(out, c.ones[:, :], what[:, 0, :], start=True, stop=False)
            with pe.Fori(1, TILES - 1) as t:
                pe.matmul(out, c.ones[:, :], what[:, bass.ds(t, 1), :], start=False, stop=False)
            pe.matmul(out, c.ones[0:LAST, :], what[0:LAST, TILES - 1, :], start=False, stop=True).then_inc(self.summed.sem, 1)

    def vector(self, dve):
        c, v = self.c, self.c.v
        deg = c.dinv[:, :]
        dve.tensor_scalar(deg, self.sums[:, :, D], 1.0, None, ALU.add).then_inc(self.asked.sem, 1)
        dve.wait_ge(self.answered.sem, self.n0 + 1)
        v.mark(dve.reciprocal(deg, deg))
        dve.wait_ge(self.summed.sem, self.s0 + 1)
        v.mark(dve.tensor_scalar(self.mean, c.bank[0][:, 0:D], 1.0 / NODES, None, ALU.mult))
        v.wait(dve)
        v.mark(dve.tensor_tensor(self.centred, self.sums[:, :, 0:D], along(self.mean, TILES), ALU.subtract))
        v.wait(dve)
        dve.tensor_tensor(self.square, self.centred, self.centred, ALU.mult).then_inc(self.ready.sem, 1)
        dve.wait_ge(self.summed.sem, self.s0 + 2)
        dve.tensor_scalar(self.gain, c.bank[1][:, 0:D], 1.0 / NODES, EPS, ALU.mult, ALU.add
                          ).then_inc(self.asked.sem, 1)
        dve.wait_ge(self.answered.sem, self.n0 + 2)
        v.mark(dve.reciprocal(self.gain, self.gain))
        v.wait(dve)
        v.mark(dve.tensor_tensor(self.gain, self.gain, self.gamma, ALU.mult))
        v.wait(dve)
        v.mark(dve.tensor_tensor(self.centred, self.centred, along(self.gain, TILES), ALU.mult))
        v.wait(dve)
        v.mark(dve.tensor_tensor(self.centred, self.centred, along(self.beta, TILES), ALU.add))
        v.wait(dve)
        dve.tensor_scalar(self.square, self.centred, 0.0, None, ALU.min).then_inc(self.asked.sem, 1)
        h = self.sums[:, :, 0:D]
        v.mark(dve.tensor_tensor(h, c.x[:, :, :], over(c.mean[:, :], D), ALU.subtract))
        v.wait(dve)
        v.mark(dve.tensor_tensor(h, h, over(c.rstd[:, :], D), ALU.mult))
        v.wait(dve)
        v.mark(dve.scalar_tensor_tensor(out=h, in0=self.centred, scalar=0.0, in1=h, op0=ALU.max, op1=ALU.add))
        v.wait(dve)
        dve.wait_ge(self.answered.sem, self.n0 + 3)
        v.mark(dve.scalar_tensor_tensor(out=h, in0=self.square, scalar=-1.0, in1=h, op0=ALU.add, op1=ALU.add))
        v.wait(dve)
        v.mark(dve.tensor_tensor(c.x[:, :, :], c.x[:, :, :], h, ALU.add))
        v.wait(dve)

    def scalar(self, act):
        c = self.c
        act.wait_ge(self.asked.sem, self.q0 + 1)
        act.activation(c.dinv[:, :], c.dinv[:, :], ACT.Sqrt).then_inc(self.answered.sem, 1)
        act.wait_ge(self.asked.sem, self.q0 + 2)
        act.activation(self.gain, self.gain, ACT.Sqrt).then_inc(self.answered.sem, 1)
        act.wait_ge(self.asked.sem, self.q0 + 3)
        act.activation(self.square, self.square, ACT.Exp).then_inc(self.answered.sem, 1)


class Route(Stage):

    def __init__(self, c, logits, kind):
        self.c, self.logits, self.kind = c, logits, kind
        self.T = 1 if kind == "pooled" else TILES
        n = [0]

        def part(size):
            n[0] += size
            return c.arena[:, n[0] - size:n[0]]

        T = self.T
        self.l, self.l2, self.eq, self.first, self.second, self.p = (
            part(T * EXPERTS).rearrange("p (t e) -> p t e", e=EXPERTS) for _ in range(6))
        self.m1, self.m2, self.at, self.e2, self.s, self.w1, self.w2 = (part(T) for _ in range(7))
        self.below = part(EXPERTS)
        self.load = part(EXPERTS)
        self.asked = c.counter("exp_asked")
        self.answered = c.counter("exp_answered")
        self.n = {"softmax": 1, "probs": 2, "pooled": 3}[kind]
        self.q0, self.a0 = self.asked.reserve(self.n), self.answered.reserve(self.n)
        self.pool_sum = c.counter("logits_summed")
        self.p0 = self.pool_sum.reserve(1 if kind == "pooled" else 0)
        self.exps = {"softmax": [self.e2], "probs": [self.e2, self.p],
                     "pooled": [self.l, self.l2, self.e2]}[kind]

    def tensor(self, pe):
        if self.kind == "pooled":
            c = self.c
            pe.matmul(c.bank[0][:, 0:(TILES - 1) * EXPERTS], c.ones[:, :],
                      self.logits[:, 0:TILES - 1, :].rearrange("p t e -> p (t e)"), start=True, stop=True)
            pe.matmul(c.bank[1][:, 0:EXPERTS], c.ones[0:LAST, :], self.logits[0:LAST, TILES - 1, :],
                      start=True, stop=True).then_inc(self.pool_sum.sem, 1)

    def scalar(self, act):
        for n, what in enumerate(self.exps):
            act.wait_ge(self.asked.sem, self.q0 + n + 1)
            act.activation(what, what, ACT.Exp).then_inc(self.answered.sem, 1)

    def vector(self, dve):
        c, v, T = self.c, self.c.v, self.T
        asked = [0]

        def step(ins):
            v.mark(ins)
            v.wait(dve)

        def exp(ins):
            ins.then_inc(self.asked.sem, 1)
            asked[0] += 1
            dve.wait_ge(self.answered.sem, self.a0 + asked[0])

        logits = self.logits
        step(dve.tensor_scalar(self.below, c.iota[:, 0:EXPERTS], float(-EXPERTS), None, ALU.add))
        if self.kind == "pooled":
            dve.wait_ge(self.pool_sum.sem, self.p0 + 1)
            logits = self.l
            l, l2 = self.l[:, 0, :], self.l2[:, 0, :]
            step(dve.tensor_reduce(l, c.bank[0][:, 0:(TILES - 1) * EXPERTS].rearrange("p (t e) -> p e t", e=EXPERTS),
                                   AX_X, ALU.add))
            step(dve.tensor_tensor(l, l, c.bank[1][:, 0:EXPERTS], ALU.add))
            step(dve.tensor_scalar(l, l, 1.0 / NODES, None, ALU.mult))
            capacity = float(-(-NODES * 5 // (4 * EXPERTS)))
            for which, a in enumerate((l, l2)):
                step(dve.tensor_reduce(self.m1, a, AX_X, ALU.max))
                exp(dve.tensor_scalar(a, a, self.m1[:, 0:1], None, ALU.subtract))
                step(dve.tensor_reduce(self.s, a, AX_X, ALU.add))
                step(dve.reciprocal(self.s, self.s))
                step(dve.tensor_scalar(a, a, self.s[:, 0:1], None, ALU.mult))
                if which == 0:
                    step(dve.tensor_scalar(self.load, a, float(NODES), None, ALU.mult))
                    step(dve.tensor_scalar(self.eq[:, 0, :], self.load, capacity, None, ALU.is_gt))
                    step(dve.tensor_scalar(self.load, self.load, capacity, None, ALU.max))
                    step(dve.reciprocal(self.load, self.load))
                    step(dve.tensor_scalar(self.load, self.load, capacity, -1.0, ALU.mult, ALU.add))
                    step(dve.tensor_tensor(self.load, self.load, self.eq[:, 0, :], ALU.mult))
                    step(dve.scalar_tensor_tensor(out=l2, in0=self.load, scalar=1.0, in1=a,
                                                  op0=ALU.add, op1=ALU.mult))
            logits = self.l2
        below = along(self.below, T)

        def pick(values, best, onehot):
            step(dve.tensor_reduce(best, values, AX_X, ALU.max))
            step(dve.tensor_tensor(self.eq, values, over(best, EXPERTS), ALU.is_equal))
            step(dve.tensor_tensor(self.eq, self.eq, below, ALU.mult))
            step(dve.tensor_reduce(self.at, self.eq, AX_X, ALU.min))
            step(dve.tensor_tensor(onehot, below, over(self.at, EXPERTS), ALU.is_equal))

        pick(logits, self.m1, self.first)
        rest = self.p
        step(dve.scalar_tensor_tensor(out=rest, in0=self.first, scalar=-1e30, in1=logits, op0=ALU.mult, op1=ALU.add))
        pick(rest, self.m2, self.second)
        exp(dve.tensor_tensor(self.e2, self.m2, self.m1, ALU.subtract))
        if self.kind == "probs":
            exp(dve.tensor_tensor(self.p, logits, over(self.m1, EXPERTS), ALU.subtract))
            step(dve.tensor_reduce(self.s, self.p, AX_X, ALU.add))
            step(dve.reciprocal(self.w1, self.s))
            step(dve.tensor_tensor(self.w2, self.e2, self.w1, ALU.mult))
            step(dve.tensor_tensor(self.s, self.w1, self.w2, ALU.add))
            step(dve.tensor_scalar(self.s, self.s, 1e-12, None, ALU.max))
            step(dve.reciprocal(self.s, self.s))
            step(dve.tensor_tensor(self.w1, self.w1, self.s, ALU.mult))
            step(dve.tensor_tensor(self.w2, self.w2, self.s, ALU.mult))
        else:
            step(dve.tensor_scalar(self.s, self.e2, 1.0, None, ALU.add))
            step(dve.reciprocal(self.w1, self.s))
            step(dve.tensor_tensor(self.w2, self.e2, self.w1, ALU.mult))
        step(dve.tensor_tensor(self.first, self.first, over(self.w1, EXPERTS), ALU.mult))
        step(dve.tensor_tensor(self.second, self.second, over(self.w2, EXPERTS), ALU.mult))
        if T == 1:
            step(dve.tensor_tensor(self.first, self.first, self.second, ALU.add))
            step(dve.tensor_copy(c.gates[:, :, :], along(self.first[:, 0, :], TILES)))
        else:
            step(dve.tensor_tensor(c.gates[:, :, :], self.first, self.second, ALU.add))


class BiasStart(Stage):

    def __init__(self, c, b2, out):
        self.c, self.b2, self.out = c, b2, out
        self.rows = c.arena[:, 0:BATCH * EXPERTS]
        self.turned_gates = c.arena[0:EXPERTS, 64:64 + BATCH * P]
        self.ready, self.turned, self.copied, self.product = (c.counter(f"gates_{w}") for w in
                                                              ("ready", "turned", "copied", "product"))
        self.r0, self.t0, self.c0, self.p0 = (s.reserve(BATCHES) for s in
                                              (self.ready, self.turned, self.copied, self.product))

    def vector(self, dve):
        c, v = self.c, self.c.v
        with v.loop(dve, BATCHES, BATCH) as i:
            dve.tensor_copy(self.rows.rearrange("p (t e) -> p t e", e=EXPERTS),
                            c.gates[:, bass.ds(i * BATCH, BATCH), :]).then_inc(self.ready.sem, 1)
            dve.wait_ge(self.product.sem, self.p0 + i + 1)
            for u in range(BATCH):
                v.mark(dve.tensor_copy(self.out[:, tiles5(i, u), :],
                                       c.bank[2 + u][:, 0:D].rearrange("p (a d) -> p a d", a=1)))
            v.wait(dve)

    def tensor(self, pe):
        c = self.c
        with pe.Fori(0, BATCHES) as i:
            pe.wait_ge(self.ready.sem, self.r0 + i + 1)
            for u in range(BATCH):
                ins = pe.transpose(c.bank[u // 4][0:EXPERTS, (u % 4) * P:(u % 4 + 1) * P],
                                   self.rows[:, u * EXPERTS:(u + 1) * EXPERTS], c.ident[:, :])
            ins.then_inc(self.turned.sem, 1)
            pe.wait_ge(self.copied.sem, self.c0 + i + 1)
            for u in range(BATCH):
                ins = pe.matmul(c.bank[2 + u][:, 0:D], self.turned_gates[:, u * P:(u + 1) * P], self.b2,
                                start=True, stop=True)
            ins.then_inc(self.product.sem, 1)

    def scalar(self, act):
        c = self.c
        with act.Fori(0, BATCHES) as i:
            act.wait_ge(self.turned.sem, self.t0 + i + 1)
            act.copy(self.turned_gates[:, 0:4 * P], c.bank[0][0:EXPERTS, :])
            act.copy(self.turned_gates[:, 4 * P:], c.bank[1][0:EXPERTS, 0:P]).then_inc(self.copied.sem, 1)


class Experts(Stage):

    def __init__(self, c, columns, out, W1, b1, W2, H, func):
        self.c, self.columns, self.out, self.H, self.func = c, columns, out, H, func
        self.W1, self.W2 = W1, W2
        self.HC, self.KC = H // P, D // P
        self.width = BATCH * P
        self.half = self.width // 2
        o = 2 * H
        self.w1 = [c.w_area[:, k * o:(k + 1) * o].rearrange("p (k n) -> p k n", n=H) for k in range(2)]
        self.w2 = [c.w_area[:, (2 + k) * o:(3 + k) * o].rearrange("p (k n) -> p k n", n=D) for k in range(2)]
        self.b1 = b1
        self.hidden = c.arena[:, 0:2 * self.HC * self.width].rearrange("p (s h n) -> p s h n", s=2, h=self.HC)
        self.pairs = EXPERTS // 2
        self.pair_b1 = c.cols[:, 32:32 + 2 * self.HC]
        self.bias = c.counter("pair_bias_ready")
        self.b0 = self.bias.reserve(self.pairs)
        self.groups = EXPERTS * BATCHES
        self.parts = 2 * self.HC
        self.landed = [c.counter(f"expert{k}_landed") for k in range(2)]
        self.l0 = [s.reserve(32 * self.pairs) for s in self.landed]
        self.up = c.counter("hidden_summed")
        self.u0 = self.up.reserve(self.groups * self.parts)
        self.active = c.counter("hidden_ready")
        self.a0 = self.active.reserve(self.groups * self.parts)
        self.down = c.counter("expert_summed")
        self.d0 = self.down.reserve(self.groups * BATCH)
        self.added = c.counter("expert_added")
        self.g0 = self.added.reserve(self.groups * BATCH)

    def sync(self, sp):
        with sp.Fori(0, self.pairs) as i:
            for k in range(2):
                sp.wait_ge(self.down.sem, self.d0 + TILES * (2 * i + k - 1))
                sp.dma_start(self.w1[k], self.W1[bass.ds(2 * i + k, 1)].rearrange("a (b p) h -> p (a b) h", p=P)
                             ).then_inc(self.landed[k].sem, 16)
                sp.dma_start(self.w2[k], self.W2[bass.ds(2 * i + k, 1)].rearrange("a (b p) h -> p (a b) h", p=P)
                             ).then_inc(self.landed[k].sem, 16)
        for k in range(2):
            sp.wait_ge(self.landed[k].sem, self.l0[k] + 32 * self.pairs)

    def slot(self, n, u):
        return self.c.bank[4 + (BATCH * n + u) % 2][:, 0:D]

    def tensor(self, pe):
        c = self.c

        def up(i, n):
            k, g = divmod(n, BATCHES)
            if g == 0:
                pe.wait_ge(self.landed[k].sem, self.l0[k] + 32 * (i + 1))
            for q in range(self.parts):
                m, half = divmod(q, 2)
                count = self.parts * (2 * BATCHES * i + n) + q
                pe.wait_ge(self.active.sem, self.a0 + count - 3)
                for b in range(self.KC):
                    at = g * self.width + half * self.half
                    ins = pe.matmul(c.bank[q % 4][:, 0:self.half], self.w1[k][:, b, m * P:(m + 1) * P],
                                    self.columns[:, b, at:at + self.half], start=b == 0, stop=b == self.KC - 1)
                ins.then_inc(self.up.sem, 1)

        def down(i, n):
            k = n // BATCHES
            pe.wait_ge(self.active.sem, self.a0 + self.parts * (2 * BATCHES * i + n + 1))
            for u in range(BATCH):
                pe.wait_ge(self.added.sem, self.g0 + BATCH * (2 * BATCHES * i + n) + u - 1)
                for m in range(self.HC):
                    ins = pe.matmul(self.slot(n, u), self.hidden[:, n % 2, m, u * P:(u + 1) * P],
                                    self.w2[k][:, m, :], start=m == 0, stop=m == self.HC - 1)
                ins.then_inc(self.down.sem, 1)

        with pe.Fori(0, self.pairs) as i:
            up(i, 0)
            for n in range(2 * BATCHES):
                if n + 1 < 2 * BATCHES:
                    up(i, n + 1)
                down(i, n)

    def scalar(self, act):
        c = self.c
        with act.Fori(0, self.pairs) as i:
            c.hold(act, "scalar", self.active.sem, self.a0 + self.parts * 2 * BATCHES * i)
            act.copy(self.pair_b1, self.b1[:, bass.ds(2 * i * self.HC, 2 * self.HC)]).then_inc(self.bias.sem, 1)
            act.wait_ge(self.bias.sem, self.b0 + i + 1)
            for n in range(2 * BATCHES):
                k = n // BATCHES
                act.wait_ge(self.down.sem, self.d0 + BATCH * (2 * BATCHES * i + n - 1))
                for q in range(self.parts):
                    m, half = divmod(q, 2)
                    act.wait_ge(self.up.sem, self.u0 + self.parts * (2 * BATCHES * i + n) + q + 1)
                    act.activation(self.hidden[:, n % 2, m, half * self.half:(half + 1) * self.half],
                                   c.bank[q % 4][:, 0:self.half], self.func,
                                   bias=self.pair_b1[:, k * self.HC + m:k * self.HC + m + 1]
                                   ).then_inc(self.active.sem, 1)

    def vector(self, dve):
        c = self.c
        with dve.Fori(0, self.pairs) as i:
            for n in range(2 * BATCHES):
                k, g = divmod(n, BATCHES)
                for u in range(BATCH):
                    t = g * BATCH + u
                    count = BATCH * (2 * BATCHES * i + n) + u
                    dve.wait_ge(self.down.sem, self.d0 + count + 1)
                    dve.wait_ge(self.added.sem, self.g0 + count + 1 - TILES)
                    dve.scalar_tensor_tensor(out=self.out[:, t, :], in0=self.slot(n, u),
                                             scalar=c.gates[:, t, bass.ds(2 * i + k, 1)], in1=self.out[:, t, :],
                                             op0=ALU.mult, op1=ALU.add).then_inc(self.added.sem, 1)



class Finish(Stage):

    def __init__(self, c):
        self.c = c
        self.s0 = c.store.reserve(32)

    def sync(self, sp):
        c, whole = self.c, (TILES - 1) * P
        sp.dma_start(c.out[0:whole, :].rearrange("(t p) d -> p t d", p=P), c.x[:, 0:TILES - 1, :]
                     ).then_inc(c.store.sem, 16)
        sp.dma_start(c.out[whole:NODES, :], c.x[0:LAST, TILES - 1, :]).then_inc(c.store.sem, 16)
        sp.wait_ge(c.store.sem, self.s0 + 32)


def gnn_ffn_layers(nc, T, out, stages_of):
    with ExitStack() as ctx:
        c = Core(nc, ctx, T, out)
        stages = stages_of(c)
        block = ctx.enter_context(nc.Block())

        @block.sync
        def _(sp):
            for counter in c.counters.values():
                if counter.lead:
                    sp.sem_inc(counter.sem, counter.lead)
            for n, stage in enumerate(stages):
                c.enter("sync", sp, n)
                stage.sync(sp)
                c.leave("sync", sp)

        @block.tensor
        def _(pe):
            for n, stage in enumerate(stages):
                c.enter("tensor", pe, n)
                stage.tensor(pe)
                c.leave("tensor", pe)

        @block.vector
        def _(dve):
            for n, stage in enumerate(stages):
                c.enter("vector", dve, n)
                stage.vector(dve)
                c.leave("vector", dve)

        @block.scalar
        def _(act):
            for n, stage in enumerate(stages):
                c.enter("scalar", act, n)
                stage.scalar(act)
                c.leave("scalar", act)

        @block.gpsimd
        def _(pool):
            for n, stage in enumerate(stages):
                c.enter("gpsimd", pool, n)
                stage.gpsimd(pool)
                c.leave("gpsimd", pool)


class BetweenConvolutions:

    def __init__(self, c, rows, width, first=None):
        self.c, self.rows, self.width, self.first = c, rows, width, first
        self.chunks = -(-width // 512)
        self.groups = 2 * self.chunks
        self.stats = c.stat_in[:, 0:BATCH * self.groups * 3]
        self.mean, self.rstd = c.batch_mean[:, 0:BATCH], c.batch_mean[:, BATCH:2 * BATCH]
        self.s = Statistics(c, BATCH, self.groups, width, uses=BATCHES)
        self.steps = BATCH * self.chunks + self.s.STEPS

    def statistics(self, dve, i, ready):
        c, v = self.c, self.c.v
        for u in range(BATCH):
            ready(u)
            for j in range(self.chunks):
                n = min(512, self.width)
                at = (u * self.chunks + j) * 6
                v.mark(dve.bn_stats(self.stats[:, at:at + 6], self.rows[:, u, j * n:(j + 1) * n]))
        v.wait(dve)
        self.s.vector(dve, self.stats.rearrange("p (t g s) -> p t g s", g=self.groups, s=3),
                      self.mean, self.rstd, use=i)

    def normalise(self, dve, u):
        rows = self.rows[:, u, :]
        return dve.tensor_scalar(rows, rows, self.mean[:, u:u + 1], self.rstd[:, u:u + 1],
                                 ALU.subtract, ALU.mult)


class FirstConvolutions(Stage):

    def __init__(self, c, sums, own, W1, b1, W2, gain, shift, out, table):
        self.c = c
        hidden, width = 1024, 512

        def combine(dve, i, u, to):
            to3 = to.rearrange("p (a d) -> p a d", a=1)
            c.v.mark(dve.tensor_tensor(to3, sums[:, tiles5(i, u), :], own[:, tiles5(i, u), :], ALU.add))
            c.v.wait(dve)
            return dve.tensor_scalar(to, to, c.dinv[:, tiles5(i, u)], None, ALU.mult)

        def add_bias(dve, i, u, banks):
            dve.wait_ge(self.second.turned.sem, self.second.t0 + self.second.G * (BATCH * (i - 1) + u + 1))
            for j, bank in enumerate(banks):
                ins = dve.tensor_tensor(self.second.rows[:, u, j * 512:(j + 1) * 512], bank[:, :],
                                        b1[:, j * 512:(j + 1) * 512], ALU.add)
            return ins

        def scale(act, i, u, banks):
            return act.activation(out[:, tiles5(i, u), :], banks[0][:, :].rearrange("p (a d) -> p a d", a=1),
                                  ACT.Identity, scale=c.dinv[:, tiles5(i, u)])

        self.first = Project(c, D, hidden, W1, combine, add_bias, "vector", tag="first_",
                             rows=c.big_a[:, 6656:6656 + BATCH * D], columns=c.big_a[:, 8192:8192 + 2 * D])
        self.second = Project(c, hidden, width, W2, lambda dve, i, u, to: self.between.normalise(dve, u), scale,
                              "scalar", affine=(gain, shift), store=(out, table), first_bank=6)
        self.between = BetweenConvolutions(c, self.second.rows, hidden)
        self.relu_ready = c.counter("relu_ready")
        self.r0 = self.relu_ready.reserve(TILES)

    def tensor(self, pe):
        with pe.Fori(0, BATCHES) as i:
            self.first.tensor_batch(pe, i)
            self.second.tensor_batch(pe, i)

    def vector(self, dve):
        c = self.c

        def ready(u):
            dve.wait_ge(self.relu_ready.sem, self.r0 + BATCH * i + u + 1)

        with c.v.loop(dve, BATCHES, BATCH + self.between.steps) as i:
            self.first.vector_batch(dve, i)
            self.between.statistics(dve, i, ready)
            self.second.vector_batch(dve, i)

    def scalar(self, act):
        with act.Fori(0, BATCHES) as i:
            self.first.scalar_batch(act, i)
            for u in range(BATCH):
                act.wait_ge(self.first.used.sem, self.first.u0 + BATCH * i + u + 1)
                rows = self.second.rows[:, u, :]
                act.activation(rows, rows, ACT.Relu).then_inc(self.relu_ready.sem, 1)
            self.between.s.scalar(act, use=i)
            self.second.scalar_batch(act, i)

    def sync(self, sp):
        self.second.sync(sp)


class PrepareSecond:

    def __init__(self, c, project_of, sums, own, bias, width):
        self.c, self.project_of, self.sums, self.own, self.bias = c, project_of, sums, own, bias
        self.between = BetweenConvolutions(c, c.arena[:, 0:BATCH * width].rearrange("p (u d) -> p u d", d=width),
                                           width)
        self.steps = 3 * BATCH + self.between.steps

    def vector(self, dve, i):
        c, v, rows, project = self.c, self.c.v, self.between.rows, self.project_of()
        for u in range(BATCH):
            dve.wait_ge(project.turned.sem, project.t0 + project.G * (BATCH * (i - 1) + u + 1))
            v.mark(dve.tensor_tensor(rows[:, u:u + 1, :], self.sums[:, tiles5(i, u), :],
                                     self.own[:, tiles5(i, u), :], ALU.add))
        v.wait(dve)
        for u in range(BATCH):
            v.mark(dve.scalar_tensor_tensor(out=rows[:, u, :], in0=rows[:, u, :], scalar=c.dinv[:, tiles5(i, u)],
                                            in1=self.bias, op0=ALU.mult, op1=ALU.add))
        v.wait(dve)
        for u in range(BATCH):
            v.mark(dve.tensor_scalar(rows[:, u, :], rows[:, u, :], 0.0, None, ALU.max))
        v.wait(dve)
        self.between.statistics(dve, i, lambda u: None)

    def scalar(self, act, i):
        self.between.s.scalar(act, use=i)


class GatherLast(Stage):

    def __init__(self, c, out):
        self.c, self.out = c, out
        self.edge = c.arena[:, 0:TILES].bitcast(I32)
        self.edge_f = c.arena[:, 32:32 + TILES]
        self.has = c.arena[:, 64:64 + TILES]
        self.row = c.arena[:, 96:96 + TILES].bitcast(I32)
        self.ready = c.counter("last_edges_ready")
        self.r0 = self.ready.reserve(1)
        self.rows = c.counter("last_rows_landed", 0)
        self.l0 = self.rows.reserve(16 * TILES)
        self.landed = c.counter("last_features_landed", 0)
        self.n0 = self.landed.reserve(16 * TILES)

    def gpsimd(self, pool):
        c = self.c
        dst = c.T["dst"].rearrange("(e a) -> e a", a=1)
        pool.wait_ge(self.ready.sem, self.r0 + 1)
        for t in range(TILES):
            pool.indirect_dma_start(self.row[:, t:t + 1], None, dst,
                                    bass.IndirectOffsetOnAxis(ap=self.edge[:, t:t + 1], axis=0)
                                    ).then_inc(self.rows.sem, 16)
        pool.wait_ge(self.rows.sem, self.l0 + 16 * TILES)
        for t in range(TILES):
            pool.indirect_dma_start(self.out[:, t, :], None, c.table,
                                    bass.IndirectOffsetOnAxis(ap=self.row[:, t:t + 1], axis=0)
                                    ).then_inc(self.landed.sem, 16)

    def vector(self, dve):
        c, v = self.c, self.c.v
        v.mark(dve.tensor_scalar(self.edge_f, c.last_edge[:, :], 1.0, 0.0, ALU.subtract, ALU.max))
        v.mark(dve.tensor_scalar(self.has, c.last_edge[:, :], 0.0, None, ALU.is_gt))
        v.wait(dve)
        dve.tensor_copy(self.edge, self.edge_f).then_inc(self.ready.sem, 1)
        dve.wait_ge(self.landed.sem, self.n0 + 16 * TILES)
        v.mark(dve.tensor_tensor(self.out, self.out, over(self.has, D), ALU.mult))
        v.wait(dve)


def tiles_of(area, width=D, at=0):
    return area[:, at:at + TILES * width].rearrange("p (t d) -> p t d", d=width)


def network(c):
    T = c.T
    stages = []

    def do(stage):
        stages.append(stage)
        return stage

    def everywhere(name, at, n, area=None):
        to = (c.vec if area is None else area)[:, at:at + n]
        return to, T[name].partition_broadcast(P)

    def by_partition(name, at, n):
        return c.cols[:, at:at + n // P], T[name].rearrange("(b p) -> p b", p=P)

    def normalise_from(src):
        def prepare(dve, i, u, to):
            return dve.tensor_scalar(to.rearrange("p (a d) -> p a d", a=1), src[:, tiles5(i, u), :],
                                     c.mean[:, tiles5(i, u)], c.rstd[:, tiles5(i, u)], ALU.subtract, ALU.mult)
        return prepare

    def normalised(dve, out, src):
        yield dve.tensor_tensor(out, src, over(c.mean[:, :], D), ALU.subtract)
        yield dve.tensor_tensor(out, out, over(c.rstd[:, :], D), ALU.mult)

    x = c.x[:, :, :]
    sums = tiles_of(c.big_a)

    def project_nodes(W):
        do(RowStats(c, c.x))
        out = tiles_of(c.big_b)

        def take(act, i, u, banks):
            return act.copy(out[:, tiles5(i, u), :], banks[0][:, 0:D].rearrange("p (a d) -> p a d", a=1))

        do(Project(c, D, D, W, normalise_from(c.x), take, "scalar", store=(out, c.table)))

    def ffn(prefix, H, func, kind, src, affine, router, bias_names, W1, b1, W2, b2):
        HC = H // P
        columns = c.big_b[:, 0:2 * TILES * P].rearrange("p (b n) -> p b n", b=2)
        routing = c.w_area[:, 0:2 * EXPERTS].rearrange("p (b e) -> p b e", e=EXPERTS)
        br = c.w_area[:, 64:64 + EXPERTS]
        b1_columns = c.w_area[:, 7000:7000 + EXPERTS * HC]
        b2_rows = c.w_area[0:EXPERTS, 6400:6400 + D]
        pairs = [(b1_columns.rearrange("p (e m) -> p e m", e=EXPERTS), T[b1].rearrange("e (m p) -> p e m", p=P)),
                 (b2_rows, T[b2])]
        if kind == "probs":
            pairs += [(routing[:, b, :], T[router][:, b * P:(b + 1) * P].rearrange("e p -> p e")) for b in range(2)]
        else:
            pairs.append((routing, T[router].rearrange("(b p) e -> p b e", p=P)))
        biases = [c.w_area[:, 64 + 16 * k:64 + 16 * k + EXPERTS] for k in range(len(bias_names))]
        pairs += [(to, T[name].partition_broadcast(P)) for to, name in zip(biases, bias_names)]
        do(Load(c, pairs))
        if not biases:
            do(Steps(c, lambda dve: iter([dve.memset(br, 0.0)])))
        if len(biases) == 2:
            do(Steps(c, lambda dve: iter([dve.tensor_tensor(br, biases[0], biases[1], ALU.add)])))

        def take(dve, i, u, banks):
            return dve.tensor_tensor(c.logits[:, tiles5(i, u), :],
                                     banks[0][:, 0:EXPERTS].rearrange("p (a e) -> p a e", a=1),
                                     br.rearrange("p (a e) -> p a e", a=1), ALU.add)

        do(Project(c, D, EXPERTS, routing, normalise_from(src), take, "vector", affine=affine,
                   keep_columns=columns))
        do(Route(c, c.logits, kind))
        do(BiasStart(c, b2_rows, sums))
        do(Experts(c, columns, sums, T[W1], b1_columns, T[W2], H, func))

    do(Setup(c))
    by_src = do(SortEdges(c, "src", "src", "dst", "edge_weight"))
    do(LastEdge(c, by_src))
    by_dst = do(SortEdges(c, "dst", "dst", "src", None))

    w0 = do(TurnWeights(c, T["L0_gnn_W"], D, D))
    project_nodes(w0.out)
    do(GatherAdd(c, by_src, D))
    do(Steps(c, lambda dve: iter([dve.tensor_tensor(x, x, sums, ALU.add)])))
    do(RowStats(c, c.x))
    do(Steps(c, lambda dve: normalised(dve, sums, x)))
    do(RowStats(c, sums))
    gain, shift = c.cols[:, 0:2], c.cols[:, 2:4]
    do(Load(c, [by_partition("L0_ffn_gamma", 0, D), by_partition("L0_ffn_beta", 2, D)]))
    ffn("L0", 512, ACT.Gelu, "softmax", sums, (gain, shift), "L0_ffn_Wr", ["L0_ffn_br"],
        "L0_ffn_W1", "L0_ffn_b1", "L0_ffn_W2", "L0_ffn_b2")
    do(Steps(c, lambda dve: iter([dve.tensor_tensor(x, x, sums, ALU.add)])))

    w1 = do(TurnWeights(c, T["L1_gnn_W"].rearrange("h o k -> (h o) k"), D, D))
    do(Load(c, [(c.vec[:, 0:D], T["L1_gnn_gamma"].rearrange("h o -> (h o)").partition_broadcast(P)),
                (c.vec[:, D:2 * D], T["L1_gnn_beta"].rearrange("h o -> (h o)").partition_broadcast(P))]))
    project_nodes(w1.out)
    with_degree = do(GatherAdd(c, by_dst, D, degree=True))
    do(BatchNorm(c, with_degree.sums, c.vec[:, 0:D], c.vec[:, D:2 * D]))
    do(RowStats(c, c.x))
    do(Load(c, [everywhere("L1_ffn_gamma", 0, D), everywhere("L1_ffn_beta", D, D)]))
    ffn("L1", 512, ACT.Gelu, "pooled", c.x, None, "L1_ffn_Wr", ["L1_ffn_br"],
        "L1_ffn_W1", "L1_ffn_b1", "L1_ffn_W2", "L1_ffn_b2")
    other = tiles_of(c.big_b)

    def residual(dve):
        yield from normalised(dve, other, x)
        yield dve.tensor_tensor(sums, sums, other, ALU.add)

    def normed(gamma, beta):
        def make(dve):
            yield from normalised(dve, sums, sums)
            yield dve.tensor_tensor(sums, sums, along(gamma, TILES), ALU.mult)
            yield dve.tensor_tensor(sums, sums, along(beta, TILES), ALU.add)
            yield dve.tensor_tensor(x, x, sums, ALU.add)
        return make

    do(Steps(c, residual))
    do(RowStats(c, sums))
    do(Steps(c, normed(c.vec[:, 0:D], c.vec[:, D:2 * D])))

    do(RowStats(c, c.x))
    own = tiles_of(c.big_b, D, TILES * D)

    def scaled(dve):
        yield from normalised(dve, own, x)
        yield dve.tensor_tensor(own, own, over(c.dinv[:, :], D), ALU.mult)

    do(Steps(c, scaled))
    do(StoreTable(c, own))
    conv1 = c.w_area[:, 0:2048].rearrange("p (b n) -> p b n", b=2)
    conv2 = c.w_area[:, 2048:6144].rearrange("p (b n) -> p b n", b=8)
    conv3 = c.w_area[:, 6144:7168].rearrange("p (b n) -> p b n", b=4)
    do(Load(c, [(w, T[name].rearrange("(b p) n -> p b n", p=P)) for w, name in
                ((conv1, "L2_gnn_W1"), (conv2, "L2_gnn_W2"), (conv3, "L2_gnn_W3"))]
            + [everywhere("L2_gnn_b1", 0, 1024), everywhere("L2_gnn_b2", 1024, 512),
               everywhere("L2_gnn_b3", 1536, D), everywhere("L2_gnn_g3", 1792, D),
               everywhere("L2_gnn_beta3", 2048, D),
               by_partition("L2_gnn_g1", 0, 1024), by_partition("L2_gnn_beta1", 8, 1024),
               by_partition("L2_gnn_g2", 16, 512), by_partition("L2_gnn_beta2", 20, 512)]))
    do(GatherAdd(c, by_dst, D))
    wide = tiles_of(c.big_b, 512)
    do(FirstConvolutions(c, sums, own, conv1, c.vec[:, 0:1024], conv2, c.cols[:, 0:8], c.cols[:, 8:16],
                         wide, c.wide_table))
    wide_sums = do(GatherAdd(c, by_dst, 512)).sums
    third = tiles_of(c.big_b)

    def scale(act, i, u, banks):
        return act.activation(third[:, tiles5(i, u), :], banks[0][:, 0:D].rearrange("p (a d) -> p a d", a=1),
                              ACT.Identity, scale=c.dinv[:, tiles5(i, u)])

    holder = []
    prepare = PrepareSecond(c, lambda: holder[0], wide_sums, wide, c.vec[:, 1024:1536], 512)
    holder.append(do(Project(c, 512, D, conv3, lambda dve, i, u, to: prepare.between.normalise(dve, u), scale,
                             "scalar", affine=(c.cols[:, 16:20], c.cols[:, 20:24]), store=(third, c.table),
                             steps=prepare.steps, before_batch=prepare)))
    do(GatherAdd(c, by_dst, D))

    def last_convolution(dve):
        yield dve.tensor_tensor(sums, sums, third, ALU.add)
        yield dve.tensor_tensor(sums, sums, over(c.dinv[:, :], D), ALU.mult)
        yield dve.tensor_tensor(sums, sums, along(c.vec[:, 1536:1792], TILES), ALU.add)
        yield dve.tensor_scalar(sums, sums, 0.0, None, ALU.max)

    do(Steps(c, last_convolution))
    do(RowStats(c, sums))
    do(Steps(c, normed(c.vec[:, 1792:2048], c.vec[:, 2048:2304])))
    do(RowStats(c, c.x))
    ffn("L2", 512, ACT.Relu, "softmax", c.x, None, "L2_ffn_Wg", ["L2_ffn_bg", "L2_ffn_bias"],
        "L2_ffn_W1", "L2_ffn_b1", "L2_ffn_W2", "L2_ffn_b2")
    do(Steps(c, lambda dve: iter([dve.tensor_tensor(x, x, sums, ALU.add)])))

    do(RowStats(c, c.x))
    do(Steps(c, lambda dve: normalised(dve, third, x)))
    do(StoreTable(c, third))
    do(GatherLast(c, sums))
    w3 = do(TurnWeights(c, T["L3_gnn_W"], D, 2 * D, [everywhere("L3_gnn_b", 0, D)]))
    do(Steps(c, lambda dve: iter([dve.tensor_tensor(x, x, along(c.vec[:, 0:D], TILES), ALU.add)])))

    def beside(dve, i, u, to):
        to = to.rearrange("p (a d) -> p a d", a=1)
        dve.tensor_copy(to[:, :, 0:D], third[:, tiles5(i, u), :])
        return dve.tensor_copy(to[:, :, D:2 * D], sums[:, tiles5(i, u), :])

    def add(dve, i, u, banks):
        tile = c.x[:, tiles5(i, u), :]
        return dve.tensor_tensor(tile, tile, banks[0][:, 0:D].rearrange("p (a d) -> p a d", a=1), ALU.add)

    do(Project(c, 2 * D, D, w3.out, beside, add, "vector"))
    do(RowStats(c, c.x))
    ffn("L3", 256, ACT.Gelu, "probs", c.x, None, "L3_ffn_router_w", [],
        "L3_ffn_w1", "L3_ffn_b1", "L3_ffn_w2", "L3_ffn_b2")

    def last(dve):
        yield from normalised(dve, third, x)
        yield dve.tensor_tensor(x, x, third, ALU.add)
        yield dve.tensor_tensor(x, x, sums, ALU.add)

    do(Steps(c, last))
    do(Finish(c))
    return stages


_INS = [
    'x', 'src', 'dst', 'edge_weight', 'L0_gnn_W', 'L0_ffn_gamma', 'L0_ffn_beta', 'L0_ffn_Wr', 'L0_ffn_br',
    'L0_ffn_W1', 'L0_ffn_b1', 'L0_ffn_W2', 'L0_ffn_b2', 'L1_gnn_W', 'L1_gnn_gamma', 'L1_gnn_beta', 'L1_ffn_Wr',
    'L1_ffn_br', 'L1_ffn_W1', 'L1_ffn_b1', 'L1_ffn_W2', 'L1_ffn_b2', 'L1_ffn_gamma', 'L1_ffn_beta', 'L2_gnn_W1',
    'L2_gnn_b1', 'L2_gnn_g1', 'L2_gnn_beta1', 'L2_gnn_W2', 'L2_gnn_b2', 'L2_gnn_g2', 'L2_gnn_beta2', 'L2_gnn_W3',
    'L2_gnn_b3', 'L2_gnn_g3', 'L2_gnn_beta3', 'L2_ffn_Wg', 'L2_ffn_bg', 'L2_ffn_bias', 'L2_ffn_W1', 'L2_ffn_b1',
    'L2_ffn_W2', 'L2_ffn_b2', 'L3_gnn_W', 'L3_gnn_b', 'L3_ffn_router_w', 'L3_ffn_w1', 'L3_ffn_b1', 'L3_ffn_w2',
    'L3_ffn_b2',
]
_OUTS = [((NODES, D), 'float32')]


def kernel(**inputs):
    import numpy as _np
    import concourse.bacc as _bacc
    from concourse import mybir as _mybir
    from concourse.bass_utils import run_bass_kernel_spmd as _run

    nc = _bacc.Bacc("TRN2", target_bir_lowering=False, num_devices=1)
    arrays, T = {}, {}
    for name in _INS:
        a = _np.ascontiguousarray(inputs[name])
        arrays[f"in_{name}_dram"] = a
        T[name] = nc.dram_tensor(f"in_{name}_dram", a.shape, _mybir.dt.from_np(a.dtype), kind="ExternalInput").ap()
    outs = [nc.dram_tensor(f"out_{i}_dram", shape, _mybir.dt.from_np(_np.dtype(dtype)), kind="ExternalOutput").ap()
            for i, (shape, dtype) in enumerate(_OUTS)]
    gnn_ffn_layers(nc, T, outs[0], network)
    r = _run(nc, [arrays], core_ids=[0])
    return r.results[0]["out_0_dram"]
```

```python
from contextlib import ExitStack, contextmanager

import concourse.bass as bass
from concourse import mybir

F32 = mybir.dt.float32
I32 = mybir.dt.int32
F32R = mybir.dt.float32r
ALU = mybir.AluOpType
ACT = mybir.ActivationFunctionType
AX_X = mybir.AxisListType.X

P = 128
NODES = 3125
EDGES = 50000
D = 256
TILES = -(-NODES // P)
LAST = NODES - (TILES - 1) * P
BATCH = 5
BATCHES = TILES // BATCH
EPS = 1e-5
EXPERTS = 8
UNIT = 256
LOW_BITS = 12
LEAD = 64

PER_ROW = -(-EDGES // P)
FULL_ROWS = EDGES // PER_ROW
REST = EDGES - FULL_ROWS * PER_ROW
PAIR = 2
CHUNKS_NEEDED = PAIR * ((EDGES + TILES * (PAIR * P - 1)) // (PAIR * P))
STEP_PAIRS = 10
SHORT = 5
AHEAD = 3
RING = PAIR * STEP_PAIRS
HALF = RING // 2
GROUPS = (4, 3, 3, 4, 3, 3)
TURN_AFTER = (0, 1, 3, 5, 6, 8)
TAKE_AFTER = (1, 3, 4, 6, 8, 9)
CHUNKS = -(-CHUNKS_NEEDED // RING) * RING
SORT_ROOM = 10000
RING_AT = 7050
SPILL = CHUNKS + 1
SCATTER_STEP = 23
SCATTER_PARTS = (12, 11)
assert sum(GROUPS) == RING and PER_ROW % SCATTER_STEP == 0 and TILES % BATCH == 0


class Counter:

    def __init__(self, sem, lead=LEAD):
        self.sem, self.lead = sem, lead
        self.next = lead

    def reserve(self, n):
        base = self.next
        self.next += n
        return base


class Chain:

    def __init__(self, sem):
        self.sem, self.base, self.n = sem, 0, 0

    def mark(self, ins):
        ins.then_inc(self.sem, 1)
        self.n += 1

    def wait(self, eng):
        eng.wait_ge(self.sem, self.base + self.n)

    @contextmanager
    def loop(self, eng, trips, per_trip):
        start = self.base + self.n
        with eng.Fori(0, trips) as i:
            self.base, self.n = start + per_trip * i, 0
            yield i
            assert self.n == per_trip, (self.n, per_trip)
        self.base, self.n = start + per_trip * trips, 0


def tiles5(i, u):
    return bass.ds(i * BATCH + u, 1)


def before(i, u):
    return BATCH * i + (u - 1 if u >= 2 else (-1 if u == 1 else 0))


def high_bits(dve, out, values):
    return dve.tensor_scalar(out.bitcast(I32), values.bitcast(I32), -(1 << LOW_BITS), None, ALU.bitwise_and)


class Core:

    def __init__(self, nc, ctx, T, out):
        self.nc, self.T, self.out = nc, T, out
        self.ctx = ctx
        self.sems = []
        f = self.sbuf
        self.x = f("x_nodes", [P, TILES, D])
        self.big_a, self.big_a_r = self.sbuf_twice("big_a", TILES * 2 * D)
        self.big_b, self.big_b_r = self.sbuf_twice("big_b", TILES * 2 * D)
        self.w_area, self.w_area_r = self.sbuf_twice("w_area", 7168)
        self.arena, self.arena_r = self.sbuf_twice("arena", 7168)
        self.vec = f("vectors", [P, 2304])
        self.iota = f("iota_row", [P, CHUNKS])
        self.ident = f("ident", [P, P])
        self.ones = f("ones", [P, P])
        self.earlier = self.vec[:, 0:P]
        self.mean = f("mean", [P, TILES])
        self.rstd = f("rstd", [P, TILES])
        self.logits = f("logits", [P, TILES, EXPERTS])[:, :, :]
        self.stat_tmp = f("stat_tmp", [P, 4, 64])
        self.gates = f("gates", [P, TILES, EXPERTS])
        self.cols = f("columns", [P, 64])
        self.dinv = f("dinv", [P, TILES])
        self.chosen = self.cols[:, 48:50].bitcast(I32)
        self.chosen_weight = self.cols[:, 50:52]
        self.edge_row = f("edge_row", [P, CHUNKS], I32)
        self.edge_node = f("edge_node", [P, CHUNKS])
        self.edge_value = f("edge_weight_sorted", [P, CHUNKS])
        self.pair_tiles = f("pair_tiles", [33, CHUNKS // PAIR], I32)
        self.last_edge = f("last_edge", [P, TILES])
        self.bank = [ctx.enter_context(nc.psum_tensor(f"bank{b}", [P, 512], F32)) for b in range(8)]
        self.table = nc.dram_tensor("table", [TILES * P, D], F32, kind="Internal").ap()
        self.wide_table = nc.dram_tensor("wide_table", [TILES * P, 2 * D], F32, kind="Internal").ap()
        self.stat_in = f("stat_in", [P, BATCH * 12])
        self.batch_mean = f("batch_mean", [P, 2 * BATCH])
        self.engines = ("tensor", "vector", "scalar", "gpsimd", "sync")
        self.done = {e: ctx.enter_context(nc.semaphore(f"{e}_stages_done")) for e in self.engines}
        self.gate = {e: ctx.enter_context(nc.semaphore(f"{e}_gate")) for e in self.engines}
        self.v = Chain(ctx.enter_context(nc.semaphore("vector_steps")))
        self.a = Chain(ctx.enter_context(nc.semaphore("scalar_steps")))
        self.counters = {}
        self.loads = self.counter("loads_landed")
        self.store = self.counter("stores_landed")

    def sbuf(self, name, shape, dt=F32):
        return self.ctx.enter_context(self.nc.sbuf_tensor(name, shape, dt))

    def sbuf_twice(self, name, size):
        with self.nc.sbuf_tensor(name, [P, size], F32) as plain:
            pass
        return plain, self.sbuf(f"{name}_rounded", [P, size], F32R)

    def counter(self, name, lead=LEAD):
        if name not in self.counters:
            self.counters[name] = Counter(self.ctx.enter_context(self.nc.semaphore(name)), lead)
        return self.counters[name]

    def hold(self, eng, name, sem, value):
        eng.wait_ge(sem, value)
        eng.sem_inc(self.gate[name], 1)

    def run(self, name, eng, stages):
        left = {e: 0 for e in self.engines}
        seen = {e: 0 for e in self.engines}
        through = {}
        for stage in stages:
            for other in stage.join:
                for e, n in through[other].items():
                    left[e] = max(left[e], n)
            if stage.takes_part(name):
                for other in self.engines:
                    if other != name and left[other] > seen[other]:
                        eng.wait_ge(self.done[other], left[other])
                        seen[other] = left[other]
                stage.part(name)(eng)
                if name == "sync":
                    eng.sem_inc(self.done[name], 1)
                else:
                    eng.drain().then_inc(self.done[name], 1)
            through[stage] = {}
            for e in self.engines:
                if stage.takes_part(e):
                    through[stage][e] = stage.number[e]
                    if not stage.background:
                        left[e] = max(left[e], stage.number[e])


class Stage:

    background = False
    join = ()
    tensor = vector = scalar = gpsimd = sync = None

    def part(self, name):
        return {"tensor": self.tensor, "vector": self.vector, "scalar": self.scalar,
                "gpsimd": self.gpsimd, "sync": self.sync}[name]

    def takes_part(self, name):
        return self.part(name) is not None


def number(stages, engines):
    count = {e: 0 for e in engines}
    for stage in stages:
        stage.number = {}
        for e in engines:
            if stage.takes_part(e):
                count[e] += 1
                stage.number[e] = count[e]


class Setup(Stage):

    def __init__(self, c):
        self.c = c
        self.int_row = c.big_b[:, 0:CHUNKS].bitcast(I32)
        self.made = c.counter("constants_made")
        self.m = self.made.reserve(6)
        self.l = c.loads.reserve(32)
        self.cleared = c.counter("cleared")
        self.z = self.cleared.reserve(1)

    def gpsimd(self, pool):
        c = self.c
        pool.iota(self.int_row, [[1, CHUNKS]], base=0, channel_multiplier=0).then_inc(self.made.sem, 1)
        pool.memset(c.ident[:, :], 0.0).then_inc(self.made.sem, 1)
        pool.memset(c.ones[:, :], 1.0).then_inc(self.made.sem, 1)
        pool.memset(c.earlier[:, :], 1.0).then_inc(self.made.sem, 1)
        pool.wait_ge(self.made.sem, self.m + 4)
        pool.affine_select(out=c.ident[:, :], in_=c.ident[:, :], compare_op=ALU.not_equal, fill=1.0,
                           base=0, pattern=[[-1, P]], channel_multiplier=1).then_inc(self.made.sem, 1)
        pool.affine_select(out=c.earlier[:, :], in_=c.earlier[:, :], compare_op=ALU.is_gt, fill=0.0,
                           base=0, pattern=[[1, P]], channel_multiplier=-1).then_inc(self.made.sem, 1)

    def vector(self, dve):
        c = self.c
        dve.memset(c.x[:, TILES - 1, :], 0.0).then_inc(self.cleared.sem, 1)
        dve.wait_ge(self.made.sem, self.m + 1)
        c.v.mark(dve.tensor_copy(c.iota[:, :], self.int_row))

    def sync(self, sp):
        c, whole = self.c, (TILES - 1) * P
        sp.dma_start(c.x[:, 0:TILES - 1, :], c.T["x"][0:whole, :].rearrange("(t p) d -> p t d", p=P)
                     ).then_inc(c.loads.sem, 16)
        sp.wait_ge(self.cleared.sem, self.z + 1)
        sp.dma_start(c.x[0:LAST, TILES - 1, :], c.T["x"][whole:NODES, :]).then_inc(c.loads.sem, 16)
        sp.wait_ge(c.loads.sem, self.l + 32)


class SortPlan(Stage):

    def __init__(self, c, name, key, other, weight, keep, tile_row, made=None):
        self.c, self.name = c, name
        if made is not None:
            self.gpsimd = None
        self.key, self.other, self.weight = c.T[key], c.T[other], weight and c.T[weight]
        self.slots = c.nc.dram_tensor(f"{name}_slots", [P, SPILL * 4], F32, kind="Internal").ap()
        self.rec, self.slot_i = keep[:, 0:PER_ROW * 4], keep[:, PER_ROW * 4:PER_ROW * 5].bitcast(I32)
        self.tile_all = keep[:, PER_ROW * 5:PER_ROW * 5 + CHUNKS]
        self.tile_row = tile_row
        self.row, self.node = c.edge_row[:, :], c.edge_node[:, :]
        self.value = weight and c.edge_value[:, :]
        n = [0]

        def part(size):
            n[0] += size
            return c.big_b[:, n[0] - size:n[0]]

        self.key_i, self.other_i, self.low_i, self.high_i, self.id_i = (
            part(PER_ROW).bitcast(I32) for _ in range(5))
        self.wt, self.high, self.position, self.ids, self.one = (part(PER_ROW) for _ in range(5))
        self.mask, self.term = part(BATCH * PER_ROW), part(BATCH * PER_ROW)
        self.total, self.chunks, self.ends, self.start = (part(TILES) for _ in range(4))
        self.chunks_i = part(TILES).bitcast(I32)
        assert n[0] <= SORT_ROOM
        self.fill = c.arena[:, 0:SPILL * 4]
        self.scan = c.big_a[:, 0:TILES * PER_ROW]
        self.cleared = c.counter("cleared")
        self.z = self.cleared.reserve(1)
        self.made = c.counter("edge_ids_made")
        self.i0 = self.made.reserve(1) if made is None else made.i0
        self.filled = c.counter("filling_ready")
        self.f0 = self.filled.reserve(1)
        self.l = c.loads.reserve(16 * (6 if weight else 4))
        self.counted = c.counter("bucket_counts_ready")
        self.k0 = self.counted.reserve(1)
        self.summed = c.counter("bucket_sums_ready")
        self.s0 = self.summed.reserve(1)
        self.slot_filled = c.counter("slots_filled")
        self.g0 = self.slot_filled.reserve(16)

    def sync(self, sp):
        c = self.c
        sp.wait_ge(self.cleared.sem, self.z + 1)
        pairs = [(self.key_i, self.key), (self.other_i, self.other)]
        if self.weight is not None:
            pairs.append((self.wt, self.weight))
        for to, src in pairs:
            sp.dma_start(to[0:FULL_ROWS, :], src[0:FULL_ROWS * PER_ROW].rearrange("(p j) -> p j", j=PER_ROW)
                         ).then_inc(c.loads.sem, 16)
            sp.dma_start(to[FULL_ROWS:FULL_ROWS + 1, 0:REST],
                         src[FULL_ROWS * PER_ROW:EDGES].rearrange("(p j) -> p j", p=1)).then_inc(c.loads.sem, 16)
        sp.wait_ge(self.filled.sem, self.f0 + 1)
        sp.dma_start(self.slots, self.fill).then_inc(self.slot_filled.sem, 16)
        sp.wait_ge(c.loads.sem, self.l + 16 * 2 * len(pairs))
        sp.wait_ge(self.slot_filled.sem, self.g0 + 16)

    def gpsimd(self, pool):
        pool.iota(self.id_i, [[1, PER_ROW]], base=0, channel_multiplier=PER_ROW).then_inc(self.made.sem, 1)

    def tensor(self, pe):
        c = self.c
        pe.wait_ge(self.counted.sem, self.k0 + 1)
        pe.matmul(c.bank[0][:, 0:TILES], c.earlier[:, :], self.total, start=True, stop=True)
        pe.matmul(c.bank[1][:, 0:TILES], c.ones[:, :], self.total, start=True, stop=True
                  ).then_inc(self.summed.sem, 1)

    def vector(self, dve):
        c, v = self.c, self.c.v
        rec = self.rec.rearrange("p (j r) -> p j r", r=4)
        rec_i = rec.bitcast(I32)
        dve.memset(self.other_i, 0)
        dve.memset(self.wt, 0.0)
        dve.memset(self.key_i, -1).then_inc(self.cleared.sem, 1)
        fill = self.fill.rearrange("p (c r) -> p c r", r=4)
        v.mark(dve.memset(self.one, 1.0))
        v.mark(dve.memset(self.fill, 0.0))
        v.wait(dve)
        dve.memset(fill[:, :, 1:2], -1.0).then_inc(self.filled.sem, 1)
        dve.wait_ge(self.made.sem, self.i0 + 1)
        v.mark(dve.tensor_copy(self.ids, self.id_i))
        v.wait(dve)
        v.mark(dve.tensor_scalar(self.position, self.ids, float(EDGES), None, ALU.is_ge))
        v.mark(dve.tensor_scalar(rec[:, :, 3], self.ids, 1.0, None, ALU.add))
        v.wait(dve)
        v.mark(dve.scalar_tensor_tensor(out=self.position, in0=self.ids, scalar=float(P * CHUNKS - EDGES),
                                        in1=self.position, op0=ALU.add, op1=ALU.mult))
        dve.wait_ge(c.loads.sem, self.l + 16 * (6 if self.weight is not None else 4))
        v.mark(dve.tensor_scalar(self.high_i, self.key_i, 7, None, ALU.arith_shift_right))
        v.mark(dve.tensor_scalar(self.low_i, self.key_i, P - 1, None, ALU.bitwise_and))
        v.mark(dve.tensor_copy(rec_i[:, :, 0], self.other_i))
        v.mark(dve.tensor_copy(rec[:, :, 2], self.wt))
        v.wait(dve)
        v.mark(dve.tensor_copy(self.high, self.high_i))
        v.mark(dve.tensor_copy(rec[:, :, 1], self.low_i))
        v.wait(dve)

        def buffer(area, u):
            return area[:, u * PER_ROW:(u + 1) * PER_ROW]

        def scans(i, u):
            return self.scan[:, bass.ds((i * BATCH + u) * PER_ROW, PER_ROW)]

        def masks(i):
            for u in range(BATCH):
                v.mark(dve.tensor_scalar(buffer(self.mask, u), self.high, c.iota[:, tiles5(i, u)], None,
                                         ALU.is_equal))
            v.wait(dve)

        with v.loop(dve, BATCHES, 2 * BATCH) as i:
            masks(i)
            for u in range(BATCH):
                v.mark(dve.tensor_tensor_scan(scans(i, u), self.one, buffer(self.mask, u), 0.0,
                                              ALU.mult, ALU.add))
            v.wait(dve)
        scan = self.scan.rearrange("p (b j) -> p b j", j=PER_ROW)
        dve.tensor_copy(self.total, scan[:, :, PER_ROW - 1]).then_inc(self.counted.sem, 1)
        dve.wait_ge(self.summed.sem, self.s0 + 1)
        v.mark(dve.tensor_scalar(self.chunks_i, c.bank[1][:, 0:TILES], float(PAIR * P - 1), None, ALU.add))
        v.wait(dve)
        v.mark(dve.tensor_scalar(self.chunks_i, self.chunks_i, 8, None, ALU.arith_shift_right))
        v.wait(dve)
        v.mark(dve.tensor_copy(self.chunks, self.chunks_i))
        v.wait(dve)
        v.mark(dve.tensor_tensor_scan(self.ends, self.one[:, 0:TILES], self.chunks, 0.0, ALU.mult, ALU.add))
        v.wait(dve)
        v.mark(dve.tensor_tensor(self.ends, self.ends, self.chunks, ALU.subtract))
        v.wait(dve)
        v.mark(dve.tensor_scalar(self.start, self.ends, float(PAIR * P), -1.0, ALU.mult, ALU.add))
        v.mark(dve.tensor_scalar(self.ends, self.ends, float(PAIR), None, ALU.mult))
        v.wait(dve)
        v.mark(dve.tensor_tensor(self.start, self.start, c.bank[0][:, 0:TILES], ALU.add))
        v.wait(dve)
        with v.loop(dve, BATCHES, 3 * BATCH) as i:
            masks(i)
            for u in range(BATCH):
                v.mark(dve.scalar_tensor_tensor(out=buffer(self.term, u), in0=scans(i, u),
                                                scalar=self.start[:, tiles5(i, u)], in1=buffer(self.mask, u),
                                                op0=ALU.add, op1=ALU.mult))
            v.wait(dve)
            for u in range(BATCH):
                v.mark(dve.tensor_tensor(self.position, self.position, buffer(self.term, u), ALU.add))
                v.wait(dve)
        v.mark(dve.tensor_copy(self.slot_i, self.position))
        v.wait(dve)
        v.mark(dve.tensor_scalar(self.high_i, self.slot_i, 7, None, ALU.arith_shift_right))
        v.mark(dve.tensor_scalar(self.low_i, self.slot_i, P - 1, None, ALU.bitwise_and))
        v.wait(dve)
        v.mark(dve.tensor_copy(self.high, self.high_i))
        v.mark(dve.tensor_copy(self.position, self.low_i))
        v.wait(dve)
        v.mark(dve.scalar_tensor_tensor(out=self.slot_i, in0=self.position, scalar=float(SPILL), in1=self.high,
                                        op0=ALU.mult, op1=ALU.add))


class ChunkTiles(Stage):

    def __init__(self, c, plan):
        self.c, self.plan = c, plan

    def vector(self, dve):
        c, v, plan = self.c, self.c.v, self.plan
        v.mark(dve.memset(plan.tile_all, 0.0))
        v.wait(dve)
        with v.loop(dve, TILES - 1, 1) as b:
            v.mark(dve.scalar_tensor_tensor(out=plan.tile_all, in0=c.iota[:, 0:CHUNKS],
                                            scalar=plan.ends[:, bass.ds(b + 1, 1)], in1=plan.tile_all,
                                            op0=ALU.is_ge, op1=ALU.add))
            v.wait(dve)
        r = plan.tile_row
        of_pairs = plan.tile_all.rearrange("p (n a) -> p n a", a=PAIR)[:, :, 0]
        v.mark(dve.tensor_copy(c.pair_tiles[r:r + 1, :], of_pairs[r:r + 1, :]))


class Scatter(Stage):

    background = True

    def __init__(self, c, plan):
        self.c, self.plan = c, plan
        a, b = SCATTER_PARTS
        at = RING_AT
        self.ring = [c.arena[:, at:at + 4 * a], c.arena[:, at + 4 * a:at + 4 * (a + b)]]
        at += 4 * (a + b)
        self.ring_to = [c.arena[:, at:at + a].bitcast(I32), c.arena[:, at + a:at + a + b].bitcast(I32)]
        self.steps = PER_ROW // SCATTER_STEP
        self.ring_ready = c.counter("scatter_ring_ready")
        self.r0 = self.ring_ready.reserve(4 * self.steps)
        self.scattered = [c.counter(f"edges_scattered{h}", 0) for h in range(2)]
        self.e0 = [s.reserve(16 * self.steps * n) for s, n in zip(self.scattered, SCATTER_PARTS)]

    def gpsimd(self, pool):
        c, plan = self.c, self.plan
        rec_i = plan.rec.rearrange("p (j r) -> p j r", r=4).bitcast(I32)
        target = plan.slots.rearrange("p (c r) -> (p c) r", r=4)

        def step(i, h, later):
            n, j = SCATTER_PARTS[h], i * SCATTER_STEP + h * SCATTER_PARTS[0]
            if later:
                c.hold(pool, "gpsimd", self.scattered[h].sem, self.e0[h] + 16 * n * i)
            pool.tensor_copy(self.ring[h].rearrange("p (j r) -> p j r", r=4).bitcast(I32),
                             rec_i[:, bass.ds(j, n), :]).then_inc(self.ring_ready.sem, 1)
            pool.tensor_copy(self.ring_to[h], plan.slot_i[:, bass.ds(j, n)]).then_inc(self.ring_ready.sem, 1)
            c.hold(pool, "gpsimd", self.ring_ready.sem, self.r0 + 4 * i + 2 * h + 2)
            for k in range(n):
                pool.indirect_dma_start(
                    target, bass.IndirectOffsetOnAxis(ap=self.ring_to[h][:, k:k + 1], axis=0),
                    self.ring[h][:, 4 * k:4 * k + 4], None).then_inc(self.scattered[h].sem, 16)

        step(0, 0, False)
        step(0, 1, False)
        with pool.Fori(1, self.steps) as i:
            step(i, 0, True)
            step(i, 1, True)
        for h, n in enumerate(SCATTER_PARTS):
            pool.wait_ge(self.scattered[h].sem, self.e0[h] + 16 * self.steps * n)


class ReadSlots(Stage):

    def __init__(self, c, plan, scatter, back):
        self.c, self.plan = c, plan
        self.join = (scatter,)
        self.back = back[:, 0:CHUNKS * 4]
        self.landed = c.counter("slots_read_back")
        self.b0 = self.landed.reserve(16)

    def sync(self, sp):
        sp.dma_start(self.back, self.plan.slots[:, 0:CHUNKS * 4]).then_inc(self.landed.sem, 16)
        sp.wait_ge(self.landed.sem, self.b0 + 16)

    def vector(self, dve):
        back, plan = self.back.rearrange("p (c r) -> p c r", r=4), self.plan
        dve.wait_ge(self.landed.sem, self.b0 + 16)
        dve.tensor_copy(plan.row, back[:, :, 0].bitcast(I32))
        dve.tensor_copy(plan.node, back[:, :, 1])
        if plan.value is not None:
            dve.tensor_copy(plan.value, back[:, :, 2])


class GatherAdd(Stage):

    def __init__(self, c, edges, width, degree=False, beside=None):
        self.c, self.edges, self.width, self.degree, self.beside = c, edges, width, degree, beside
        self.total = width + degree
        self.trips = CHUNKS // RING
        self.sums = c.big_a[:, 0:TILES * self.total].rearrange("p (t d) -> p t d", d=self.total)
        stride = width + 2
        self.slots = STEP_PAIRS if width == D else STEP_PAIRS // 2
        at = self.slots * PAIR * stride
        self.rows = c.arena[:, 0:at].rearrange("p (k d) -> p k d", d=stride)
        self.onehot = c.arena[:, at:at + SHORT * PAIR * P].rearrange("p (k d) -> p k d", d=P)
        at += SHORT * PAIR * P
        self.ring = c.arena[:, at:at + RING].bitcast(I32)
        assert at + RING <= 7168 and STEP_PAIRS % SHORT == 0 and STEP_PAIRS % self.slots == 0
        self.uses = STEP_PAIRS // self.slots
        n = self.trips * STEP_PAIRS
        self.index_ready = c.counter("gather_index_ready")
        self.i0 = self.index_ready.reserve(2 * self.trips)
        self.landed = [c.counter(f"pair_landed{k}", 0) for k in range(self.slots)]
        self.l0 = [s.reserve(16 * PAIR * self.uses * self.trips) for s in self.landed]
        self.onehot_ready = c.counter("onehot_ready")
        self.o0 = self.onehot_ready.reserve(n)
        self.summed = c.counter("pair_summed")
        self.s0 = self.summed.reserve(n)
        self.added = c.counter("pair_added")
        self.a0 = self.added.reserve(n)
        self.cleared = c.counter("sums_cleared")
        self.z0 = self.cleared.reserve(2)

    def landed_with(self, eng, i, q):
        slot = q % self.slots
        eng.wait_ge(self.landed[slot].sem, self.l0[slot] + 16 * PAIR * (self.uses * i + q // self.slots + 1))

    def scalar(self, act):
        def fill(i, h):
            act.copy(self.ring[:, h * HALF:(h + 1) * HALF],
                     self.edges.row[:, bass.ds(i * RING + h * HALF, HALF)]).then_inc(self.index_ready.sem, 1)

        fill(0, 0)
        fill(0, 1)
        if self.beside is not None:
            for j in range(len(GROUPS)):
                self.beside.scalar_group(act, 0, j)
        with act.Fori(1, self.trips) as i:
            for h in range(2):
                for q in range(h * HALF // PAIR, (h + 1) * HALF // PAIR):
                    self.landed_with(act, i - 1, q)
                fill(i, h)
                if self.beside is not None:
                    for j in range(h * len(GROUPS) // 2, (h + 1) * len(GROUPS) // 2):
                        self.beside.scalar_group(act, i, j)

    def gpsimd(self, pool):
        c = self.c
        with pool.Fori(0, self.trips) as i:
            for q in range(STEP_PAIRS):
                if q % (HALF // PAIR) == 0:
                    c.hold(pool, "gpsimd", self.index_ready.sem, self.i0 + 2 * i + q // (HALF // PAIR) + 1)
                c.hold(pool, "gpsimd", self.summed.sem, self.s0 + STEP_PAIRS * i + q - self.slots + 1)
                for k in range(PAIR * q, PAIR * (q + 1)):
                    pool.indirect_dma_start(self.rows[:, k % (self.slots * PAIR), 0:self.width], None,
                                            c.table if self.width == D else c.wide_table,
                                            bass.IndirectOffsetOnAxis(ap=self.ring[:, k:k + 1], axis=0)
                                            ).then_inc(self.landed[q % self.slots].sem, 16)

    def tensor(self, pe):
        c = self.c
        pe.wait_ge(self.cleared.sem, self.z0 + 2)
        with pe.Fori(0, self.trips) as i:
            for q in range(STEP_PAIRS):
                pe.wait_ge(self.onehot_ready.sem, self.o0 + STEP_PAIRS * i + q + 1)
                pe.wait_ge(self.added.sem, self.a0 + STEP_PAIRS * i + q - SHORT + 1)
                self.landed_with(pe, i, q)
                for a in range(PAIR):
                    ins = pe.matmul(c.bank[q % SHORT][:, 0:self.total], self.onehot[:, q % SHORT * PAIR + a, :],
                                    self.rows[:, (q % self.slots) * PAIR + a, 0:self.total],
                                    start=a == 0, stop=a == PAIR - 1)
                ins.then_inc(self.summed.sem, 1)
                if self.beside is not None and q in TURN_AFTER:
                    self.beside.tensor_group(pe, i, TURN_AFTER.index(q))

    def vector(self, dve):
        c, e = self.c, self.edges
        dve.memset(c.big_a[:, 0:TILES * self.total], 0.0).then_inc(self.cleared.sem, 1)
        dve.memset(self.rows[:, :, self.width:self.width + 1], 1.0).then_inc(self.cleared.sem, 1)
        dve.wait_ge(self.cleared.sem, self.z0 + 2)

        def select(i, q):
            dve.wait_ge(self.summed.sem, self.s0 + STEP_PAIRS * i + q - SHORT + 1)
            for a in range(PAIR):
                at = bass.ds(RING * i + PAIR * q + a, 1)
                to = self.onehot[:, q % SHORT * PAIR + a, :]
                if e.value is None:
                    ins = dve.tensor_scalar(to, c.iota[:, 0:P], e.node[:, at], None, ALU.is_equal)
                else:
                    ins = dve.tensor_scalar(to, c.iota[:, 0:P], e.node[:, at], e.value[:, at],
                                            ALU.is_equal, ALU.mult)
            ins.then_inc(self.onehot_ready.sem, 1)

        def step(i, last):
            r = e.tile_row
            for q in range(STEP_PAIRS):
                tile = dve.value_load(c.pair_tiles[r:r + 1, bass.ds(STEP_PAIRS * i + q, 1)],
                                      min_val=0, max_val=TILES - 1)
                dve.wait_ge(self.summed.sem, self.s0 + STEP_PAIRS * i + q + 1)
                dve.wait_ge(self.added.sem, self.a0 + STEP_PAIRS * i + q)
                into = self.sums[:, bass.ds(tile, 1), :]
                part = c.bank[q % SHORT][:, 0:self.total].rearrange("p (a d) -> p a d", a=1)
                dve.tensor_tensor(into, into, part, ALU.add).then_inc(self.added.sem, 1)
                if q + AHEAD < STEP_PAIRS:
                    select(i, q + AHEAD)
                elif not last:
                    select(i + 1, q + AHEAD - STEP_PAIRS)
                if self.beside is not None and q in TAKE_AFTER:
                    self.beside.vector_group(dve, i, TAKE_AFTER.index(q))

        for q in range(AHEAD):
            select(0, q)
        with dve.Fori(0, self.trips - 1) as i:
            step(i, False)
        step(self.trips - 1, True)
        if self.beside is not None:
            self.beside.vector_end(dve)


class LastEdge:

    def __init__(self, c, edges, back, room):
        self.c, self.edges = c, edges
        self.trips = CHUNKS // RING
        self.back = back[:, 0:CHUNKS * 4].rearrange("p (c r) -> p c r", r=4)
        self.nodes, self.ids, self.minus, self.best, self.masked = (
            room[:, k * CHUNKS:(k + 1) * CHUNKS] for k in range(5))
        at = 5 * CHUNKS
        self.apart = room[:, at:at + 4 * P].rearrange("p (k d) -> p k d", d=P)
        self.tagged = room[:, at + 4 * P:at + 12 * P].rearrange("p (s k d) -> p s k d", s=2, d=P)
        n = self.trips * len(GROUPS)
        self.apart_ready = c.counter("distances_ready")
        self.d0 = self.apart_ready.reserve(n)
        self.tagged_ready = c.counter("tagged_ready")
        self.t0 = self.tagged_ready.reserve(n)
        self.turned = c.counter("tagged_turned")
        self.u0 = self.turned.reserve(n)
        self.taken = c.counter("tagged_taken")
        self.k0 = self.taken.reserve(n)

    def prepare(self, dve):
        yield dve.tensor_copy(self.nodes, self.back[:, :, 1])
        yield dve.tensor_copy(self.ids, self.back[:, :, 3])
        yield dve.tensor_scalar(self.minus, self.ids, -1.0, None, ALU.mult)

    def chunks(self, i, j):
        return [RING * i + sum(GROUPS[:j]) + k for k in range(GROUPS[j])]

    def scalar_group(self, act, i, j):
        c, n = self.c, len(GROUPS) * i + j
        act.wait_ge(self.tagged_ready.sem, self.t0 + n)
        for k, chunk in enumerate(self.chunks(i, j)):
            ins = act.activation(self.apart[:, k, :], c.iota[:, 0:P], ACT.Abs,
                                 bias=self.nodes[:, bass.ds(chunk, 1)], scale=-1.0)
        ins.then_inc(self.apart_ready.sem, 1)
        act.wait_ge(self.apart_ready.sem, self.d0 + n + 1)
        act.wait_ge(self.turned.sem, self.u0 + n - 1)
        for k, chunk in enumerate(self.chunks(i, j)):
            at = bass.ds(chunk, 1)
            ins = act.activation(self.tagged[:, j % 2, k, :], self.apart[:, k, :], ACT.Relu,
                                 bias=self.ids[:, at], scale=self.minus[:, at])
        ins.then_inc(self.tagged_ready.sem, 1)

    def bank(self, j):
        return self.c.bank[SHORT + j % 2][:, 0:GROUPS[j] * P]

    def tensor_group(self, pe, i, j):
        n = len(GROUPS) * i + j
        pe.wait_ge(self.tagged_ready.sem, self.t0 + n + 1)
        pe.wait_ge(self.taken.sem, self.k0 + n - 1)
        for k in range(GROUPS[j]):
            ins = pe.transpose(self.bank(j)[:, k * P:(k + 1) * P], self.tagged[:, j % 2, k, :],
                               self.c.ident[:, :])
        ins.then_inc(self.turned.sem, 1)

    def vector_group(self, dve, i, j):
        dve.wait_ge(self.turned.sem, self.u0 + len(GROUPS) * i + j + 1)
        dve.tensor_reduce(self.best[:, bass.ds(self.chunks(i, j)[0], GROUPS[j])],
                          self.bank(j).rearrange("p (k d) -> p k d", d=P), AX_X, ALU.max
                          ).then_inc(self.taken.sem, 1)

    def vector_end(self, dve):
        c, e, v = self.c, self.edges, self.c.v
        dve.wait_ge(self.taken.sem, self.k0 + len(GROUPS) * self.trips)
        with v.loop(dve, TILES, 2) as t:
            v.mark(dve.scalar_tensor_tensor(out=self.masked, in0=e.tile_all, scalar=c.iota[:, bass.ds(t, 1)],
                                            in1=self.best, op0=ALU.is_equal, op1=ALU.mult))
            v.wait(dve)
            v.mark(dve.tensor_reduce(c.last_edge[:, bass.ds(t, 1)], self.masked, AX_X, ALU.max))
            v.wait(dve)


class RowStats(Stage):

    def __init__(self, c, src):
        self.c, self.src = c, src
        self.stats = c.arena[:, 0:TILES * 6]
        self.s = Statistics(c, TILES, 2, D)

    def vector(self, dve):
        c, v = self.c, self.c.v
        with v.loop(dve, BATCHES, BATCH) as i:
            for u in range(BATCH):
                v.mark(dve.bn_stats(self.stats.rearrange("p (t s) -> p t s", s=6)[:, tiles5(i, u), :],
                                    self.src[:, tiles5(i, u), :]))
        v.wait(dve)
        self.s.vector(dve, self.stats.rearrange("p (t g s) -> p t g s", g=2, s=3), c.mean[:, :], c.rstd[:, :])

    def scalar(self, act):
        self.s.scalar(act)


class Statistics:

    def __init__(self, c, rows, groups, width, uses=1):
        self.c, self.rows, self.groups, self.width = c, rows, groups, width
        n = rows * groups
        self.dev = c.stat_tmp[:, 0, 0:n].rearrange("p (t g) -> p t g", g=groups)
        self.sq = c.stat_tmp[:, 1, 0:n].rearrange("p (t g) -> p t g", g=groups)
        self.var, self.std = c.stat_tmp[:, 2, 0:rows], c.stat_tmp[:, 3, 0:rows]
        self.var_ready = c.counter("variance_ready")
        self.v0 = self.var_ready.reserve(uses)
        self.std_ready = c.counter("deviation_ready")
        self.d0 = self.std_ready.reserve(uses)
        self.STEPS = 7

    def vector(self, dve, stats, mean, rstd, use=0):
        v = self.c.v
        shape = [P, self.rows, self.groups]
        per_group = float(self.width // self.groups)
        v.mark(dve.tensor_reduce(mean, stats[:, :, :, 1], AX_X, ALU.add))
        v.wait(dve)
        v.mark(dve.tensor_scalar(mean, mean, 1.0 / self.groups, None, ALU.mult))
        v.wait(dve)
        v.mark(dve.tensor_tensor(self.dev, stats[:, :, :, 1], mean.unsqueeze(2).broadcast_to(shape), ALU.subtract))
        v.wait(dve)
        v.mark(dve.scalar_tensor_tensor(out=self.sq, in0=self.dev, scalar=per_group, in1=self.dev,
                                        op0=ALU.mult, op1=ALU.mult))
        v.wait(dve)
        v.mark(dve.tensor_tensor(self.sq, self.sq, stats[:, :, :, 2], ALU.add))
        v.wait(dve)
        v.mark(dve.tensor_reduce(self.var, self.sq, AX_X, ALU.add))
        v.wait(dve)
        dve.tensor_scalar(self.var, self.var, 1.0 / self.width, EPS, ALU.mult, ALU.add
                          ).then_inc(self.var_ready.sem, 1)
        dve.wait_ge(self.std_ready.sem, self.d0 + use + 1)
        v.mark(dve.reciprocal(rstd, self.std))
        v.wait(dve)

    def scalar(self, act, use=0):
        act.wait_ge(self.var_ready.sem, self.v0 + use + 1)
        act.activation(self.std, self.var, ACT.Sqrt).then_inc(self.std_ready.sem, 1)


class Project(Stage):

    def __init__(self, c, K, N, weights, prepare, take, taker, affine=None, store=None, keep_columns=None,
                 tag="", steps=0, before_batch=None, rows=None, columns=None, first_bank=2):
        self.c, self.K, self.N, self.w = c, K, N, weights
        self.prepare, self.take, self.taker, self.affine, self.store = prepare, take, taker, affine, store
        self.keep, self.steps, self.before_batch, self.first_bank = keep_columns, steps, before_batch, first_bank
        self.blocks = K // P
        self.G = -(-self.blocks // 4)
        self.C = -(-N // 512)
        rows = c.arena[:, 0:BATCH * K] if rows is None else rows
        columns = c.arena[:, 5120:5120 + 2 * self.blocks * P] if columns is None else columns
        self.rows = rows.rearrange("p (u d) -> p u d", d=K)
        self.columns = columns.rearrange("p (s n) -> p s n", s=2)
        self.masked = c.arena[:, 5632:5632 + 2 * P]
        n = TILES
        self.row_ready = c.counter(tag + "rows_ready")
        self.r0 = self.row_ready.reserve(n)
        self.turned = c.counter(tag + "rows_turned")
        self.t0 = self.turned.reserve(n * self.G)
        self.column_ready = c.counter(tag + "columns_ready")
        self.c0 = self.column_ready.reserve(n * self.G)
        self.product = c.counter(tag + "product_ready")
        self.p0 = self.product.reserve(n)
        self.used = c.counter(tag + "product_used")
        self.u0 = self.used.reserve(n)
        self.kept = c.counter(tag + "columns_kept")
        self.k0 = self.kept.reserve(n if keep_columns is not None else 0)
        self.stored = c.store.reserve(16 * BATCHES if store is not None else 0)

    def banks(self, u):
        return [self.c.bank[self.first_bank + (u % 2) * self.C + j] for j in range(self.C)]

    def turn_bank(self, u, g):
        return self.c.bank[(u * self.G + g) % 2]

    def tensor_batch(self, pe, i):
        c = self.c

        def turn(i, u):
            pe.wait_ge(self.row_ready.sem, self.r0 + BATCH * i + u + 1)
            for g in range(self.G):
                copied = before(i, u) if self.G == 1 else 2 * (BATCH * i + u - 1) + g + 1
                pe.wait_ge(self.column_ready.sem, self.c0 + copied)
                for b in range(4 * g, min(4 * g + 4, self.blocks)):
                    ins = pe.transpose(self.turn_bank(u, g)[:, (b % 4) * P:(b % 4 + 1) * P],
                                       self.rows[:, u, b * P:(b + 1) * P], c.ident[:, :])
                ins.then_inc(self.turned.sem, 1)

        def multiply(i, u):
            pe.wait_ge(self.column_ready.sem, self.c0 + self.G * (BATCH * i + u + 1))
            pe.wait_ge(self.used.sem, self.u0 + before(i, u))
            for j, bank in enumerate(self.banks(u)):
                lo, hi = j * 512, min(j * 512 + 512, self.N)
                for b in range(self.blocks):
                    ins = pe.matmul(bank[:, 0:hi - lo], self.columns[:, u % 2, b * P:(b + 1) * P],
                                    self.w[:, b, lo:hi], start=b == 0, stop=b == self.blocks - 1)
            ins.then_inc(self.product.sem, 1)

        turn(i, 0)
        for u in range(BATCH):
            if u + 1 < BATCH:
                turn(i, u + 1)
            multiply(i, u)

    def tensor(self, pe):
        with pe.Fori(0, BATCHES) as i:
            self.tensor_batch(pe, i)

    def copy_columns(self, act, i, u):
        for g in range(self.G):
            act.wait_ge(self.turned.sem, self.t0 + self.G * (BATCH * i + u) + g + 1)
            if g == 0:
                act.wait_ge(self.product.sem, self.p0 + before(i, u))
                if self.keep is not None:
                    act.wait_ge(self.kept.sem, self.k0 + before(i, u))
            hi = min(4 * g + 4, self.blocks)
            bank = self.turn_bank(u, g)
            if self.affine is None:
                ins = act.copy(self.columns[:, u % 2, 4 * g * P:hi * P], bank[:, 0:(hi - 4 * g) * P])
            else:
                gain, shift = self.affine
                for b in range(4 * g, hi):
                    ins = act.activation(self.columns[:, u % 2, b * P:(b + 1) * P],
                                         bank[:, (b - 4 * g) * P:(b - 4 * g + 1) * P], ACT.Identity,
                                         bias=shift[:, b:b + 1], scale=gain[:, b:b + 1])
            ins.then_inc(self.column_ready.sem, 1)

    def take_one(self, eng, i, u):
        eng.wait_ge(self.product.sem, self.p0 + BATCH * i + u + 1)
        self.take(eng, i, u, self.banks(u)).then_inc(self.used.sem, 1)

    def scalar_batch(self, act, i):
        self.copy_columns(act, i, 0)
        for u in range(BATCH):
            if u + 1 < BATCH:
                self.copy_columns(act, i, u + 1)
            if self.taker == "scalar":
                self.take_one(act, i, u)

    def scalar(self, act):
        with act.Fori(0, BATCHES) as i:
            if self.before_batch is not None:
                self.before_batch.scalar(act, i)
            self.scalar_batch(act, i)

    def vector_batch(self, dve, i):
        if self.before_batch is not None:
            self.before_batch.vector(dve, i)
        for u in range(BATCH):
            dve.wait_ge(self.turned.sem, self.t0 + self.G * (BATCH * (i - 1) + u + 1))
            self.prepare(dve, i, u, self.rows[:, u, :]).then_inc(self.row_ready.sem, 1)
        for u in range(BATCH):
            if self.keep is not None:
                dve.wait_ge(self.column_ready.sem, self.c0 + self.G * (BATCH * i + u + 1))
                high, low = self.keep
                at = bass.ds((i * BATCH + u) * P, P)
                dve.wait_ge(self.kept.sem, self.k0 + BATCH * i + u)
                self.c.v.mark(high_bits(dve, self.masked, self.columns[:, u % 2, :]))
                self.c.v.wait(dve)
                for b in range(self.blocks):
                    masked = self.masked[:, b * P:(b + 1) * P]
                    self.c.v.mark(dve.tensor_copy(high[b][:, at], masked))
                    ins = dve.tensor_tensor(low[b][:, at], self.columns[:, u % 2, b * P:(b + 1) * P], masked,
                                            ALU.subtract)
                ins.then_inc(self.kept.sem, 1)
            if self.taker == "vector":
                self.take_one(dve, i, u)

    def vector(self, dve):
        with self.c.v.loop(dve, BATCHES, self.steps) as i:
            self.vector_batch(dve, i)

    def takes_part(self, name):
        return self.store is not None if name == "sync" else name != "gpsimd"

    def sync(self, sp):
        src, to = self.store
        with sp.Fori(0, BATCHES) as i:
            sp.wait_ge(self.used.sem, self.u0 + BATCH * (i + 1))
            sp.dma_start(to.rearrange("(t p) d -> p t d", p=P)[:, bass.ds(i * BATCH, BATCH), :],
                         src[:, bass.ds(i * BATCH, BATCH), :]).then_inc(self.c.store.sem, 16)
        sp.wait_ge(self.c.store.sem, self.stored + 16 * BATCHES)


class TurnWeights(Stage):

    def __init__(self, c, W, rows, K, vectors=()):
        self.c, self.W, self.parts, self.blocks, self.rows = c, W, rows // P, K // P, rows
        self.plain = c.arena[:, 0:self.parts * K].rearrange("p (r k) -> p r k", k=K)
        self.out = c.w_area[:, 0:self.blocks * rows].rearrange("p (b n) -> p b n", n=rows)
        self.vectors = vectors
        self.l0 = c.loads.reserve(16 * len(vectors))
        self.landed = c.counter("plain_weights_landed")
        self.n0 = self.landed.reserve(16)
        self.turned = c.counter("weights_turned")
        self.t0 = self.turned.reserve(self.blocks)

    def sync(self, sp):
        c = self.c
        sp.dma_start(self.plain, self.W.rearrange("(r p) k -> p r k", p=P)).then_inc(self.landed.sem, 16)
        for to, src in self.vectors:
            sp.dma_start(to, src).then_inc(c.loads.sem, 16)
        sp.wait_ge(self.landed.sem, self.n0 + 16)
        sp.wait_ge(c.loads.sem, self.l0 + 16 * len(self.vectors))

    def tensor(self, pe):
        pe.wait_ge(self.landed.sem, self.n0 + 16)
        for b in range(self.blocks):
            for r in range(self.parts):
                ins = pe.transpose(self.c.bank[b][:, r * P:(r + 1) * P], self.plain[:, r, b * P:(b + 1) * P],
                                   self.c.ident[:, :])
            ins.then_inc(self.turned.sem, 1)

    def scalar(self, act):
        for b in range(self.blocks):
            act.wait_ge(self.turned.sem, self.t0 + b + 1)
            act.copy(self.out[:, b, :], self.c.bank[b][:, 0:self.rows])


class Load(Stage):

    def __init__(self, c, pairs):
        self.c, self.pairs = c, pairs
        self.l0 = c.loads.reserve(16 * len(pairs))

    def sync(self, sp):
        for to, src in self.pairs:
            with self.c.nc.allow_non_contiguous_dma(reason="vectors of a few hundred elements"):
                sp.dma_start(to, src).then_inc(self.c.loads.sem, 16)
        sp.wait_ge(self.c.loads.sem, self.l0 + 16 * len(self.pairs))


def over(ap, width):
    return ap.unsqueeze(2).broadcast_to([ap.shape[0], ap.shape[1], width])


def along(ap, n):
    return ap.unsqueeze(1).broadcast_to([ap.shape[0], n, ap.shape[1]])


class Steps(Stage):

    def __init__(self, c, make):
        self.c, self.make = c, make

    def vector(self, dve):
        for ins in self.make(dve):
            self.c.v.mark(ins)
            self.c.v.wait(dve)


class StoreTable(Stage):

    def __init__(self, c, src):
        self.c, self.src = c, src
        self.s0 = c.store.reserve(16)

    def sync(self, sp):
        sp.dma_start(self.c.table.rearrange("(t p) d -> p t d", p=P), self.src).then_inc(self.c.store.sem, 16)
        sp.wait_ge(self.c.store.sem, self.s0 + 16)


class BatchNorm(Stage):

    def __init__(self, c, sums, gamma, beta):
        self.c, self.gamma, self.beta = c, gamma, beta
        self.sums = sums
        self.centred = c.big_b[:, 0:TILES * D].rearrange("p (t d) -> p t d", d=D)
        self.square = c.big_b[:, TILES * D:2 * TILES * D].rearrange("p (t d) -> p t d", d=D)
        self.mean, self.gain = c.arena[:, 0:D], c.arena[:, D:2 * D]
        self.ready = c.counter("columns_to_sum")
        self.r0 = self.ready.reserve(1)
        self.summed = c.counter("columns_summed")
        self.s0 = self.summed.reserve(2)
        self.asked = c.counter("norm_asked")
        self.q0 = self.asked.reserve(3)
        self.answered = c.counter("norm_answered")
        self.n0 = self.answered.reserve(3)

    def tensor(self, pe):
        c = self.c
        for n, what in enumerate((self.sums[:, :, 0:D], self.square)):
            if n == 1:
                pe.wait_ge(self.ready.sem, self.r0 + 1)
            out = c.bank[n][:, 0:D]
            pe.matmul(out, c.ones[:, :], what[:, 0, :], start=True, stop=False)
            with pe.Fori(1, TILES - 1) as t:
                pe.matmul(out, c.ones[:, :], what[:, bass.ds(t, 1), :], start=False, stop=False)
            pe.matmul(out, c.ones[0:LAST, :], what[0:LAST, TILES - 1, :], start=False, stop=True).then_inc(self.summed.sem, 1)

    def vector(self, dve):
        c, v = self.c, self.c.v
        deg = c.dinv[:, :]
        dve.tensor_scalar(deg, self.sums[:, :, D], 1.0, None, ALU.add).then_inc(self.asked.sem, 1)
        dve.wait_ge(self.answered.sem, self.n0 + 1)
        v.mark(dve.reciprocal(deg, deg))
        dve.wait_ge(self.summed.sem, self.s0 + 1)
        v.mark(dve.tensor_scalar(self.mean, c.bank[0][:, 0:D], 1.0 / NODES, None, ALU.mult))
        v.wait(dve)
        v.mark(dve.tensor_tensor(self.centred, self.sums[:, :, 0:D], along(self.mean, TILES), ALU.subtract))
        v.wait(dve)
        dve.tensor_tensor(self.square, self.centred, self.centred, ALU.mult).then_inc(self.ready.sem, 1)
        dve.wait_ge(self.summed.sem, self.s0 + 2)
        dve.tensor_scalar(self.gain, c.bank[1][:, 0:D], 1.0 / NODES, EPS, ALU.mult, ALU.add
                          ).then_inc(self.asked.sem, 1)
        dve.wait_ge(self.answered.sem, self.n0 + 2)
        v.mark(dve.reciprocal(self.gain, self.gain))
        v.wait(dve)
        v.mark(dve.tensor_tensor(self.gain, self.gain, self.gamma, ALU.mult))
        v.wait(dve)
        v.mark(dve.tensor_tensor(self.centred, self.centred, along(self.gain, TILES), ALU.mult))
        v.wait(dve)
        v.mark(dve.tensor_tensor(self.centred, self.centred, along(self.beta, TILES), ALU.add))
        v.wait(dve)
        dve.tensor_scalar(self.square, self.centred, 0.0, None, ALU.min).then_inc(self.asked.sem, 1)
        h = self.sums[:, :, 0:D]
        v.mark(dve.tensor_tensor(h, c.x[:, :, :], over(c.mean[:, :], D), ALU.subtract))
        v.wait(dve)
        v.mark(dve.tensor_tensor(h, h, over(c.rstd[:, :], D), ALU.mult))
        v.wait(dve)
        v.mark(dve.scalar_tensor_tensor(out=h, in0=self.centred, scalar=0.0, in1=h, op0=ALU.max, op1=ALU.add))
        v.wait(dve)
        dve.wait_ge(self.answered.sem, self.n0 + 3)
        v.mark(dve.scalar_tensor_tensor(out=h, in0=self.square, scalar=-1.0, in1=h, op0=ALU.add, op1=ALU.add))
        v.wait(dve)
        v.mark(dve.tensor_tensor(c.x[:, :, :], c.x[:, :, :], h, ALU.add))
        v.wait(dve)

    def scalar(self, act):
        c = self.c
        act.wait_ge(self.asked.sem, self.q0 + 1)
        act.activation(c.dinv[:, :], c.dinv[:, :], ACT.Sqrt).then_inc(self.answered.sem, 1)
        act.wait_ge(self.asked.sem, self.q0 + 2)
        act.activation(self.gain, self.gain, ACT.Sqrt).then_inc(self.answered.sem, 1)
        act.wait_ge(self.asked.sem, self.q0 + 3)
        act.activation(self.square, self.square, ACT.Exp).then_inc(self.answered.sem, 1)


class Route(Stage):

    def __init__(self, c, logits, kind):
        self.c, self.logits, self.kind = c, logits, kind
        self.T = 1 if kind == "pooled" else TILES
        n = [0]

        def part(size):
            n[0] += size
            return c.arena[:, n[0] - size:n[0]]

        T = self.T
        self.l, self.l2, self.eq, self.first, self.second, self.p = (
            part(T * EXPERTS).rearrange("p (t e) -> p t e", e=EXPERTS) for _ in range(6))
        self.m1, self.m2, self.at, self.e2, self.s, self.w1, self.w2 = (part(T) for _ in range(7))
        self.below = part(EXPERTS)
        self.load = part(EXPERTS)
        self.asked = c.counter("exp_asked")
        self.answered = c.counter("exp_answered")
        self.n = {"softmax": 1, "probs": 2, "pooled": 3}[kind]
        self.q0, self.a0 = self.asked.reserve(self.n), self.answered.reserve(self.n)
        self.pool_sum = c.counter("logits_summed")
        self.p0 = self.pool_sum.reserve(1 if kind == "pooled" else 0)
        self.exps = {"softmax": [self.e2], "probs": [self.e2, self.p],
                     "pooled": [self.l, self.l2, self.e2]}[kind]

    def takes_part(self, name):
        return name in ("vector", "scalar") or (name == "tensor" and self.kind == "pooled")

    def tensor(self, pe):
        c = self.c
        pe.matmul(c.bank[0][:, 0:(TILES - 1) * EXPERTS], c.ones[:, :],
                  self.logits[:, 0:TILES - 1, :].rearrange("p t e -> p (t e)"), start=True, stop=True)
        pe.matmul(c.bank[1][:, 0:EXPERTS], c.ones[0:LAST, :], self.logits[0:LAST, TILES - 1, :],
                  start=True, stop=True).then_inc(self.pool_sum.sem, 1)

    def scalar(self, act):
        for n, what in enumerate(self.exps):
            act.wait_ge(self.asked.sem, self.q0 + n + 1)
            act.activation(what, what, ACT.Exp).then_inc(self.answered.sem, 1)

    def vector(self, dve):
        c, v, T = self.c, self.c.v, self.T
        asked = [0]

        def step(ins):
            v.mark(ins)
            v.wait(dve)

        def exp(ins):
            ins.then_inc(self.asked.sem, 1)
            asked[0] += 1
            dve.wait_ge(self.answered.sem, self.a0 + asked[0])

        logits = self.logits
        step(dve.tensor_scalar(self.below, c.iota[:, 0:EXPERTS], float(-EXPERTS), None, ALU.add))
        if self.kind == "pooled":
            dve.wait_ge(self.pool_sum.sem, self.p0 + 1)
            logits = self.l
            l, l2 = self.l[:, 0, :], self.l2[:, 0, :]
            step(dve.tensor_reduce(l, c.bank[0][:, 0:(TILES - 1) * EXPERTS].rearrange("p (t e) -> p e t", e=EXPERTS),
                                   AX_X, ALU.add))
            step(dve.tensor_tensor(l, l, c.bank[1][:, 0:EXPERTS], ALU.add))
            step(dve.tensor_scalar(l, l, 1.0 / NODES, None, ALU.mult))
            capacity = float(-(-NODES * 5 // (4 * EXPERTS)))
            for which, a in enumerate((l, l2)):
                step(dve.tensor_reduce(self.m1, a, AX_X, ALU.max))
                exp(dve.tensor_scalar(a, a, self.m1[:, 0:1], None, ALU.subtract))
                step(dve.tensor_reduce(self.s, a, AX_X, ALU.add))
                step(dve.reciprocal(self.s, self.s))
                step(dve.tensor_scalar(a, a, self.s[:, 0:1], None, ALU.mult))
                if which == 0:
                    step(dve.tensor_scalar(self.load, a, float(NODES), None, ALU.mult))
                    step(dve.tensor_scalar(self.eq[:, 0, :], self.load, capacity, None, ALU.is_gt))
                    step(dve.tensor_scalar(self.load, self.load, capacity, None, ALU.max))
                    step(dve.reciprocal(self.load, self.load))
                    step(dve.tensor_scalar(self.load, self.load, capacity, -1.0, ALU.mult, ALU.add))
                    step(dve.tensor_tensor(self.load, self.load, self.eq[:, 0, :], ALU.mult))
                    step(dve.scalar_tensor_tensor(out=l2, in0=self.load, scalar=1.0, in1=a,
                                                  op0=ALU.add, op1=ALU.mult))
            logits = self.l2
        below = along(self.below, T)

        def pick(values, best, onehot):
            step(dve.tensor_reduce(best, values, AX_X, ALU.max))
            step(dve.tensor_tensor(self.eq, values, over(best, EXPERTS), ALU.is_equal))
            step(dve.tensor_tensor(self.eq, self.eq, below, ALU.mult))
            step(dve.tensor_reduce(self.at, self.eq, AX_X, ALU.min))
            step(dve.tensor_tensor(onehot, below, over(self.at, EXPERTS), ALU.is_equal))

        pick(logits, self.m1, self.first)
        if self.kind == "pooled":
            step(dve.tensor_scalar(c.chosen[:, 0:1], self.at, float(EXPERTS), None, ALU.add))
        rest = self.p
        step(dve.scalar_tensor_tensor(out=rest, in0=self.first, scalar=-1e30, in1=logits, op0=ALU.mult, op1=ALU.add))
        pick(rest, self.m2, self.second)
        if self.kind == "pooled":
            step(dve.tensor_scalar(c.chosen[:, 1:2], self.at, float(EXPERTS), None, ALU.add))
        exp(dve.tensor_tensor(self.e2, self.m2, self.m1, ALU.subtract))
        if self.kind == "probs":
            exp(dve.tensor_tensor(self.p, logits, over(self.m1, EXPERTS), ALU.subtract))
            step(dve.tensor_reduce(self.s, self.p, AX_X, ALU.add))
            step(dve.reciprocal(self.w1, self.s))
            step(dve.tensor_tensor(self.w2, self.e2, self.w1, ALU.mult))
            step(dve.tensor_tensor(self.s, self.w1, self.w2, ALU.add))
            step(dve.tensor_scalar(self.s, self.s, 1e-12, None, ALU.max))
            step(dve.reciprocal(self.s, self.s))
            step(dve.tensor_tensor(self.w1, self.w1, self.s, ALU.mult))
            step(dve.tensor_tensor(self.w2, self.w2, self.s, ALU.mult))
        else:
            step(dve.tensor_scalar(self.s, self.e2, 1.0, None, ALU.add))
            step(dve.reciprocal(self.w1, self.s))
            step(dve.tensor_tensor(self.w2, self.e2, self.w1, ALU.mult))
        step(dve.tensor_tensor(self.first, self.first, over(self.w1, EXPERTS), ALU.mult))
        step(dve.tensor_tensor(self.second, self.second, over(self.w2, EXPERTS), ALU.mult))
        if T == 1:
            step(dve.tensor_tensor(self.first, self.first, self.second, ALU.add))
            step(dve.tensor_copy(c.gates[:, :, :], along(self.first[:, 0, :], TILES)))
            step(dve.tensor_copy(c.chosen_weight[:, 0:1], self.w1))
            step(dve.tensor_copy(c.chosen_weight[:, 1:2], self.w2))
        else:
            step(dve.tensor_tensor(c.gates[:, :, :], self.first, self.second, ALU.add))


class BiasStart(Stage):

    def __init__(self, c, b2, out):
        self.c, self.b2, self.out = c, b2, out
        self.rows = c.arena[:, 0:BATCH * EXPERTS]
        self.turned_gates = c.arena[0:EXPERTS, 64:64 + BATCH * P]
        self.ready, self.turned, self.copied, self.product = (c.counter(f"gates_{w}") for w in
                                                              ("ready", "turned", "copied", "product"))
        self.r0, self.t0, self.c0, self.p0 = (s.reserve(BATCHES) for s in
                                              (self.ready, self.turned, self.copied, self.product))

    def vector(self, dve):
        c, v = self.c, self.c.v
        with v.loop(dve, BATCHES, BATCH) as i:
            dve.tensor_copy(self.rows.rearrange("p (t e) -> p t e", e=EXPERTS),
                            c.gates[:, bass.ds(i * BATCH, BATCH), :]).then_inc(self.ready.sem, 1)
            dve.wait_ge(self.product.sem, self.p0 + i + 1)
            for u in range(BATCH):
                v.mark(dve.tensor_copy(self.out[:, tiles5(i, u), :],
                                       c.bank[2 + u][:, 0:D].rearrange("p (a d) -> p a d", a=1)))
            v.wait(dve)

    def tensor(self, pe):
        c = self.c
        with pe.Fori(0, BATCHES) as i:
            pe.wait_ge(self.ready.sem, self.r0 + i + 1)
            for u in range(BATCH):
                ins = pe.transpose(c.bank[u // 4][0:EXPERTS, (u % 4) * P:(u % 4 + 1) * P],
                                   self.rows[:, u * EXPERTS:(u + 1) * EXPERTS], c.ident[:, :])
            ins.then_inc(self.turned.sem, 1)
            pe.wait_ge(self.copied.sem, self.c0 + i + 1)
            for u in range(BATCH):
                ins = pe.matmul(c.bank[2 + u][:, 0:D], self.turned_gates[:, u * P:(u + 1) * P], self.b2,
                                start=True, stop=True)
            ins.then_inc(self.product.sem, 1)

    def scalar(self, act):
        c = self.c
        with act.Fori(0, BATCHES) as i:
            act.wait_ge(self.turned.sem, self.t0 + i + 1)
            act.copy(self.turned_gates[:, 0:4 * P], c.bank[0][0:EXPERTS, :])
            act.copy(self.turned_gates[:, 4 * P:], c.bank[1][0:EXPERTS, 0:P]).then_inc(self.copied.sem, 1)


class Experts(Stage):

    def __init__(self, c, columns, out, W1, b1, W2, H, func, chosen=False):
        self.c, self.columns, self.out, self.H, self.func = c, columns, out, H, func
        self.W1, self.W2, self.b1, self.chosen = W1, W2, b1, chosen
        self.one_expert = H == 2 * UNIT
        self.trips = (2 if chosen else EXPERTS) // (1 if self.one_expert else 2)
        assert self.one_expert or not chosen
        self.MC, self.KC = UNIT // P, D // P
        self.width = BATCH * P
        self.half = self.width // 2
        size = self.KC * UNIT + self.MC * D

        def weights(area, at):
            return (area[:, at:at + self.KC * UNIT].rearrange("p (b n) -> p b n", n=UNIT),
                    area[:, at + self.KC * UNIT:at + size].rearrange("p (b n) -> p b n", n=D))

        self.plain = [weights(c.w_area, k * size) for k in range(2)]
        self.high = [weights(c.w_area_r, (2 + 2 * k) * size) for k in range(2)]
        self.low = [weights(c.w_area_r, (3 + 2 * k) * size) for k in range(2)]
        self.weights_masked = c.w_area[:, 6 * size:6 * size + self.KC * UNIT]
        assert 6 * size + self.KC * UNIT <= 7000
        n = self.MC * self.width
        self.hidden_high, self.hidden_low = (
            [c.arena_r[:, (2 * k + a) * n:(2 * k + a + 1) * n].rearrange("p (m n) -> p m n", m=self.MC)
             for k in range(2)] for a in range(2))
        self.hidden = [c.arena[:, 4 * n + m * self.width:4 * n + (m + 1) * self.width] for m in range(self.MC)]
        self.masked = c.arena[:, 4 * n + self.MC * self.width:4 * n + (self.MC + 1) * self.width]
        assert 4 * n + (self.MC + 1) * self.width <= RING_AT
        self.step_b1 = c.cols[:, 32:32 + 2 * self.MC]
        self.units = 2 * self.trips
        self.groups = self.units * BATCHES
        self.parts = 2 * self.MC
        self.bias = c.counter("step_bias_ready")
        self.b0 = self.bias.reserve(self.trips)
        self.landed = [c.counter(f"unit_weights{k}_landed") for k in range(2)]
        self.l0 = [s.reserve(32 * self.trips) for s in self.landed]
        self.split = c.counter("unit_weights_split")
        self.s0 = self.split.reserve(2 * self.units)
        self.up = c.counter("hidden_summed")
        self.u0 = self.up.reserve(self.groups * self.parts)
        self.active = c.counter("hidden_active")
        self.a0 = self.active.reserve(self.groups * self.parts)
        self.high_known = c.counter("hidden_masked")
        self.h0 = self.high_known.reserve(self.groups * self.MC)
        self.high_ready = c.counter("hidden_high_ready")
        self.i0 = self.high_ready.reserve(self.groups * self.MC)
        self.low_ready = c.counter("hidden_low_ready")
        self.r0 = self.low_ready.reserve(self.groups * self.MC)
        self.down = c.counter("expert_summed")
        self.d0 = self.down.reserve(self.groups * BATCH)
        self.added = c.counter("expert_added")
        self.g0 = self.added.reserve(self.groups * BATCH)

    def expert(self, eng, i, k):
        if self.chosen:
            return eng.value_load(self.c.chosen[0:1, bass.ds(i, 1)], min_val=0, max_val=EXPERTS - 1)
        return i if self.one_expert else 2 * i + k

    def sync(self, sp):
        with sp.Fori(0, self.trips) as i:
            for k in range(2):
                self.c.hold(sp, "sync", self.split.sem, self.s0 + 2 * (2 * i + k - 1))
                e = self.expert(sp, i, k)
                at = k * UNIT if self.one_expert else 0
                w1, w2 = self.plain[k]
                sp.dma_start(w1, self.W1[bass.ds(e, 1), :, at:at + UNIT].rearrange("a (b p) h -> p (a b) h", p=P)
                             ).then_inc(self.landed[k].sem, 16)
                sp.dma_start(w2, self.W2[bass.ds(e, 1), at:at + UNIT, :].rearrange("a (b p) h -> p (a b) h", p=P)
                             ).then_inc(self.landed[k].sem, 16)
        for k in range(2):
            sp.wait_ge(self.landed[k].sem, self.l0[k] + 32 * self.trips)

    def down_bank(self, n, u):
        return self.c.bank[4 + (BATCH * n + u) % 4][:, 0:D]

    def tensor(self, pe):
        c = self.c

        def product(out, pairs):
            terms = [(left[x], right[y]) for left, right in pairs for x, y in ((0, 0), (0, 1), (1, 0))]
            for n, (left, right) in enumerate(terms):
                ins = pe.matmul(out, left, right, start=n == 0,
                                stop=n == len(terms) - 1)
            return ins

        def up(i, n):
            k, g = divmod(n, BATCHES)
            if g == 0:
                pe.wait_ge(self.split.sem, self.s0 + 2 * (2 * i + k + 1))
            for q in range(self.parts):
                m, half = divmod(q, 2)
                count = self.parts * (2 * BATCHES * i + n) + q
                pe.wait_ge(self.active.sem, self.a0 + count - 3)
                at = g * self.width + half * self.half
                product(c.bank[q % 4][:, 0:self.half],
                        [([w[k][0][:, b, m * P:(m + 1) * P] for w in (self.high, self.low)],
                          [x[b][:, at:at + self.half] for x in self.columns]) for b in range(self.KC)]
                        ).then_inc(self.up.sem, 1)

        def down(i, n):
            k = n // BATCHES
            pe.wait_ge(self.high_ready.sem, self.i0 + self.MC * (2 * BATCHES * i + n + 1))
            pe.wait_ge(self.low_ready.sem, self.r0 + self.MC * (2 * BATCHES * i + n + 1))
            for u in range(BATCH):
                back = 2 if n == 0 and u < 2 else 4
                pe.wait_ge(self.added.sem, self.g0 + BATCH * (2 * BATCHES * i + n) + u + 1 - back)
                product(self.down_bank(n, u),
                        [([h[n % 2][:, m, u * P:(u + 1) * P] for h in (self.hidden_high, self.hidden_low)],
                          [w[k][1][:, m, :] for w in (self.high, self.low)]) for m in range(self.MC)]
                        ).then_inc(self.down.sem, 1)

        def step(i, last):
            for n in range(2 * BATCHES):
                if n + 1 < 2 * BATCHES:
                    up(i, n + 1)
                elif not last:
                    up(i + 1, 0)
                down(i, n)

        up(0, 0)
        with pe.Fori(0, self.trips - 1) as i:
            step(i, False)
        step(self.trips - 1, True)

    def scalar(self, act):
        c = self.c
        with act.Fori(0, self.trips) as i:
            c.hold(act, "scalar", self.active.sem, self.a0 + self.parts * 2 * BATCHES * i)
            columns = self.MC * 2
            first = self.expert(act, i, 0) * (columns if self.one_expert else columns // 2)
            act.copy(self.step_b1, self.b1[:, bass.ds(first, columns)]).then_inc(self.bias.sem, 1)
            act.wait_ge(self.bias.sem, self.b0 + i + 1)
            for n in range(2 * BATCHES):
                k, g = n // BATCHES, 2 * BATCHES * i + n

                def activate(q):
                    m, half = divmod(q, 2)
                    if half == 0:
                        act.wait_ge(self.low_ready.sem, self.r0 + self.MC * (g - 1) + m + 1)
                    act.wait_ge(self.up.sem, self.u0 + self.parts * g + q + 1)
                    act.activation(self.hidden[m][:, half * self.half:(half + 1) * self.half],
                                   c.bank[q % 4][:, 0:self.half], self.func,
                                   bias=self.step_b1[:, k * self.MC + m:k * self.MC + m + 1]
                                   ).then_inc(self.active.sem, 1)

                def round_high(m):
                    act.wait_ge(self.high_known.sem, self.h0 + self.MC * g + m + 1)
                    if m == 0:
                        act.wait_ge(self.down.sem, self.d0 + BATCH * (g - 1))
                    act.copy(self.hidden_high[n % 2][:, m, :], self.masked).then_inc(self.high_ready.sem, 1)

                activate(0)
                activate(1)
                activate(2)
                round_high(0)
                activate(3)
                round_high(1)

    def vector(self, dve):
        c, v = self.c, self.c.v

        def split_weights(i, k, which):
            if which == 0:
                dve.wait_ge(self.landed[k].sem, self.l0[k] + 32 * (i + 1))
                dve.wait_ge(self.down.sem, self.d0 + TILES * (2 * i + k - 1))
            plain, high, low = self.plain[k][which], self.high[k][which], self.low[k][which]
            masked = self.weights_masked.rearrange("p (b n) -> p b n", b=2)
            dve.wait_ge(self.split.sem, self.s0 + 2 * (2 * i + k) + which)
            v.mark(high_bits(dve, masked, plain))
            v.wait(dve)
            v.mark(dve.tensor_copy(high, masked))
            dve.tensor_tensor(low, plain, masked, ALU.subtract).then_inc(self.split.sem, 1)

        def split_hidden(i, n, m):
            g = 2 * BATCHES * i + n
            dve.wait_ge(self.active.sem, self.a0 + self.parts * g + 2 * (m + 1))
            dve.wait_ge(self.high_ready.sem, self.i0 + self.MC * g + m)
            dve.wait_ge(self.low_ready.sem, self.r0 + self.MC * g + m)
            if m == 0:
                dve.wait_ge(self.down.sem, self.d0 + BATCH * (g - 1))
            high_bits(dve, self.masked, self.hidden[m]).then_inc(self.high_known.sem, 1)
            dve.wait_ge(self.high_known.sem, self.h0 + self.MC * g + m + 1)
            dve.tensor_tensor(self.hidden_low[n % 2][:, m, :], self.hidden[m], self.masked, ALU.subtract
                              ).then_inc(self.low_ready.sem, 1)

        def add(i, n, u):
            k, g = divmod(n, BATCHES)
            t = g * BATCH + u
            count = BATCH * (2 * BATCHES * i + n) + u
            dve.wait_ge(self.down.sem, self.d0 + count + 1)
            if u == 0:
                dve.wait_ge(self.added.sem, self.g0 + count + BATCH - TILES)
            if self.chosen:
                gate = c.chosen_weight[:, bass.ds(i, 1)]
            else:
                gate = c.gates[:, t, bass.ds(self.expert(dve, i, k), 1)]
            dve.scalar_tensor_tensor(out=self.out[:, t, :], in0=self.down_bank(n, u), scalar=gate,
                                     in1=self.out[:, t, :], op0=ALU.mult, op1=ALU.add
                                     ).then_inc(self.added.sem, 1)

        def step(i, last):
            for n in range(2 * BATCHES):
                g = n % BATCHES
                if g in (1, 3) and not (last and n >= BATCHES):
                    split_weights(i + n // BATCHES, 1 - n // BATCHES, g // 2)
                after = (i, n + 1) if n + 1 < 2 * BATCHES else (i + 1, 0)
                more = not (last and n + 1 == 2 * BATCHES)
                if more:
                    split_hidden(*after, 0)
                add(i, n, 0)
                add(i, n, 1)
                if more:
                    split_hidden(*after, 1)
                for u in range(2, BATCH):
                    add(i, n, u)

        split_weights(0, 0, 0)
        split_weights(0, 0, 1)
        for m in range(self.MC):
            split_hidden(0, 0, m)
        with v.loop(dve, self.trips - 1, 8) as i:
            step(i, False)
        step(self.trips - 1, True)


class Finish(Stage):

    def __init__(self, c):
        self.c = c
        self.s0 = c.store.reserve(32)

    def sync(self, sp):
        c, whole = self.c, (TILES - 1) * P
        sp.dma_start(c.out[0:whole, :].rearrange("(t p) d -> p t d", p=P), c.x[:, 0:TILES - 1, :]
                     ).then_inc(c.store.sem, 16)
        sp.dma_start(c.out[whole:NODES, :], c.x[0:LAST, TILES - 1, :]).then_inc(c.store.sem, 16)
        sp.wait_ge(c.store.sem, self.s0 + 32)


def gnn_ffn_layers(nc, T, out, stages_of):
    with ExitStack() as ctx:
        c = Core(nc, ctx, T, out)
        stages = stages_of(c)
        number(stages, c.engines)
        block = ctx.enter_context(nc.Block())

        @block.sync
        def _(sp):
            for counter in c.counters.values():
                if counter.lead:
                    sp.sem_inc(counter.sem, counter.lead)
            c.run("sync", sp, stages)

        @block.tensor
        def _(pe):
            c.run("tensor", pe, stages)

        @block.vector
        def _(dve):
            c.run("vector", dve, stages)

        @block.scalar
        def _(act):
            c.run("scalar", act, stages)

        @block.gpsimd
        def _(pool):
            c.run("gpsimd", pool, stages)


class BetweenConvolutions:

    def __init__(self, c, rows, width, first=None):
        self.c, self.rows, self.width, self.first = c, rows, width, first
        self.chunks = -(-width // 512)
        self.groups = 2 * self.chunks
        self.stats = c.stat_in[:, 0:BATCH * self.groups * 3]
        self.mean, self.rstd = c.batch_mean[:, 0:BATCH], c.batch_mean[:, BATCH:2 * BATCH]
        self.s = Statistics(c, BATCH, self.groups, width, uses=BATCHES)
        self.steps = BATCH * self.chunks + self.s.STEPS

    def statistics(self, dve, i, ready):
        c, v = self.c, self.c.v
        for u in range(BATCH):
            ready(u)
            for j in range(self.chunks):
                n = min(512, self.width)
                at = (u * self.chunks + j) * 6
                v.mark(dve.bn_stats(self.stats[:, at:at + 6], self.rows[:, u, j * n:(j + 1) * n]))
        v.wait(dve)
        self.s.vector(dve, self.stats.rearrange("p (t g s) -> p t g s", g=self.groups, s=3),
                      self.mean, self.rstd, use=i)

    def normalise(self, dve, u):
        rows = self.rows[:, u, :]
        return dve.tensor_scalar(rows, rows, self.mean[:, u:u + 1], self.rstd[:, u:u + 1],
                                 ALU.subtract, ALU.mult)


class FirstConvolutions(Stage):

    def __init__(self, c, sums, own, W1, b1, W2, gain, shift, out, table):
        self.c = c
        hidden, width = 1024, 512

        def combine(dve, i, u, to):
            to3 = to.rearrange("p (a d) -> p a d", a=1)
            c.v.mark(dve.tensor_tensor(to3, sums[:, tiles5(i, u), :], own[:, tiles5(i, u), :], ALU.add))
            c.v.wait(dve)
            return dve.tensor_scalar(to, to, c.dinv[:, tiles5(i, u)], None, ALU.mult)

        def add_bias(dve, i, u, banks):
            dve.wait_ge(self.second.turned.sem, self.second.t0 + self.second.G * (BATCH * (i - 1) + u + 1))
            for j, bank in enumerate(banks):
                ins = dve.tensor_tensor(self.second.rows[:, u, j * 512:(j + 1) * 512], bank[:, :],
                                        b1[:, j * 512:(j + 1) * 512], ALU.add)
            return ins

        def scale(act, i, u, banks):
            return act.activation(out[:, tiles5(i, u), :], banks[0][:, :].rearrange("p (a d) -> p a d", a=1),
                                  ACT.Identity, scale=c.dinv[:, tiles5(i, u)])

        self.first = Project(c, D, hidden, W1, combine, add_bias, "vector", tag="first_",
                             rows=c.big_a[:, 6656:6656 + BATCH * D], columns=c.big_a[:, 8192:8192 + 2 * D])
        self.second = Project(c, hidden, width, W2, lambda dve, i, u, to: self.between.normalise(dve, u), scale,
                              "scalar", affine=(gain, shift), store=(out, table), first_bank=6)
        self.between = BetweenConvolutions(c, self.second.rows, hidden)
        self.relu_ready = c.counter("relu_ready")
        self.r0 = self.relu_ready.reserve(TILES)

    def tensor(self, pe):
        with pe.Fori(0, BATCHES) as i:
            self.first.tensor_batch(pe, i)
            self.second.tensor_batch(pe, i)

    def vector(self, dve):
        c = self.c

        def ready(u):
            dve.wait_ge(self.relu_ready.sem, self.r0 + BATCH * i + u + 1)

        with c.v.loop(dve, BATCHES, BATCH + self.between.steps) as i:
            self.first.vector_batch(dve, i)
            self.between.statistics(dve, i, ready)
            self.second.vector_batch(dve, i)

    def scalar(self, act):
        with act.Fori(0, BATCHES) as i:
            self.first.scalar_batch(act, i)
            for u in range(BATCH):
                act.wait_ge(self.first.used.sem, self.first.u0 + BATCH * i + u + 1)
                rows = self.second.rows[:, u, :]
                act.activation(rows, rows, ACT.Relu).then_inc(self.relu_ready.sem, 1)
            self.between.s.scalar(act, use=i)
            self.second.scalar_batch(act, i)

    def sync(self, sp):
        self.second.sync(sp)


class PrepareSecond:

    def __init__(self, c, project_of, sums, own, bias, width):
        self.c, self.project_of, self.sums, self.own, self.bias = c, project_of, sums, own, bias
        self.between = BetweenConvolutions(c, c.arena[:, 0:BATCH * width].rearrange("p (u d) -> p u d", d=width),
                                           width)
        self.steps = 3 * BATCH + self.between.steps

    def vector(self, dve, i):
        c, v, rows, project = self.c, self.c.v, self.between.rows, self.project_of()
        for u in range(BATCH):
            dve.wait_ge(project.turned.sem, project.t0 + project.G * (BATCH * (i - 1) + u + 1))
            v.mark(dve.tensor_tensor(rows[:, u:u + 1, :], self.sums[:, tiles5(i, u), :],
                                     self.own[:, tiles5(i, u), :], ALU.add))
        v.wait(dve)
        for u in range(BATCH):
            v.mark(dve.scalar_tensor_tensor(out=rows[:, u, :], in0=rows[:, u, :], scalar=c.dinv[:, tiles5(i, u)],
                                            in1=self.bias, op0=ALU.mult, op1=ALU.add))
        v.wait(dve)
        for u in range(BATCH):
            v.mark(dve.tensor_scalar(rows[:, u, :], rows[:, u, :], 0.0, None, ALU.max))
        v.wait(dve)
        self.between.statistics(dve, i, lambda u: None)

    def scalar(self, act, i):
        self.between.s.scalar(act, use=i)


class GatherLast(Stage):

    def __init__(self, c, out):
        self.c, self.out = c, out
        self.edge = c.arena[:, 0:TILES].bitcast(I32)
        self.edge_f = c.arena[:, 32:32 + TILES]
        self.has = c.arena[:, 64:64 + TILES]
        self.row = c.arena[:, 96:96 + TILES].bitcast(I32)
        self.ready = c.counter("last_edges_ready")
        self.r0 = self.ready.reserve(1)
        self.rows = c.counter("last_rows_landed", 0)
        self.l0 = self.rows.reserve(16 * TILES)
        self.landed = c.counter("last_features_landed", 0)
        self.n0 = self.landed.reserve(16 * TILES)

    def gpsimd(self, pool):
        c = self.c
        dst = c.T["dst"].rearrange("(e a) -> e a", a=1)
        pool.wait_ge(self.ready.sem, self.r0 + 1)
        for t in range(TILES):
            pool.indirect_dma_start(self.row[:, t:t + 1], None, dst,
                                    bass.IndirectOffsetOnAxis(ap=self.edge[:, t:t + 1], axis=0)
                                    ).then_inc(self.rows.sem, 16)
        pool.wait_ge(self.rows.sem, self.l0 + 16 * TILES)
        for t in range(TILES):
            pool.indirect_dma_start(self.out[:, t, :], None, c.table,
                                    bass.IndirectOffsetOnAxis(ap=self.row[:, t:t + 1], axis=0)
                                    ).then_inc(self.landed.sem, 16)

    def vector(self, dve):
        c, v = self.c, self.c.v
        v.mark(dve.tensor_scalar(self.edge_f, c.last_edge[:, :], 1.0, 0.0, ALU.subtract, ALU.max))
        v.mark(dve.tensor_scalar(self.has, c.last_edge[:, :], 0.0, None, ALU.is_gt))
        v.wait(dve)
        dve.tensor_copy(self.edge, self.edge_f).then_inc(self.ready.sem, 1)
        dve.wait_ge(self.landed.sem, self.n0 + 16 * TILES)
        v.mark(dve.tensor_tensor(self.out, self.out, over(self.has, D), ALU.mult))
        v.wait(dve)


def tiles_of(area, width=D, at=0):
    return area[:, at:at + TILES * width].rearrange("p (t d) -> p t d", d=width)


def network(c):
    T = c.T
    stages = []

    def do(stage):
        stages.append(stage)
        return stage

    def everywhere(name, at, n, area=None):
        to = (c.vec if area is None else area)[:, at:at + n]
        return to, T[name].partition_broadcast(P)

    def by_partition(name, at, n):
        return c.cols[:, at:at + n // P], T[name].rearrange("(b p) -> p b", p=P)

    def normalise_from(src):
        def prepare(dve, i, u, to):
            return dve.tensor_scalar(to.rearrange("p (a d) -> p a d", a=1), src[:, tiles5(i, u), :],
                                     c.mean[:, tiles5(i, u)], c.rstd[:, tiles5(i, u)], ALU.subtract, ALU.mult)
        return prepare

    def normalised(dve, out, src):
        yield dve.tensor_tensor(out, src, over(c.mean[:, :], D), ALU.subtract)
        yield dve.tensor_tensor(out, out, over(c.rstd[:, :], D), ALU.mult)

    x = c.x[:, :, :]
    sums = tiles_of(c.big_a)

    def project_nodes(W):
        do(RowStats(c, c.x))
        out = tiles_of(c.big_b)

        def take(act, i, u, banks):
            return act.copy(out[:, tiles5(i, u), :], banks[0][:, 0:D].rearrange("p (a d) -> p a d", a=1))

        do(Project(c, D, D, W, normalise_from(c.x), take, "scalar", store=(out, c.table)))

    def ffn(prefix, H, func, kind, src, affine, router, bias_names, W1, b1, W2, b2):
        HC = H // P
        n = TILES * P
        columns = [[area[:, k * n:(k + 1) * n] for area, k in places] for places in
                   (((c.big_b_r, 0), (c.big_b_r, 1)), ((c.big_b_r, 2), (c.big_a_r, 2)))]
        routing = c.w_area[:, 0:2 * EXPERTS].rearrange("p (b e) -> p b e", e=EXPERTS)
        br = c.w_area[:, 64:64 + EXPERTS]
        b1_columns = c.w_area[:, 7000:7000 + EXPERTS * HC]
        b2_rows = c.w_area[0:EXPERTS, 6400:6400 + D]
        pairs = [(b1_columns.rearrange("p (e m) -> p e m", e=EXPERTS), T[b1].rearrange("e (m p) -> p e m", p=P)),
                 (b2_rows, T[b2])]
        if kind == "probs":
            pairs += [(routing[:, b, :], T[router][:, b * P:(b + 1) * P].rearrange("e p -> p e")) for b in range(2)]
        else:
            pairs.append((routing, T[router].rearrange("(b p) e -> p b e", p=P)))
        biases = [c.w_area[:, 64 + 16 * k:64 + 16 * k + EXPERTS] for k in range(len(bias_names))]
        pairs += [(to, T[name].partition_broadcast(P)) for to, name in zip(biases, bias_names)]
        do(Load(c, pairs))
        if not biases:
            do(Steps(c, lambda dve: iter([dve.memset(br, 0.0)])))
        if len(biases) == 2:
            do(Steps(c, lambda dve: iter([dve.tensor_tensor(br, biases[0], biases[1], ALU.add)])))

        def take(dve, i, u, banks):
            return dve.tensor_tensor(c.logits[:, tiles5(i, u), :],
                                     banks[0][:, 0:EXPERTS].rearrange("p (a e) -> p a e", a=1),
                                     br.rearrange("p (a e) -> p a e", a=1), ALU.add)

        do(Project(c, D, EXPERTS, routing, normalise_from(src), take, "vector", affine=affine,
                   keep_columns=columns, steps=3 * BATCH))
        do(Route(c, c.logits, kind))
        do(BiasStart(c, b2_rows, sums))
        do(Experts(c, columns, sums, T[W1], b1_columns, T[W2], H, func, chosen=kind == "pooled"))

    do(Setup(c))
    by_src = do(SortPlan(c, "src", "src", "dst", "edge_weight", c.big_a[:, 10000:12800], 0))
    src_scatter = do(Scatter(c, by_src))
    do(ChunkTiles(c, by_src))
    by_dst = do(SortPlan(c, "dst", "dst", "src", None, c.big_b[:, 10000:12800], 32, made=by_src))
    do(ChunkTiles(c, by_dst))

    w0 = do(TurnWeights(c, T["L0_gnn_W"], D, D))
    project_nodes(w0.out)
    do(ReadSlots(c, by_src, src_scatter, c.big_a))
    do(GatherAdd(c, by_src, D))
    dst_scatter = do(Scatter(c, by_dst))
    do(Steps(c, lambda dve: iter([dve.tensor_tensor(x, x, sums, ALU.add)])))
    do(RowStats(c, c.x))
    do(Steps(c, lambda dve: normalised(dve, sums, x)))
    do(RowStats(c, sums))
    gain, shift = c.cols[:, 0:2], c.cols[:, 2:4]
    do(Load(c, [by_partition("L0_ffn_gamma", 0, D), by_partition("L0_ffn_beta", 2, D)]))
    ffn("L0", 512, ACT.Gelu, "softmax", sums, (gain, shift), "L0_ffn_Wr", ["L0_ffn_br"],
        "L0_ffn_W1", "L0_ffn_b1", "L0_ffn_W2", "L0_ffn_b2")
    do(Steps(c, lambda dve: iter([dve.tensor_tensor(x, x, sums, ALU.add)])))

    w1 = do(TurnWeights(c, T["L1_gnn_W"].rearrange("h o k -> (h o) k"), D, D))
    do(Load(c, [(c.vec[:, 0:D], T["L1_gnn_gamma"].rearrange("h o -> (h o)").partition_broadcast(P)),
                (c.vec[:, D:2 * D], T["L1_gnn_beta"].rearrange("h o -> (h o)").partition_broadcast(P))]))
    project_nodes(w1.out)
    do(ReadSlots(c, by_dst, dst_scatter, c.big_a))
    last_edge = LastEdge(c, by_src, c.big_b[:, 0:2000], c.big_b[:, 2000:10000])
    do(Load(c, [(c.big_b[:, 0:CHUNKS * 4], by_src.slots[:, 0:CHUNKS * 4])]))
    do(Steps(c, last_edge.prepare))
    with_degree = do(GatherAdd(c, by_dst, D, degree=True, beside=last_edge))
    do(BatchNorm(c, with_degree.sums, c.vec[:, 0:D], c.vec[:, D:2 * D]))
    do(RowStats(c, c.x))
    do(Load(c, [everywhere("L1_ffn_gamma", 0, D), everywhere("L1_ffn_beta", D, D)]))
    ffn("L1", 512, ACT.Gelu, "pooled", c.x, None, "L1_ffn_Wr", ["L1_ffn_br"],
        "L1_ffn_W1", "L1_ffn_b1", "L1_ffn_W2", "L1_ffn_b2")
    other = tiles_of(c.big_b)

    def residual(dve):
        yield from normalised(dve, other, x)
        yield dve.tensor_tensor(sums, sums, other, ALU.add)

    def normed(gamma, beta):
        def make(dve):
            yield from normalised(dve, sums, sums)
            yield dve.tensor_tensor(sums, sums, along(gamma, TILES), ALU.mult)
            yield dve.tensor_tensor(sums, sums, along(beta, TILES), ALU.add)
            yield dve.tensor_tensor(x, x, sums, ALU.add)
        return make

    do(Steps(c, residual))
    do(RowStats(c, sums))
    do(Steps(c, normed(c.vec[:, 0:D], c.vec[:, D:2 * D])))

    do(RowStats(c, c.x))
    own = tiles_of(c.big_b, D, TILES * D)

    def scaled(dve):
        yield from normalised(dve, own, x)
        yield dve.tensor_tensor(own, own, over(c.dinv[:, :], D), ALU.mult)

    do(Steps(c, scaled))
    do(StoreTable(c, own))
    conv1 = c.w_area[:, 0:2048].rearrange("p (b n) -> p b n", b=2)
    conv2 = c.w_area[:, 2048:6144].rearrange("p (b n) -> p b n", b=8)
    conv3 = c.w_area[:, 6144:7168].rearrange("p (b n) -> p b n", b=4)
    do(Load(c, [(w, T[name].rearrange("(b p) n -> p b n", p=P)) for w, name in
                ((conv1, "L2_gnn_W1"), (conv2, "L2_gnn_W2"), (conv3, "L2_gnn_W3"))]
            + [everywhere("L2_gnn_b1", 0, 1024), everywhere("L2_gnn_b2", 1024, 512),
               everywhere("L2_gnn_b3", 1536, D), everywhere("L2_gnn_g3", 1792, D),
               everywhere("L2_gnn_beta3", 2048, D),
               by_partition("L2_gnn_g1", 0, 1024), by_partition("L2_gnn_beta1", 8, 1024),
               by_partition("L2_gnn_g2", 16, 512), by_partition("L2_gnn_beta2", 20, 512)]))
    do(GatherAdd(c, by_dst, D))
    wide = tiles_of(c.big_b, 512)
    do(FirstConvolutions(c, sums, own, conv1, c.vec[:, 0:1024], conv2, c.cols[:, 0:8], c.cols[:, 8:16],
                         wide, c.wide_table))
    wide_sums = do(GatherAdd(c, by_dst, 512)).sums
    third = tiles_of(c.big_b)

    def scale(act, i, u, banks):
        return act.activation(third[:, tiles5(i, u), :], banks[0][:, 0:D].rearrange("p (a d) -> p a d", a=1),
                              ACT.Identity, scale=c.dinv[:, tiles5(i, u)])

    holder = []
    prepare = PrepareSecond(c, lambda: holder[0], wide_sums, wide, c.vec[:, 1024:1536], 512)
    holder.append(do(Project(c, 512, D, conv3, lambda dve, i, u, to: prepare.between.normalise(dve, u), scale,
                             "scalar", affine=(c.cols[:, 16:20], c.cols[:, 20:24]), store=(third, c.table),
                             steps=prepare.steps, before_batch=prepare)))
    do(GatherAdd(c, by_dst, D))

    def last_convolution(dve):
        yield dve.tensor_tensor(sums, sums, third, ALU.add)
        yield dve.tensor_tensor(sums, sums, over(c.dinv[:, :], D), ALU.mult)
        yield dve.tensor_tensor(sums, sums, along(c.vec[:, 1536:1792], TILES), ALU.add)
        yield dve.tensor_scalar(sums, sums, 0.0, None, ALU.max)

    do(Steps(c, last_convolution))
    do(RowStats(c, sums))
    do(Steps(c, normed(c.vec[:, 1792:2048], c.vec[:, 2048:2304])))
    do(RowStats(c, c.x))
    ffn("L2", 512, ACT.Relu, "softmax", c.x, None, "L2_ffn_Wg", ["L2_ffn_bg", "L2_ffn_bias"],
        "L2_ffn_W1", "L2_ffn_b1", "L2_ffn_W2", "L2_ffn_b2")
    do(Steps(c, lambda dve: iter([dve.tensor_tensor(x, x, sums, ALU.add)])))

    do(RowStats(c, c.x))
    do(Steps(c, lambda dve: normalised(dve, third, x)))
    do(StoreTable(c, third))
    do(GatherLast(c, sums))
    w3 = do(TurnWeights(c, T["L3_gnn_W"], D, 2 * D, [everywhere("L3_gnn_b", 0, D)]))
    do(Steps(c, lambda dve: iter([dve.tensor_tensor(x, x, along(c.vec[:, 0:D], TILES), ALU.add)])))

    def beside(dve, i, u, to):
        to = to.rearrange("p (a d) -> p a d", a=1)
        dve.tensor_copy(to[:, :, 0:D], third[:, tiles5(i, u), :])
        return dve.tensor_copy(to[:, :, D:2 * D], sums[:, tiles5(i, u), :])

    def add(dve, i, u, banks):
        tile = c.x[:, tiles5(i, u), :]
        return dve.tensor_tensor(tile, tile, banks[0][:, 0:D].rearrange("p (a d) -> p a d", a=1), ALU.add)

    do(Project(c, 2 * D, D, w3.out, beside, add, "vector"))
    do(RowStats(c, c.x))
    ffn("L3", 256, ACT.Gelu, "probs", c.x, None, "L3_ffn_router_w", [],
        "L3_ffn_w1", "L3_ffn_b1", "L3_ffn_w2", "L3_ffn_b2")

    def last(dve):
        yield from normalised(dve, third, x)
        yield dve.tensor_tensor(x, x, third, ALU.add)
        yield dve.tensor_tensor(x, x, sums, ALU.add)

    do(Steps(c, last))
    do(Finish(c))
    return stages


_INS = [
    'x', 'src', 'dst', 'edge_weight', 'L0_gnn_W', 'L0_ffn_gamma', 'L0_ffn_beta', 'L0_ffn_Wr', 'L0_ffn_br',
    'L0_ffn_W1', 'L0_ffn_b1', 'L0_ffn_W2', 'L0_ffn_b2', 'L1_gnn_W', 'L1_gnn_gamma', 'L1_gnn_beta', 'L1_ffn_Wr',
    'L1_ffn_br', 'L1_ffn_W1', 'L1_ffn_b1', 'L1_ffn_W2', 'L1_ffn_b2', 'L1_ffn_gamma', 'L1_ffn_beta', 'L2_gnn_W1',
    'L2_gnn_b1', 'L2_gnn_g1', 'L2_gnn_beta1', 'L2_gnn_W2', 'L2_gnn_b2', 'L2_gnn_g2', 'L2_gnn_beta2', 'L2_gnn_W3',
    'L2_gnn_b3', 'L2_gnn_g3', 'L2_gnn_beta3', 'L2_ffn_Wg', 'L2_ffn_bg', 'L2_ffn_bias', 'L2_ffn_W1', 'L2_ffn_b1',
    'L2_ffn_W2', 'L2_ffn_b2', 'L3_gnn_W', 'L3_gnn_b', 'L3_ffn_router_w', 'L3_ffn_w1', 'L3_ffn_b1', 'L3_ffn_w2',
    'L3_ffn_b2',
]
_OUTS = [((NODES, D), 'float32')]


def kernel(**inputs):
    import numpy as _np
    import concourse.bacc as _bacc
    from concourse import mybir as _mybir
    from concourse.bass_utils import run_bass_kernel_spmd as _run

    nc = _bacc.Bacc("TRN2", target_bir_lowering=False, num_devices=1)
    arrays, T = {}, {}
    for name in _INS:
        a = _np.ascontiguousarray(inputs[name])
        arrays[f"in_{name}_dram"] = a
        T[name] = nc.dram_tensor(f"in_{name}_dram", a.shape, _mybir.dt.from_np(a.dtype), kind="ExternalInput").ap()
    outs = [nc.dram_tensor(f"out_{i}_dram", shape, _mybir.dt.from_np(_np.dtype(dtype)), kind="ExternalOutput").ap()
            for i, (shape, dtype) in enumerate(_OUTS)]
    gnn_ffn_layers(nc, T, outs[0], network)
    r = _run(nc, [arrays], core_ids=[0])
    return r.results[0]["out_0_dram"]
```

```python
from contextlib import ExitStack, contextmanager

import concourse.bass as bass
from concourse import mybir

F32 = mybir.dt.float32
I32 = mybir.dt.int32
F32R = mybir.dt.float32r
ALU = mybir.AluOpType
ACT = mybir.ActivationFunctionType
AX_X = mybir.AxisListType.X

P = 128
NODES = 3125
EDGES = 50000
D = 256
TILES = -(-NODES // P)
LAST = NODES - (TILES - 1) * P
BATCH = 5
BATCHES = TILES // BATCH
EPS = 1e-5
EXPERTS = 8
UNIT = 256
LOW_BITS = 12
LEAD = 64

PER_ROW = -(-EDGES // P)
FULL_ROWS = EDGES // PER_ROW
REST = EDGES - FULL_ROWS * PER_ROW
PAIR = 2
CHUNKS_NEEDED = PAIR * ((EDGES + TILES * (PAIR * P - 1)) // (PAIR * P))
STEP_PAIRS = 10
SHORT = 5
AHEAD = 3
RING = PAIR * STEP_PAIRS
HALF = RING // 2
GROUPS = (3, 2, 3, 2)
TURN_AFTER = (0, 3, 5, 7)
TAKE_AFTER = (2, 4, 7, 9)
CHUNKS = -(-CHUNKS_NEEDED // RING) * RING
SORT_ROOM = 10000
RING_AT = 7050
SPILL = CHUNKS + 1
SCATTER_STEP = 23
SCATTER_PARTS = (12, 11)
assert 2 * sum(GROUPS) == RING and PER_ROW % SCATTER_STEP == 0 and TILES % BATCH == 0


class Counter:

    def __init__(self, sem, lead=LEAD):
        self.sem, self.lead = sem, lead
        self.next = lead

    def reserve(self, n):
        base = self.next
        self.next += n
        return base


class Chain:

    def __init__(self, sem):
        self.sem, self.base, self.n = sem, 0, 0

    def mark(self, ins):
        ins.then_inc(self.sem, 1)
        self.n += 1

    def wait(self, eng):
        eng.wait_ge(self.sem, self.base + self.n)

    @contextmanager
    def loop(self, eng, trips, per_trip):
        start = self.base + self.n
        with eng.Fori(0, trips) as i:
            self.base, self.n = start + per_trip * i, 0
            yield i
            assert self.n == per_trip, (self.n, per_trip)
        self.base, self.n = start + per_trip * trips, 0


def tiles5(i, u):
    return bass.ds(i * BATCH + u, 1)


def before(i, u):
    return BATCH * i + (u - 1 if u >= 2 else (-1 if u == 1 else 0))


def high_bits(dve, out, values):
    return dve.tensor_scalar(out.bitcast(I32), values.bitcast(I32), -(1 << LOW_BITS), None, ALU.bitwise_and)


class Core:

    def __init__(self, nc, ctx, T, out):
        self.nc, self.T, self.out = nc, T, out
        self.ctx = ctx
        f = self.sbuf
        self.x = f("x_nodes", [P, TILES, D])
        self.big_a, self.big_a_r = self.sbuf_twice("big_a", TILES * 2 * D)
        self.big_b, self.big_b_r = self.sbuf_twice("big_b", TILES * 2 * D)
        self.w_area, self.w_area_r = self.sbuf_twice("w_area", 7168)
        self.arena, self.arena_r = self.sbuf_twice("arena", 7168)
        self.vec = f("vectors", [P, 2304])
        self.iota = f("iota_row", [P, CHUNKS])
        self.ident = f("ident", [P, P])
        self.ones = f("ones", [P, P])
        self.earlier = self.vec[:, 0:P]
        self.mean = f("mean", [P, TILES])
        self.rstd = f("rstd", [P, TILES])
        self.logits = f("logits", [P, TILES, EXPERTS])[:, :, :]
        self.stat_tmp = f("stat_tmp", [P, 4, 64])
        self.gates = f("gates", [P, TILES, EXPERTS])
        self.cols = f("columns", [P, 64])
        self.dinv = f("dinv", [P, TILES])
        self.quarter = self.cols[:, 56:60]
        self.chosen = self.cols[:, 48:50].bitcast(I32)
        self.chosen_weight = self.cols[:, 50:52]
        self.edge_row = f("edge_row", [P, CHUNKS], I32)
        self.edge_node = f("edge_node", [P, CHUNKS])
        self.edge_value = f("edge_weight_sorted", [P, CHUNKS])
        self.pair_tiles = f("pair_tiles", [33, CHUNKS // PAIR], I32)
        self.last_edge = f("last_edge", [P, TILES])
        self.last_in_chunk = f("last_in_chunk", [P, CHUNKS])
        self.last_number = f("last_number", [P, TILES], I32)
        self.last_row = f("last_row", [P, TILES], I32)
        self.bank = [ctx.enter_context(nc.psum_tensor(f"bank{b}", [P, 512], F32)) for b in range(8)]
        self.table = nc.dram_tensor("table", [TILES * P, D], F32, kind="Internal").ap()
        self.wide_table = nc.dram_tensor("wide_table", [TILES * P, 2 * D], F32, kind="Internal").ap()
        self.stat_in = f("stat_in", [P, BATCH * 12])
        self.batch_mean = f("batch_mean", [P, 2 * BATCH])
        self.engines = ("tensor", "vector", "scalar", "gpsimd", "sync")
        self.done = {e: ctx.enter_context(nc.semaphore(f"{e}_stages_done")) for e in self.engines}
        self.gate = {e: ctx.enter_context(nc.semaphore(f"{e}_gate")) for e in self.engines}
        self.v = Chain(ctx.enter_context(nc.semaphore("vector_steps")))
        self.a = Chain(ctx.enter_context(nc.semaphore("scalar_steps")))
        self.counters = {}
        self.loads = self.counter("loads_landed")
        self.store = self.counter("stores_landed")

    def sbuf(self, name, shape, dt=F32):
        return self.ctx.enter_context(self.nc.sbuf_tensor(name, shape, dt))

    def sbuf_twice(self, name, size):
        with self.nc.sbuf_tensor(name, [P, size], F32) as plain:
            pass
        return plain, self.sbuf(f"{name}_rounded", [P, size], F32R)

    def counter(self, name, lead=LEAD):
        if name not in self.counters:
            self.counters[name] = Counter(self.ctx.enter_context(self.nc.semaphore(name)), lead)
        return self.counters[name]

    def hold(self, eng, name, sem, value):
        eng.wait_ge(sem, value)
        eng.sem_inc(self.gate[name], 1)

    def run(self, name, eng, stages):
        left = {e: 0 for e in self.engines}
        seen = {e: 0 for e in self.engines}
        through = {}
        for stage in stages:
            for other in stage.join:
                for e, n in through[other].items():
                    left[e] = max(left[e], n)
            if stage.takes_part(name):
                for other in self.engines:
                    if other != name and left[other] > seen[other]:
                        eng.wait_ge(self.done[other], left[other])
                        seen[other] = left[other]
                stage.part(name)(eng)
                if name == "sync":
                    eng.sem_inc(self.done[name], 1)
                else:
                    eng.drain().then_inc(self.done[name], 1)
            through[stage] = {}
            for e in self.engines:
                if stage.takes_part(e):
                    through[stage][e] = stage.number[e]
                    if not stage.background:
                        left[e] = max(left[e], stage.number[e])


class Stage:

    background = False
    join = ()
    tensor = vector = scalar = gpsimd = sync = None

    def part(self, name):
        return {"tensor": self.tensor, "vector": self.vector, "scalar": self.scalar,
                "gpsimd": self.gpsimd, "sync": self.sync}[name]

    def takes_part(self, name):
        return self.part(name) is not None


def number(stages, engines):
    count = {e: 0 for e in engines}
    for stage in stages:
        stage.number = {}
        for e in engines:
            if stage.takes_part(e):
                count[e] += 1
                stage.number[e] = count[e]


class Setup(Stage):

    def __init__(self, c):
        self.c = c
        self.int_row = c.big_b[:, 0:CHUNKS].bitcast(I32)
        self.own_row = c.big_b[:, CHUNKS:CHUNKS + 1].bitcast(I32)
        self.own_quarter = c.big_b[:, CHUNKS + 1:CHUNKS + 2]
        self.made = c.counter("constants_made")
        self.m = self.made.reserve(7)

    def gpsimd(self, pool):
        c = self.c
        pool.iota(self.int_row, [[1, CHUNKS]], base=0, channel_multiplier=0).then_inc(self.made.sem, 1)
        pool.iota(self.own_row, [[1, 1]], base=0, channel_multiplier=1).then_inc(self.made.sem, 1)
        pool.memset(c.ident[:, :], 0.0).then_inc(self.made.sem, 1)
        pool.memset(c.ones[:, :], 1.0).then_inc(self.made.sem, 1)
        pool.memset(c.earlier[:, :], 1.0).then_inc(self.made.sem, 1)
        pool.wait_ge(self.made.sem, self.m + 5)
        pool.affine_select(out=c.ident[:, :], in_=c.ident[:, :], compare_op=ALU.not_equal, fill=1.0,
                           base=0, pattern=[[-1, P]], channel_multiplier=1).then_inc(self.made.sem, 1)
        pool.affine_select(out=c.earlier[:, :], in_=c.earlier[:, :], compare_op=ALU.is_gt, fill=0.0,
                           base=0, pattern=[[1, P]], channel_multiplier=-1).then_inc(self.made.sem, 1)

    def vector(self, dve):
        c = self.c
        c.v.mark(dve.memset(c.x[:, TILES - 1, :], 0.0))
        dve.wait_ge(self.made.sem, self.m + 5)
        c.v.mark(dve.tensor_copy(c.iota[:, :], self.int_row))
        c.v.mark(dve.tensor_scalar(self.own_row, self.own_row, 3, None, ALU.arith_shift_right))
        c.v.wait(dve)
        c.v.mark(dve.tensor_scalar(self.own_row, self.own_row, 3, None, ALU.bitwise_and))
        c.v.wait(dve)
        c.v.mark(dve.tensor_copy(self.own_quarter, self.own_row))
        c.v.wait(dve)
        c.v.mark(dve.tensor_scalar(c.quarter, c.iota[:, 0:4], self.own_quarter, None, ALU.is_equal))


class SortPlan(Stage):

    def __init__(self, c, name, key, other, weight, keep, tile_row, made=None):
        self.c, self.name = c, name
        if made is not None:
            self.gpsimd = None
        self.key, self.other, self.weight = c.T[key], c.T[other], weight and c.T[weight]
        self.slots = c.nc.dram_tensor(f"{name}_slots", [P, SPILL * 4], F32, kind="Internal").ap()
        self.rec, self.slot_i = keep[:, 0:PER_ROW * 4], keep[:, PER_ROW * 4:PER_ROW * 5].bitcast(I32)
        self.tile_all = keep[:, PER_ROW * 5:PER_ROW * 5 + CHUNKS]
        self.tile_row = tile_row
        self.row, self.node = c.edge_row[:, :], c.edge_node[:, :]
        self.value = weight and c.edge_value[:, :]
        n = [0]

        def part(size):
            n[0] += size
            return c.big_b[:, n[0] - size:n[0]]

        self.key_i, self.other_i, self.low_i, self.high_i, self.id_i = (
            part(PER_ROW).bitcast(I32) for _ in range(5))
        self.wt, self.high, self.position, self.ids, self.one = (part(PER_ROW) for _ in range(5))
        self.mask, self.term = part(BATCH * PER_ROW), part(BATCH * PER_ROW)
        self.total, self.chunks, self.ends, self.start = (part(TILES) for _ in range(4))
        self.chunks_i = part(TILES).bitcast(I32)
        assert n[0] <= SORT_ROOM
        self.fill = c.arena[:, 0:SPILL * 4]
        self.scan = c.big_a[:, 0:TILES * PER_ROW]
        self.cleared = c.counter("cleared")
        self.z = self.cleared.reserve(1)
        self.made = c.counter("edge_ids_made")
        self.i0 = self.made.reserve(1) if made is None else made.i0
        self.filled = c.counter("filling_ready")
        self.f0 = self.filled.reserve(1)
        self.l = c.loads.reserve(16 * (6 if weight else 4))
        self.counted = c.counter("bucket_counts_ready")
        self.k0 = self.counted.reserve(1)
        self.summed = c.counter("bucket_sums_ready")
        self.s0 = self.summed.reserve(1)
        self.slot_filled = c.counter("slots_filled")
        self.g0 = self.slot_filled.reserve(16)

    def sync(self, sp):
        c = self.c
        sp.wait_ge(self.cleared.sem, self.z + 1)
        pairs = [(self.key_i, self.key), (self.other_i, self.other)]
        if self.weight is not None:
            pairs.append((self.wt, self.weight))
        for to, src in pairs:
            sp.dma_start(to[0:FULL_ROWS, :], src[0:FULL_ROWS * PER_ROW].rearrange("(p j) -> p j", j=PER_ROW)
                         ).then_inc(c.loads.sem, 16)
            sp.dma_start(to[FULL_ROWS:FULL_ROWS + 1, 0:REST],
                         src[FULL_ROWS * PER_ROW:EDGES].rearrange("(p j) -> p j", p=1)).then_inc(c.loads.sem, 16)
        sp.wait_ge(self.filled.sem, self.f0 + 1)
        sp.dma_start(self.slots, self.fill).then_inc(self.slot_filled.sem, 16)
        sp.wait_ge(c.loads.sem, self.l + 16 * 2 * len(pairs))
        sp.wait_ge(self.slot_filled.sem, self.g0 + 16)

    def gpsimd(self, pool):
        pool.iota(self.id_i, [[1, PER_ROW]], base=0, channel_multiplier=PER_ROW).then_inc(self.made.sem, 1)

    def tensor(self, pe):
        c = self.c
        pe.wait_ge(self.counted.sem, self.k0 + 1)
        pe.matmul(c.bank[0][:, 0:TILES], c.earlier[:, :], self.total, start=True, stop=True)
        pe.matmul(c.bank[1][:, 0:TILES], c.ones[:, :], self.total, start=True, stop=True
                  ).then_inc(self.summed.sem, 1)

    def vector(self, dve):
        c, v = self.c, self.c.v
        rec = self.rec.rearrange("p (j r) -> p j r", r=4)
        rec_i = rec.bitcast(I32)
        dve.memset(self.other_i, 0)
        dve.memset(self.wt, 0.0)
        dve.memset(self.key_i, -1).then_inc(self.cleared.sem, 1)
        fill = self.fill.rearrange("p (c r) -> p c r", r=4)
        v.mark(dve.memset(self.one, 1.0))
        v.mark(dve.memset(self.fill, 0.0))
        v.wait(dve)
        dve.memset(fill[:, :, 1:2], -1.0).then_inc(self.filled.sem, 1)
        dve.wait_ge(self.made.sem, self.i0 + 1)
        v.mark(dve.tensor_copy(self.ids, self.id_i))
        v.wait(dve)
        v.mark(dve.tensor_scalar(self.position, self.ids, float(EDGES), None, ALU.is_ge))
        v.mark(dve.tensor_scalar(rec[:, :, 3], self.ids, 1.0, None, ALU.add))
        v.wait(dve)
        v.mark(dve.scalar_tensor_tensor(out=self.position, in0=self.ids, scalar=float(P * CHUNKS - EDGES),
                                        in1=self.position, op0=ALU.add, op1=ALU.mult))
        dve.wait_ge(c.loads.sem, self.l + 16 * (6 if self.weight is not None else 4))
        v.mark(dve.tensor_scalar(self.high_i, self.key_i, 7, None, ALU.arith_shift_right))
        v.mark(dve.tensor_scalar(self.low_i, self.key_i, P - 1, None, ALU.bitwise_and))
        v.mark(dve.tensor_copy(rec_i[:, :, 0], self.other_i))
        v.mark(dve.tensor_copy(rec[:, :, 2], self.wt))
        v.wait(dve)
        v.mark(dve.tensor_copy(self.high, self.high_i))
        v.mark(dve.tensor_copy(rec[:, :, 1], self.low_i))
        v.wait(dve)

        def buffer(area, u):
            return area[:, u * PER_ROW:(u + 1) * PER_ROW]

        def scans(i, u):
            return self.scan[:, bass.ds((i * BATCH + u) * PER_ROW, PER_ROW)]

        def masks(i):
            for u in range(BATCH):
                v.mark(dve.tensor_scalar(buffer(self.mask, u), self.high, c.iota[:, tiles5(i, u)], None,
                                         ALU.is_equal))
            v.wait(dve)

        with v.loop(dve, BATCHES, 2 * BATCH) as i:
            masks(i)
            for u in range(BATCH):
                v.mark(dve.tensor_tensor_scan(scans(i, u), self.one, buffer(self.mask, u), 0.0,
                                              ALU.mult, ALU.add))
            v.wait(dve)
        scan = self.scan.rearrange("p (b j) -> p b j", j=PER_ROW)
        dve.tensor_copy(self.total, scan[:, :, PER_ROW - 1]).then_inc(self.counted.sem, 1)
        dve.wait_ge(self.summed.sem, self.s0 + 1)
        v.mark(dve.tensor_scalar(self.chunks_i, c.bank[1][:, 0:TILES], float(PAIR * P - 1), None, ALU.add))
        v.wait(dve)
        v.mark(dve.tensor_scalar(self.chunks_i, self.chunks_i, 8, None, ALU.arith_shift_right))
        v.wait(dve)
        v.mark(dve.tensor_copy(self.chunks, self.chunks_i))
        v.wait(dve)
        v.mark(dve.tensor_tensor_scan(self.ends, self.one[:, 0:TILES], self.chunks, 0.0, ALU.mult, ALU.add))
        v.wait(dve)
        v.mark(dve.tensor_tensor(self.ends, self.ends, self.chunks, ALU.subtract))
        v.wait(dve)
        v.mark(dve.tensor_scalar(self.start, self.ends, float(PAIR * P), -1.0, ALU.mult, ALU.add))
        v.mark(dve.tensor_scalar(self.ends, self.ends, float(PAIR), None, ALU.mult))
        v.wait(dve)
        v.mark(dve.tensor_tensor(self.start, self.start, c.bank[0][:, 0:TILES], ALU.add))
        v.wait(dve)
        with v.loop(dve, BATCHES, 3 * BATCH) as i:
            masks(i)
            for u in range(BATCH):
                v.mark(dve.scalar_tensor_tensor(out=buffer(self.term, u), in0=scans(i, u),
                                                scalar=self.start[:, tiles5(i, u)], in1=buffer(self.mask, u),
                                                op0=ALU.add, op1=ALU.mult))
            v.wait(dve)
            for u in range(BATCH):
                v.mark(dve.tensor_tensor(self.position, self.position, buffer(self.term, u), ALU.add))
                v.wait(dve)
        v.mark(dve.tensor_copy(self.slot_i, self.position))
        v.wait(dve)
        v.mark(dve.tensor_scalar(self.high_i, self.slot_i, 7, None, ALU.arith_shift_right))
        v.mark(dve.tensor_scalar(self.low_i, self.slot_i, P - 1, None, ALU.bitwise_and))
        v.wait(dve)
        v.mark(dve.tensor_copy(self.high, self.high_i))
        v.mark(dve.tensor_copy(self.position, self.low_i))
        v.wait(dve)
        v.mark(dve.scalar_tensor_tensor(out=self.slot_i, in0=self.position, scalar=float(SPILL), in1=self.high,
                                        op0=ALU.mult, op1=ALU.add))


class ChunkTiles(Stage):

    def __init__(self, c, plan):
        self.c, self.plan = c, plan

    def vector(self, dve):
        c, v, plan = self.c, self.c.v, self.plan
        v.mark(dve.memset(plan.tile_all, 0.0))
        v.wait(dve)
        with v.loop(dve, TILES - 1, 1) as b:
            v.mark(dve.scalar_tensor_tensor(out=plan.tile_all, in0=c.iota[:, 0:CHUNKS],
                                            scalar=plan.ends[:, bass.ds(b + 1, 1)], in1=plan.tile_all,
                                            op0=ALU.is_ge, op1=ALU.add))
            v.wait(dve)
        r = plan.tile_row
        of_pairs = plan.tile_all.rearrange("p (n a) -> p n a", a=PAIR)[:, :, 0]
        v.mark(dve.tensor_copy(c.pair_tiles[r:r + 1, :], of_pairs[r:r + 1, :]))


class Scatter(Stage):

    background = True

    def __init__(self, c, plan):
        self.c, self.plan = c, plan
        a, b = SCATTER_PARTS
        at = RING_AT
        self.ring = [c.arena[:, at:at + 4 * a], c.arena[:, at + 4 * a:at + 4 * (a + b)]]
        at += 4 * (a + b)
        self.ring_to = [c.arena[:, at:at + a].bitcast(I32), c.arena[:, at + a:at + a + b].bitcast(I32)]
        self.steps = PER_ROW // SCATTER_STEP
        self.ring_ready = c.counter("scatter_ring_ready")
        self.r0 = self.ring_ready.reserve(4 * self.steps)
        self.scattered = [c.counter(f"edges_scattered{h}", 0) for h in range(2)]
        self.e0 = [s.reserve(16 * self.steps * n) for s, n in zip(self.scattered, SCATTER_PARTS)]

    def gpsimd(self, pool):
        c, plan = self.c, self.plan
        rec_i = plan.rec.rearrange("p (j r) -> p j r", r=4).bitcast(I32)
        target = plan.slots.rearrange("p (c r) -> (p c) r", r=4)

        def step(i, h, later):
            n, j = SCATTER_PARTS[h], i * SCATTER_STEP + h * SCATTER_PARTS[0]
            if later:
                c.hold(pool, "gpsimd", self.scattered[h].sem, self.e0[h] + 16 * n * i)
            pool.tensor_copy(self.ring[h].rearrange("p (j r) -> p j r", r=4).bitcast(I32),
                             rec_i[:, bass.ds(j, n), :]).then_inc(self.ring_ready.sem, 1)
            pool.tensor_copy(self.ring_to[h], plan.slot_i[:, bass.ds(j, n)]).then_inc(self.ring_ready.sem, 1)
            c.hold(pool, "gpsimd", self.ring_ready.sem, self.r0 + 4 * i + 2 * h + 2)
            for k in range(n):
                pool.indirect_dma_start(
                    target, bass.IndirectOffsetOnAxis(ap=self.ring_to[h][:, k:k + 1], axis=0),
                    self.ring[h][:, 4 * k:4 * k + 4], None).then_inc(self.scattered[h].sem, 16)

        step(0, 0, False)
        step(0, 1, False)
        with pool.Fori(1, self.steps) as i:
            step(i, 0, True)
            step(i, 1, True)
        for h, n in enumerate(SCATTER_PARTS):
            pool.wait_ge(self.scattered[h].sem, self.e0[h] + 16 * self.steps * n)


class ReadSlots(Stage):

    def __init__(self, c, plan, scatter, back):
        self.c, self.plan = c, plan
        self.join = (scatter,)
        self.back = back[:, 0:CHUNKS * 4]
        self.landed = c.counter("slots_read_back")
        self.b0 = self.landed.reserve(16)

    def sync(self, sp):
        sp.dma_start(self.back, self.plan.slots[:, 0:CHUNKS * 4]).then_inc(self.landed.sem, 16)
        sp.wait_ge(self.landed.sem, self.b0 + 16)

    def vector(self, dve):
        back, plan = self.back.rearrange("p (c r) -> p c r", r=4), self.plan
        dve.wait_ge(self.landed.sem, self.b0 + 16)
        dve.tensor_copy(plan.row, back[:, :, 0].bitcast(I32))
        dve.tensor_copy(plan.node, back[:, :, 1])
        if plan.value is not None:
            dve.tensor_copy(plan.value, back[:, :, 2])


class GatherAdd(Stage):

    def __init__(self, c, edges, width, degree=False, beside=None, of_tiles=None, onto=None):
        self.c, self.edges, self.width, self.degree, self.onto = c, edges, width, degree, onto
        self.beside, self.of_tiles = beside, of_tiles
        self.total = width + degree
        self.trips = CHUNKS // RING
        self.sums = tiles_of(c.big_a, self.total) if onto is None else onto
        stride = width + 2
        self.slots = STEP_PAIRS if width == D else STEP_PAIRS // 2
        at = self.slots * PAIR * stride
        self.rows = c.arena[:, 0:at].rearrange("p (k d) -> p k d", d=stride)
        self.onehot = c.arena[:, at:at + SHORT * PAIR * P].rearrange("p (k d) -> p k d", d=P)
        at += SHORT * PAIR * P
        self.ring = c.arena[:, at:at + RING].bitcast(I32)
        assert at + RING <= 7168 and STEP_PAIRS % SHORT == 0 and STEP_PAIRS % self.slots == 0
        self.uses = STEP_PAIRS // self.slots
        n = self.trips * STEP_PAIRS
        self.index_ready = c.counter("gather_index_ready")
        self.i0 = self.index_ready.reserve(2 * self.trips)
        self.landed = [c.counter(f"pair_landed{k}", 0) for k in range(self.slots)]
        self.l0 = [s.reserve(16 * PAIR * self.uses * self.trips) for s in self.landed]
        self.onehot_ready = c.counter("onehot_ready")
        self.o0 = self.onehot_ready.reserve(n)
        self.summed = c.counter("pair_summed")
        self.s0 = self.summed.reserve(n)
        self.added = c.counter("pair_added")
        self.a0 = self.added.reserve(n)
        self.cleared = c.counter("sums_cleared")
        self.clears = 2 if onto is None else 1
        self.z0 = self.cleared.reserve(self.clears)

    def landed_with(self, eng, i, q):
        slot = q % self.slots
        eng.wait_ge(self.landed[slot].sem, self.l0[slot] + 16 * PAIR * (self.uses * i + q // self.slots + 1))

    def scalar(self, act):
        def fill(i, h):
            act.copy(self.ring[:, h * HALF:(h + 1) * HALF],
                     self.edges.row[:, bass.ds(i * RING + h * HALF, HALF)]).then_inc(self.index_ready.sem, 1)

        fill(0, 0)
        fill(0, 1)
        if self.beside is not None:
            for j in range(len(GROUPS)):
                self.beside.scalar_group(act, 0, j)
        with act.Fori(1, self.trips) as i:
            for h in range(2):
                for q in range(h * HALF // PAIR, (h + 1) * HALF // PAIR):
                    self.landed_with(act, i - 1, q)
                fill(i, h)
                if self.beside is not None:
                    for j in range(h * len(GROUPS) // 2, (h + 1) * len(GROUPS) // 2):
                        self.beside.scalar_group(act, i, j)

    def gpsimd(self, pool):
        c = self.c
        with pool.Fori(0, self.trips) as i:
            for q in range(STEP_PAIRS):
                if q % (HALF // PAIR) == 0:
                    c.hold(pool, "gpsimd", self.index_ready.sem, self.i0 + 2 * i + q // (HALF // PAIR) + 1)
                c.hold(pool, "gpsimd", self.summed.sem, self.s0 + STEP_PAIRS * i + q - self.slots + 1)
                for k in range(PAIR * q, PAIR * (q + 1)):
                    pool.indirect_dma_start(self.rows[:, k % (self.slots * PAIR), 0:self.width], None,
                                            c.table if self.width == D else c.wide_table,
                                            bass.IndirectOffsetOnAxis(ap=self.ring[:, k:k + 1], axis=0)
                                            ).then_inc(self.landed[q % self.slots].sem, 16)

    def tensor(self, pe):
        c = self.c
        pe.wait_ge(self.cleared.sem, self.z0 + self.clears)
        with pe.Fori(0, self.trips) as i:
            for q in range(STEP_PAIRS):
                pe.wait_ge(self.onehot_ready.sem, self.o0 + STEP_PAIRS * i + q + 1)
                pe.wait_ge(self.added.sem, self.a0 + STEP_PAIRS * i + q - SHORT + 1)
                self.landed_with(pe, i, q)
                for a in range(PAIR):
                    ins = pe.matmul(c.bank[q % SHORT][:, 0:self.total], self.onehot[:, q % SHORT * PAIR + a, :],
                                    self.rows[:, (q % self.slots) * PAIR + a, 0:self.total],
                                    start=a == 0, stop=a == PAIR - 1)
                ins.then_inc(self.summed.sem, 1)
                if self.beside is not None and q in TURN_AFTER:
                    self.beside.tensor_group(pe, i, TURN_AFTER.index(q))

    def vector(self, dve):
        c, e = self.c, self.edges
        if self.onto is None:
            dve.memset(self.sums, 0.0).then_inc(self.cleared.sem, 1)
        dve.memset(self.rows[:, :, self.width:self.width + 1], 1.0).then_inc(self.cleared.sem, 1)
        dve.wait_ge(self.cleared.sem, self.z0 + self.clears)

        def select(i, q):
            dve.wait_ge(self.summed.sem, self.s0 + STEP_PAIRS * i + q - SHORT + 1)
            for a in range(PAIR):
                at = bass.ds(RING * i + PAIR * q + a, 1)
                to = self.onehot[:, q % SHORT * PAIR + a, :]
                if e.value is None:
                    ins = dve.tensor_scalar(to, c.iota[:, 0:P], e.node[:, at], None, ALU.is_equal)
                else:
                    ins = dve.tensor_scalar(to, c.iota[:, 0:P], e.node[:, at], e.value[:, at],
                                            ALU.is_equal, ALU.mult)
            ins.then_inc(self.onehot_ready.sem, 1)

        def step(i, last):
            r = e.tile_row
            for q in range(STEP_PAIRS):
                tile = dve.value_load(c.pair_tiles[r:r + 1, bass.ds(STEP_PAIRS * i + q, 1)],
                                      min_val=0, max_val=TILES - 1)
                dve.wait_ge(self.summed.sem, self.s0 + STEP_PAIRS * i + q + 1)
                dve.wait_ge(self.added.sem, self.a0 + STEP_PAIRS * i + q)
                into = self.sums[:, bass.ds(tile, 1), :]
                part = c.bank[q % SHORT][:, 0:self.total].rearrange("p (a d) -> p a d", a=1)
                dve.tensor_tensor(into, into, part, ALU.add).then_inc(self.added.sem, 1)
                if q + AHEAD < STEP_PAIRS:
                    select(i, q + AHEAD)
                elif not last:
                    select(i + 1, q + AHEAD - STEP_PAIRS)
                if self.beside is not None and q in TAKE_AFTER:
                    self.beside.vector_group(dve, i, TAKE_AFTER.index(q))
                if self.of_tiles is not None and q == STEP_PAIRS // 2:
                    self.of_tiles.vector_tile(dve, i)

        for q in range(AHEAD):
            select(0, q)
        with dve.Fori(0, self.trips - 1) as i:
            step(i, False)
        step(self.trips - 1, True)
        if self.of_tiles is not None:
            for t in range(self.trips, TILES):
                self.of_tiles.vector_tile(dve, t)


class LastEdge:

    def __init__(self, c, edges, back, room, best, first, trips):
        self.c, self.edges, self.best = c, edges, best
        self.first, self.trips = first, trips
        self.back = back[:, 0:CHUNKS * 4].rearrange("p (c r) -> p c r", r=4)
        self.nodes, self.ids, self.minus = (room[:, k * CHUNKS:(k + 1) * CHUNKS] for k in range(3))
        at = 3 * CHUNKS
        self.apart = room[:, at:at + 4 * P].rearrange("p (k d) -> p k d", d=P)
        self.tagged = room[:, at + 4 * P:at + 12 * P].rearrange("p (s k d) -> p s k d", s=2, d=P)
        n = self.trips * len(GROUPS)
        self.apart_ready = c.counter("distances_ready")
        self.d0 = self.apart_ready.reserve(n)
        self.tagged_ready = c.counter("tagged_ready")
        self.t0 = self.tagged_ready.reserve(n)
        self.turned = c.counter("tagged_turned")
        self.u0 = self.turned.reserve(n)
        self.taken = c.counter("tagged_taken")
        self.k0 = self.taken.reserve(n)

    def prepare(self, dve):
        yield dve.tensor_copy(self.nodes, self.back[:, :, 1])
        yield dve.tensor_copy(self.ids, self.back[:, :, 3])
        yield dve.tensor_scalar(self.minus, self.ids, -1.0, None, ALU.mult)

    def chunks(self, i, j):
        return [self.first + sum(GROUPS) * i + sum(GROUPS[:j]) + k for k in range(GROUPS[j])]

    def scalar_group(self, act, i, j):
        c, n = self.c, len(GROUPS) * i + j
        act.wait_ge(self.tagged_ready.sem, self.t0 + n)
        for k, chunk in enumerate(self.chunks(i, j)):
            ins = act.activation(self.apart[:, k, :], c.iota[:, 0:P], ACT.Abs,
                                 bias=self.nodes[:, bass.ds(chunk, 1)], scale=-1.0)
        ins.then_inc(self.apart_ready.sem, 1)
        act.wait_ge(self.apart_ready.sem, self.d0 + n + 1)
        act.wait_ge(self.turned.sem, self.u0 + n - 1)
        for k, chunk in enumerate(self.chunks(i, j)):
            at = bass.ds(chunk, 1)
            ins = act.activation(self.tagged[:, j % 2, k, :], self.apart[:, k, :], ACT.Relu,
                                 bias=self.ids[:, at], scale=self.minus[:, at])
        ins.then_inc(self.tagged_ready.sem, 1)

    def bank(self, j):
        return self.c.bank[SHORT + j % 2][:, 0:GROUPS[j] * P]

    def tensor_group(self, pe, i, j):
        n = len(GROUPS) * i + j
        pe.wait_ge(self.tagged_ready.sem, self.t0 + n + 1)
        pe.wait_ge(self.taken.sem, self.k0 + n - 1)
        for k in range(GROUPS[j]):
            ins = pe.transpose(self.bank(j)[:, k * P:(k + 1) * P], self.tagged[:, j % 2, k, :],
                               self.c.ident[:, :])
        ins.then_inc(self.turned.sem, 1)

    def vector_group(self, dve, i, j):
        dve.wait_ge(self.turned.sem, self.u0 + len(GROUPS) * i + j + 1)
        dve.tensor_reduce(self.best[:, bass.ds(self.chunks(i, j)[0], GROUPS[j])],
                          self.bank(j).rearrange("p (k d) -> p k d", d=P), AX_X, ALU.max
                          ).then_inc(self.taken.sem, 1)


class LastOfTiles:

    def __init__(self, c, tile_of_chunk, masked):
        self.c, self.tile_of_chunk, self.masked = c, tile_of_chunk, masked
        self.masked_ready = c.counter("chunks_masked")
        self.m0 = self.masked_ready.reserve(TILES)
        self.found = c.counter("last_edges_found")
        self.f0 = self.found.reserve(TILES)

    def vector_tile(self, dve, t):
        c = self.c
        dve.wait_ge(self.found.sem, self.f0 + t)
        dve.scalar_tensor_tensor(out=self.masked, in0=self.tile_of_chunk, scalar=c.iota[:, bass.ds(t, 1)],
                                 in1=c.last_in_chunk[:, :], op0=ALU.is_equal, op1=ALU.mult
                                 ).then_inc(self.masked_ready.sem, 1)
        dve.wait_ge(self.masked_ready.sem, self.m0 + t + 1)
        dve.tensor_reduce(c.last_edge[:, bass.ds(t, 1)], self.masked, AX_X, ALU.max).then_inc(self.found.sem, 1)


class RowStats(Stage):

    def __init__(self, c, src):
        self.c, self.src = c, src
        self.stats = c.arena[:, 0:TILES * 6]
        self.s = Statistics(c, TILES, 2, D)

    def vector(self, dve):
        c, v = self.c, self.c.v
        with v.loop(dve, BATCHES, BATCH) as i:
            for u in range(BATCH):
                v.mark(dve.bn_stats(self.stats.rearrange("p (t s) -> p t s", s=6)[:, tiles5(i, u), :],
                                    self.src[:, tiles5(i, u), :]))
        v.wait(dve)
        self.s.vector(dve, self.stats.rearrange("p (t g s) -> p t g s", g=2, s=3), c.mean[:, :], c.rstd[:, :])

    def scalar(self, act):
        self.s.scalar(act)


class Statistics:

    def __init__(self, c, rows, groups, width, uses=1, tag=""):
        self.c, self.rows, self.groups, self.width = c, rows, groups, width
        n = rows * groups
        self.dev = c.stat_tmp[:, 0, 0:n].rearrange("p (t g) -> p t g", g=groups)
        self.sq = c.stat_tmp[:, 1, 0:n].rearrange("p (t g) -> p t g", g=groups)
        self.var, self.std = c.stat_tmp[:, 2, 0:rows], c.stat_tmp[:, 3, 0:rows]
        self.var_ready = c.counter(tag + "variance_ready")
        self.v0 = self.var_ready.reserve(uses)
        self.std_ready = c.counter(tag + "deviation_ready")
        self.d0 = self.std_ready.reserve(uses)
        self.STEPS = 7

    def vector(self, dve, stats, mean, rstd, use=0):
        v = self.c.v
        shape = [P, self.rows, self.groups]
        per_group = float(self.width // self.groups)
        v.mark(dve.tensor_reduce(mean, stats[:, :, :, 1], AX_X, ALU.add))
        v.wait(dve)
        v.mark(dve.tensor_scalar(mean, mean, 1.0 / self.groups, None, ALU.mult))
        v.wait(dve)
        v.mark(dve.tensor_tensor(self.dev, stats[:, :, :, 1], mean.unsqueeze(2).broadcast_to(shape), ALU.subtract))
        v.wait(dve)
        v.mark(dve.scalar_tensor_tensor(out=self.sq, in0=self.dev, scalar=per_group, in1=self.dev,
                                        op0=ALU.mult, op1=ALU.mult))
        v.wait(dve)
        v.mark(dve.tensor_tensor(self.sq, self.sq, stats[:, :, :, 2], ALU.add))
        v.wait(dve)
        v.mark(dve.tensor_reduce(self.var, self.sq, AX_X, ALU.add))
        v.wait(dve)
        dve.tensor_scalar(self.var, self.var, 1.0 / self.width, EPS, ALU.mult, ALU.add
                          ).then_inc(self.var_ready.sem, 1)
        dve.wait_ge(self.std_ready.sem, self.d0 + use + 1)
        v.mark(dve.reciprocal(rstd, self.std))
        v.wait(dve)

    def scalar(self, act, use=0):
        act.wait_ge(self.var_ready.sem, self.v0 + use + 1)
        act.activation(self.std, self.var, ACT.Sqrt).then_inc(self.std_ready.sem, 1)


class Project(Stage):

    def __init__(self, c, K, N, weights, prepare, take, taker, affine=None, store=None, keep_columns=None,
                 tag="", steps=0, before_batch=None, rows=None, columns=None, first_bank=2):
        self.c, self.K, self.N, self.w = c, K, N, weights
        self.prepare, self.take, self.taker, self.affine, self.store = prepare, take, taker, affine, store
        self.keep, self.steps, self.before_batch, self.first_bank = keep_columns, steps, before_batch, first_bank
        self.blocks = K // P
        self.G = -(-self.blocks // 4)
        self.C = -(-N // 512)
        self.buffers = 1 if before_batch is None else 2
        rows = c.arena[:, 0:self.buffers * BATCH * K] if rows is None else rows
        columns = c.arena[:, 5120:5120 + 2 * self.blocks * P] if columns is None else columns
        self.rows = rows.rearrange("p (u d) -> p u d", d=K)
        self.columns = columns.rearrange("p (s n) -> p s n", s=2)
        self.masked = c.arena[:, 5632:5632 + 4 * P].rearrange("p (s n) -> p s n", s=2)
        self.masked_ready = c.counter(tag + "columns_masked")
        self.m0 = self.masked_ready.reserve(TILES if keep_columns is not None else 0)
        self.rounded = c.counter(tag + "columns_rounded")
        self.q0 = self.rounded.reserve(TILES if keep_columns is not None else 0)
        n = TILES
        self.row_ready = c.counter(tag + "rows_ready")
        self.r0 = self.row_ready.reserve(n)
        self.turned = c.counter(tag + "rows_turned")
        self.t0 = self.turned.reserve(n * self.G)
        self.column_ready = c.counter(tag + "columns_ready")
        self.c0 = self.column_ready.reserve(n * self.G)
        self.product = c.counter(tag + "product_ready")
        self.p0 = self.product.reserve(n)
        self.used = c.counter(tag + "product_used")
        self.u0 = self.used.reserve(n)
        self.kept = c.counter(tag + "columns_kept")
        self.k0 = self.kept.reserve(n if keep_columns is not None else 0)
        self.stored = c.store.reserve(16 * BATCHES if store is not None else 0)

    def banks(self, u):
        return [self.c.bank[self.first_bank + (u % 2) * self.C + j] for j in range(self.C)]

    def turn_bank(self, u, g):
        return self.c.bank[(u * self.G + g) % 2]

    def turn_and_multiply(self, pe):
        c = self.c

        def turn(i, u, first_row=0):
            pe.wait_ge(self.row_ready.sem, self.r0 + BATCH * i + u + 1)
            for g in range(self.G):
                copied = before(i, u) if self.G == 1 else 2 * (BATCH * i + u - 1) + g + 1
                pe.wait_ge(self.column_ready.sem, self.c0 + copied)
                for b in range(4 * g, min(4 * g + 4, self.blocks)):
                    ins = pe.transpose(self.turn_bank(u, g)[:, (b % 4) * P:(b % 4 + 1) * P],
                                       self.rows[:, first_row + u, b * P:(b + 1) * P], c.ident[:, :])
                ins.then_inc(self.turned.sem, 1)

        def multiply(i, u):
            pe.wait_ge(self.column_ready.sem, self.c0 + self.G * (BATCH * i + u + 1))
            pe.wait_ge(self.used.sem, self.u0 + before(i, u))
            for j, bank in enumerate(self.banks(u)):
                lo, hi = j * 512, min(j * 512 + 512, self.N)
                for b in range(self.blocks):
                    ins = pe.matmul(bank[:, 0:hi - lo], self.columns[:, u % 2, b * P:(b + 1) * P],
                                    self.w[:, b, lo:hi], start=b == 0, stop=b == self.blocks - 1)
            ins.then_inc(self.product.sem, 1)

        return turn, multiply

    def tensor_batch(self, pe, i, first_row=0):
        turn, multiply = self.turn_and_multiply(pe)
        turn(i, 0, first_row)
        for u in range(BATCH):
            if u + 1 < BATCH:
                turn(i, u + 1, first_row)
            multiply(i, u)

    def by_twos(self, loop, batch):
        assert BATCHES % 2
        with loop as k:
            batch(2 * k, 0)
            batch(2 * k + 1, BATCH)
        batch(BATCHES - 1, 0)

    def batches(self, eng, loop, first, second, ahead):
        def step(i, last):
            for u in range(BATCH):
                if u + ahead < BATCH:
                    first(i, u + ahead)
                elif not last:
                    first(i + 1, u + ahead - BATCH)
                second(i, u)

        for u in range(ahead):
            first(0, u)
        with loop as i:
            step(i, False)
        step(BATCHES - 1, True)

    def tensor(self, pe):
        if self.before_batch is None:
            self.batches(pe, pe.Fori(0, BATCHES - 1), *self.turn_and_multiply(pe), 1)
        else:
            self.by_twos(pe.Fori(0, BATCHES // 2), lambda i, first_row: self.tensor_batch(pe, i, first_row))

    def copy_columns(self, act, i, u):
        for g in range(self.G):
            act.wait_ge(self.turned.sem, self.t0 + self.G * (BATCH * i + u) + g + 1)
            if g == 0:
                act.wait_ge(self.product.sem, self.p0 + before(i, u))
                if self.keep is not None:
                    act.wait_ge(self.kept.sem, self.k0 + before(i, u))
            hi = min(4 * g + 4, self.blocks)
            bank = self.turn_bank(u, g)
            if self.affine is None:
                ins = act.copy(self.columns[:, u % 2, 4 * g * P:hi * P], bank[:, 0:(hi - 4 * g) * P])
            else:
                gain, shift = self.affine
                for b in range(4 * g, hi):
                    ins = act.activation(self.columns[:, u % 2, b * P:(b + 1) * P],
                                         bank[:, (b - 4 * g) * P:(b - 4 * g + 1) * P], ACT.Identity,
                                         bias=shift[:, b:b + 1], scale=gain[:, b:b + 1])
            ins.then_inc(self.column_ready.sem, 1)

    def round_columns(self, act, i, u):
        act.wait_ge(self.masked_ready.sem, self.m0 + BATCH * i + u + 1)
        at = bass.ds((i * BATCH + u) * P, P)
        for b in range(self.blocks):
            ins = act.copy(self.keep[0][b][:, at], self.masked[:, u % 2, b * P:(b + 1) * P])
        ins.then_inc(self.rounded.sem, 1)

    def take_one(self, eng, i, u):
        eng.wait_ge(self.product.sem, self.p0 + BATCH * i + u + 1)
        self.take(eng, i, u, self.banks(u)).then_inc(self.used.sem, 1)

    def scalar_batch(self, act, i, between=None):
        self.copy_columns(act, i, 0)
        if between is not None:
            between()
        for u in range(BATCH):
            if u + 1 < BATCH:
                self.copy_columns(act, i, u + 1)
            if self.taker == "scalar":
                self.take_one(act, i, u)

    def scalar_second(self, act, i, u):
        if self.keep is not None:
            self.round_columns(act, i, u)
        if self.taker == "scalar":
            self.take_one(act, i, u)

    def scalar(self, act):
        if self.before_batch is None:
            self.batches(act, act.Fori(0, BATCHES - 1), lambda i, u: self.copy_columns(act, i, u),
                         lambda i, u: self.scalar_second(act, i, u), 1)
        else:
            with act.Fori(0, BATCHES) as i:
                self.before_batch.scalar(act, i)
                self.scalar_batch(act, i)

    def prepare_one(self, dve, i, u, first_row=0):
        dve.wait_ge(self.turned.sem, self.t0 + self.G * (BATCH * (i - self.buffers) + u + 1))
        self.prepare(dve, i, u, self.rows[:, first_row + u, :]).then_inc(self.row_ready.sem, 1)

    def finish_one(self, dve, i, u):
        if self.keep is not None:
            dve.wait_ge(self.column_ready.sem, self.c0 + self.G * (BATCH * i + u + 1))
            low = self.keep[1]
            at = bass.ds((i * BATCH + u) * P, P)
            dve.wait_ge(self.kept.sem, self.k0 + before(i, u))
            dve.wait_ge(self.rounded.sem, self.q0 + before(i, u))
            masked = self.masked[:, u % 2, :]
            high_bits(dve, masked, self.columns[:, u % 2, :]).then_inc(self.masked_ready.sem, 1)
            dve.wait_ge(self.masked_ready.sem, self.m0 + BATCH * i + u + 1)
            for b in range(self.blocks):
                ins = dve.tensor_tensor(low[b][:, at], self.columns[:, u % 2, b * P:(b + 1) * P],
                                        masked[:, b * P:(b + 1) * P], ALU.subtract)
            ins.then_inc(self.kept.sem, 1)
        if self.taker == "vector":
            self.take_one(dve, i, u)

    def vector_batch(self, dve, i, first_row=0):
        if self.before_batch is not None:
            self.before_batch.vector(dve, i, first_row)
        for u in range(BATCH):
            self.prepare_one(dve, i, u, first_row)
        for u in range(BATCH):
            self.finish_one(dve, i, u)

    def vector(self, dve):
        if self.before_batch is None:
            self.batches(dve, self.c.v.loop(dve, BATCHES - 1, self.steps),
                         lambda i, u: self.prepare_one(dve, i, u), lambda i, u: self.finish_one(dve, i, u), 3)
        else:
            self.by_twos(self.c.v.loop(dve, BATCHES // 2, 2 * self.steps),
                         lambda i, first_row: self.vector_batch(dve, i, first_row))

    def takes_part(self, name):
        return self.store is not None if name == "sync" else name != "gpsimd"

    def sync(self, sp):
        src, to = self.store
        with sp.Fori(0, BATCHES) as i:
            sp.wait_ge(self.used.sem, self.u0 + BATCH * (i + 1))
            sp.dma_start(to.rearrange("(t p) d -> p t d", p=P)[:, bass.ds(i * BATCH, BATCH), :],
                         src[:, bass.ds(i * BATCH, BATCH), :]).then_inc(self.c.store.sem, 16)
        sp.wait_ge(self.c.store.sem, self.stored + 16 * BATCHES)


class TurnWeights(Stage):

    def __init__(self, c, W, rows, K, vectors=()):
        self.c, self.W, self.parts, self.blocks, self.rows = c, W, rows // P, K // P, rows
        self.plain = c.arena[:, 0:self.parts * K].rearrange("p (r k) -> p r k", k=K)
        self.out = c.w_area[:, 0:self.blocks * rows].rearrange("p (b n) -> p b n", n=rows)
        self.vectors = vectors
        self.l0 = c.loads.reserve(16 * len(vectors))
        self.landed = c.counter("plain_weights_landed")
        self.n0 = self.landed.reserve(16)
        self.turned = c.counter("weights_turned")
        self.t0 = self.turned.reserve(self.blocks)

    def sync(self, sp):
        c = self.c
        sp.dma_start(self.plain, self.W.rearrange("(r p) k -> p r k", p=P)).then_inc(self.landed.sem, 16)
        for to, src in self.vectors:
            sp.dma_start(to, src).then_inc(c.loads.sem, 16)
        sp.wait_ge(self.landed.sem, self.n0 + 16)
        sp.wait_ge(c.loads.sem, self.l0 + 16 * len(self.vectors))

    def tensor(self, pe):
        pe.wait_ge(self.landed.sem, self.n0 + 16)
        for b in range(self.blocks):
            for r in range(self.parts):
                ins = pe.transpose(self.c.bank[b][:, r * P:(r + 1) * P], self.plain[:, r, b * P:(b + 1) * P],
                                   self.c.ident[:, :])
            ins.then_inc(self.turned.sem, 1)

    def scalar(self, act):
        for b in range(self.blocks):
            act.wait_ge(self.turned.sem, self.t0 + b + 1)
            act.copy(self.out[:, b, :], self.c.bank[b][:, 0:self.rows])


class Load(Stage):

    background = True

    def __init__(self, c, pairs):
        self.c, self.pairs = c, pairs
        self.l0 = c.loads.reserve(16 * len(pairs))

    def sync(self, sp):
        for to, src in self.pairs:
            with self.c.nc.allow_non_contiguous_dma(reason="vectors of a few hundred elements"):
                sp.dma_start(to, src).then_inc(self.c.loads.sem, 16)
        sp.wait_ge(self.c.loads.sem, self.l0 + 16 * len(self.pairs))


def over(ap, width):
    return ap.unsqueeze(2).broadcast_to([ap.shape[0], ap.shape[1], width])


def along(ap, n):
    return ap.unsqueeze(1).broadcast_to([ap.shape[0], n, ap.shape[1]])


class Steps(Stage):

    def __init__(self, c, make):
        self.c, self.make = c, make

    def vector(self, dve):
        for ins in self.make(dve):
            self.c.v.mark(ins)
            self.c.v.wait(dve)


class Normalise(Stage):

    def __init__(self, c, out, src):
        self.c, self.out, self.src = c, out, src
        self.shift = c.stat_tmp[:, 0, 0:TILES]
        self.shift_ready = c.counter("row_shift_ready")
        self.s0 = self.shift_ready.reserve(1)
        self.cut = 15

    def vector(self, dve):
        c = self.c
        dve.scalar_tensor_tensor(out=self.shift, in0=c.mean[:, :], scalar=-1.0, in1=c.rstd[:, :],
                                 op0=ALU.mult, op1=ALU.mult).then_inc(self.shift_ready.sem, 1)
        for t in range(self.cut):
            dve.tensor_scalar(self.out[:, t, :], self.src[:, t, :], c.mean[:, t:t + 1], c.rstd[:, t:t + 1],
                              ALU.subtract, ALU.mult)

    def scalar(self, act):
        act.wait_ge(self.shift_ready.sem, self.s0 + 1)
        for t in range(self.cut, TILES):
            act.activation(self.out[:, t, :], self.src[:, t, :], ACT.Identity, bias=self.shift[:, t:t + 1],
                           scale=self.c.rstd[:, t:t + 1])


class AddOwnNormalised(Stage):

    def __init__(self, c, x):
        self.c, self.x = c, x
        self.shift, self.gain = c.stat_tmp[:, 0, 0:TILES], c.stat_tmp[:, 1, 0:TILES]
        self.ready = c.counter("row_gain_ready")
        self.r0 = self.ready.reserve(2)
        self.cut = 15

    def vector(self, dve):
        c = self.c
        dve.scalar_tensor_tensor(out=self.shift, in0=c.mean[:, :], scalar=-1.0, in1=c.rstd[:, :],
                                 op0=ALU.mult, op1=ALU.mult).then_inc(self.ready.sem, 1)
        dve.tensor_scalar(self.gain, c.rstd[:, :], 1.0, None, ALU.add).then_inc(self.ready.sem, 1)
        dve.wait_ge(self.ready.sem, self.r0 + 2)
        for t in range(self.cut):
            dve.tensor_scalar(self.x[:, t, :], self.x[:, t, :], self.gain[:, t:t + 1], self.shift[:, t:t + 1],
                              ALU.mult, ALU.add)

    def scalar(self, act):
        act.wait_ge(self.ready.sem, self.r0 + 2)
        for t in range(self.cut, TILES):
            act.activation(self.x[:, t, :], self.x[:, t, :], ACT.Identity, bias=self.shift[:, t:t + 1],
                           scale=self.gain[:, t:t + 1])


class EndConvolution(Stage):

    def __init__(self, c, rows, out, bias):
        self.c, self.rows, self.out, self.bias = c, rows, out, bias
        self.ready = c.counter("last_rows_ready")
        self.r0 = self.ready.reserve(BATCHES)

    def vector(self, dve):
        for t in range(TILES):
            ins = dve.scalar_tensor_tensor(out=self.out[:, t, :], in0=self.rows[:, t, :],
                                           scalar=self.c.dinv[:, t:t + 1], in1=self.bias,
                                           op0=ALU.mult, op1=ALU.add)
            if t % BATCH == BATCH - 1:
                ins.then_inc(self.ready.sem, 1)

    def scalar(self, act):
        for i in range(BATCHES):
            act.wait_ge(self.ready.sem, self.r0 + i + 1)
            batch = self.out[:, i * BATCH:(i + 1) * BATCH, :]
            act.activation(batch, batch, ACT.Relu)


class AddNormed(Stage):

    def __init__(self, c, x, rows, gamma, beta):
        self.c, self.x, self.rows, self.gamma, self.beta = c, x, rows, gamma, beta
        self.beta_added = c.counter("beta_added")
        self.b0 = self.beta_added.reserve(BATCHES)

    def gpsimd(self, pool):
        for i in range(BATCHES):
            batch = self.x[:, i * BATCH:(i + 1) * BATCH, :]
            pool.tensor_tensor(batch, batch, along(self.beta, BATCH), ALU.add).then_inc(self.beta_added.sem, 1)

    def vector(self, dve):
        c, v = self.c, self.c.v
        for t in range(TILES):
            v.mark(dve.scalar_tensor_tensor(out=self.rows[:, t, :], in0=self.rows[:, t, :],
                                            scalar=c.mean[:, t:t + 1], in1=self.gamma,
                                            op0=ALU.subtract, op1=ALU.mult))
        v.wait(dve)
        for t in range(TILES):
            if t % BATCH == 0:
                dve.wait_ge(self.beta_added.sem, self.b0 + t // BATCH + 1)
            v.mark(dve.scalar_tensor_tensor(out=self.x[:, t, :], in0=self.rows[:, t, :],
                                            scalar=c.rstd[:, t:t + 1], in1=self.x[:, t, :],
                                            op0=ALU.mult, op1=ALU.add))
        v.wait(dve)


class StoreTable(Stage):

    def __init__(self, c, src):
        self.c, self.src = c, src
        self.s0 = c.store.reserve(16)

    def sync(self, sp):
        sp.dma_start(self.c.table.rearrange("(t p) d -> p t d", p=P), self.src).then_inc(self.c.store.sem, 16)
        sp.wait_ge(self.c.store.sem, self.s0 + 16)


class BatchNorm(Stage):

    def __init__(self, c, sums, gamma, beta):
        self.c, self.gamma, self.beta = c, gamma, beta
        self.sums = sums
        self.centred = c.big_b[:, 0:TILES * D].rearrange("p (t d) -> p t d", d=D)
        self.square = c.big_b[:, TILES * D:2 * TILES * D].rearrange("p (t d) -> p t d", d=D)
        self.mean, self.gain = c.arena[:, 0:D], c.arena[:, D:2 * D]
        self.ready = c.counter("columns_to_sum")
        self.r0 = self.ready.reserve(1)
        self.summed = c.counter("columns_summed")
        self.s0 = self.summed.reserve(2)
        self.asked = c.counter("norm_asked")
        self.q0 = self.asked.reserve(4)
        self.shift = c.arena[:, 2 * D:2 * D + TILES]
        self.normalised = c.counter("rows_normalised")
        self.m0 = self.normalised.reserve(1)
        self.answered = c.counter("norm_answered")
        self.n0 = self.answered.reserve(3)

    def tensor(self, pe):
        c = self.c
        for n, what in enumerate((self.sums[:, :, 0:D], self.square)):
            if n == 1:
                pe.wait_ge(self.ready.sem, self.r0 + 1)
            out = c.bank[n][:, 0:D]
            pe.matmul(out, c.ones[:, :], what[:, 0, :], start=True, stop=False)
            with pe.Fori(1, TILES - 1) as t:
                pe.matmul(out, c.ones[:, :], what[:, bass.ds(t, 1), :], start=False, stop=False)
            pe.matmul(out, c.ones[0:LAST, :], what[0:LAST, TILES - 1, :], start=False, stop=True
                      ).then_inc(self.summed.sem, 1)

    def vector(self, dve):
        c, v = self.c, self.c.v
        deg = c.dinv[:, :]
        dve.tensor_scalar(deg, self.sums[:, :, D], 1.0, None, ALU.add).then_inc(self.asked.sem, 1)
        v.mark(dve.scalar_tensor_tensor(out=self.shift, in0=c.mean[:, :], scalar=-1.0, in1=c.rstd[:, :],
                                        op0=ALU.mult, op1=ALU.mult))
        dve.wait_ge(self.answered.sem, self.n0 + 1)
        v.mark(dve.reciprocal(deg, deg))
        dve.wait_ge(self.summed.sem, self.s0 + 1)
        v.mark(dve.tensor_scalar(self.mean, c.bank[0][:, 0:D], 1.0 / NODES, None, ALU.mult))
        v.wait(dve)
        dve.tensor_tensor(self.centred, self.sums[:, :, 0:D], along(self.mean, TILES), ALU.subtract
                          ).then_inc(self.asked.sem, 1)
        dve.wait_ge(self.summed.sem, self.s0 + 2)
        dve.tensor_scalar(self.gain, c.bank[1][:, 0:D], 1.0 / NODES, EPS, ALU.mult, ALU.add
                          ).then_inc(self.asked.sem, 1)
        dve.wait_ge(self.answered.sem, self.n0 + 2)
        v.mark(dve.reciprocal(self.gain, self.gain))
        v.wait(dve)
        v.mark(dve.tensor_tensor(self.gain, self.gain, self.gamma, ALU.mult))
        v.wait(dve)
        v.mark(dve.tensor_tensor(self.centred, self.centred, along(self.gain, TILES), ALU.mult))
        v.wait(dve)
        dve.tensor_tensor(self.centred, self.centred, along(self.beta, TILES), ALU.add
                          ).then_inc(self.asked.sem, 1)
        h = self.sums[:, :, 0:D]
        dve.wait_ge(self.asked.sem, self.q0 + 4)
        dve.wait_ge(self.normalised.sem, self.m0 + 1)
        v.mark(dve.scalar_tensor_tensor(out=h, in0=self.centred, scalar=0.0, in1=h, op0=ALU.max, op1=ALU.add))
        v.wait(dve)
        dve.wait_ge(self.answered.sem, self.n0 + 3)
        v.mark(dve.scalar_tensor_tensor(out=h, in0=self.square, scalar=1.0, in1=h, op0=ALU.min, op1=ALU.add))
        v.wait(dve)
        v.mark(dve.scalar_tensor_tensor(out=c.x[:, :, :], in0=h, scalar=-1.0, in1=c.x[:, :, :],
                                        op0=ALU.add, op1=ALU.add))
        v.wait(dve)

    def scalar(self, act):
        c = self.c
        act.wait_ge(self.asked.sem, self.q0 + 1)
        act.activation(c.dinv[:, :], c.dinv[:, :], ACT.Sqrt).then_inc(self.answered.sem, 1)
        act.wait_ge(self.asked.sem, self.q0 + 2)
        act.activation(self.square, self.centred, ACT.Square).then_inc(self.ready.sem, 1)
        for t in range(TILES):
            ins = act.activation(self.sums[:, t, 0:D], c.x[:, t, :], ACT.Identity, bias=self.shift[:, t:t + 1],
                                 scale=c.rstd[:, t:t + 1])
        ins.then_inc(self.normalised.sem, 1)
        act.wait_ge(self.asked.sem, self.q0 + 3)
        act.activation(self.gain, self.gain, ACT.Sqrt).then_inc(self.answered.sem, 1)
        act.wait_ge(self.asked.sem, self.q0 + 4)
        act.activation(self.square, self.centred, ACT.Exp).then_inc(self.answered.sem, 1)


class Route(Stage):

    def __init__(self, c, logits, kind):
        self.c, self.logits, self.kind = c, logits, kind
        self.T = 1 if kind == "pooled" else TILES
        n = [0]

        def part(size):
            n[0] += size
            return c.arena[:, n[0] - size:n[0]]

        T = self.T
        self.l, self.l2, self.eq, self.first, self.second, self.p = (
            part(T * EXPERTS).rearrange("p (t e) -> p t e", e=EXPERTS) for _ in range(6))
        self.m1, self.m2, self.at, self.e2, self.s, self.w1, self.w2 = (part(T) for _ in range(7))
        self.below = part(EXPERTS)
        self.load = part(EXPERTS)
        self.asked = c.counter("exp_asked")
        self.answered = c.counter("exp_answered")
        self.n = {"softmax": 1, "probs": 2, "pooled": 3}[kind]
        self.q0, self.a0 = self.asked.reserve(self.n), self.answered.reserve(self.n)
        self.pool_sum = c.counter("logits_summed")
        self.p0 = self.pool_sum.reserve(1 if kind == "pooled" else 0)
        self.exps = {"softmax": [self.e2], "probs": [self.e2, self.p],
                     "pooled": [self.l, self.l2, self.e2]}[kind]

    def takes_part(self, name):
        return name in ("vector", "scalar") or (name == "tensor" and self.kind == "pooled")

    def tensor(self, pe):
        c = self.c
        pe.matmul(c.bank[0][:, 0:(TILES - 1) * EXPERTS], c.ones[:, :],
                  self.logits[:, 0:TILES - 1, :].rearrange("p t e -> p (t e)"), start=True, stop=True)
        pe.matmul(c.bank[1][:, 0:EXPERTS], c.ones[0:LAST, :], self.logits[0:LAST, TILES - 1, :],
                  start=True, stop=True).then_inc(self.pool_sum.sem, 1)

    def scalar(self, act):
        for n, what in enumerate(self.exps):
            act.wait_ge(self.asked.sem, self.q0 + n + 1)
            act.activation(what, what, ACT.Exp).then_inc(self.answered.sem, 1)

    def vector(self, dve):
        c, v, T = self.c, self.c.v, self.T
        asked = [0]

        def step(ins):
            v.mark(ins)
            v.wait(dve)

        def exp(ins):
            ins.then_inc(self.asked.sem, 1)
            asked[0] += 1
            dve.wait_ge(self.answered.sem, self.a0 + asked[0])

        logits = self.logits
        step(dve.tensor_scalar(self.below, c.iota[:, 0:EXPERTS], float(-EXPERTS), None, ALU.add))
        if self.kind == "pooled":
            dve.wait_ge(self.pool_sum.sem, self.p0 + 1)
            logits = self.l
            l, l2 = self.l[:, 0, :], self.l2[:, 0, :]
            step(dve.tensor_reduce(l, c.bank[0][:, 0:(TILES - 1) * EXPERTS].rearrange("p (t e) -> p e t", e=EXPERTS),
                                   AX_X, ALU.add))
            step(dve.tensor_tensor(l, l, c.bank[1][:, 0:EXPERTS], ALU.add))
            step(dve.tensor_scalar(l, l, 1.0 / NODES, None, ALU.mult))
            capacity = float(-(-NODES * 5 // (4 * EXPERTS)))
            for which, a in enumerate((l, l2)):
                step(dve.tensor_reduce(self.m1, a, AX_X, ALU.max))
                exp(dve.tensor_scalar(a, a, self.m1[:, 0:1], None, ALU.subtract))
                step(dve.tensor_reduce(self.s, a, AX_X, ALU.add))
                step(dve.reciprocal(self.s, self.s))
                step(dve.tensor_scalar(a, a, self.s[:, 0:1], None, ALU.mult))
                if which == 0:
                    step(dve.tensor_scalar(self.load, a, float(NODES), None, ALU.mult))
                    step(dve.tensor_scalar(self.eq[:, 0, :], self.load, capacity, None, ALU.is_gt))
                    step(dve.tensor_scalar(self.load, self.load, capacity, None, ALU.max))
                    step(dve.reciprocal(self.load, self.load))
                    step(dve.tensor_scalar(self.load, self.load, capacity, -1.0, ALU.mult, ALU.add))
                    step(dve.tensor_tensor(self.load, self.load, self.eq[:, 0, :], ALU.mult))
                    step(dve.scalar_tensor_tensor(out=l2, in0=self.load, scalar=1.0, in1=a,
                                                  op0=ALU.add, op1=ALU.mult))
            logits = self.l2
        below = along(self.below, T)

        def pick(values, best, onehot):
            step(dve.tensor_reduce(best, values, AX_X, ALU.max))
            step(dve.tensor_tensor(self.eq, values, over(best, EXPERTS), ALU.is_equal))
            step(dve.tensor_tensor(self.eq, self.eq, below, ALU.mult))
            step(dve.tensor_reduce(self.at, self.eq, AX_X, ALU.min))
            step(dve.tensor_tensor(onehot, below, over(self.at, EXPERTS), ALU.is_equal))

        pick(logits, self.m1, self.first)
        if self.kind == "pooled":
            step(dve.tensor_scalar(c.chosen[:, 0:1], self.at, float(EXPERTS), None, ALU.add))
        rest = self.p
        step(dve.scalar_tensor_tensor(out=rest, in0=self.first, scalar=-1e30, in1=logits, op0=ALU.mult, op1=ALU.add))
        pick(rest, self.m2, self.second)
        if self.kind == "pooled":
            step(dve.tensor_scalar(c.chosen[:, 1:2], self.at, float(EXPERTS), None, ALU.add))
        exp(dve.tensor_tensor(self.e2, self.m2, self.m1, ALU.subtract))
        if self.kind == "probs":
            exp(dve.tensor_tensor(self.p, logits, over(self.m1, EXPERTS), ALU.subtract))
            step(dve.tensor_reduce(self.s, self.p, AX_X, ALU.add))
            step(dve.reciprocal(self.w1, self.s))
            step(dve.tensor_tensor(self.w2, self.e2, self.w1, ALU.mult))
            step(dve.tensor_tensor(self.s, self.w1, self.w2, ALU.add))
            step(dve.tensor_scalar(self.s, self.s, 1e-12, None, ALU.max))
            step(dve.reciprocal(self.s, self.s))
            step(dve.tensor_tensor(self.w1, self.w1, self.s, ALU.mult))
            step(dve.tensor_tensor(self.w2, self.w2, self.s, ALU.mult))
        else:
            step(dve.tensor_scalar(self.s, self.e2, 1.0, None, ALU.add))
            step(dve.reciprocal(self.w1, self.s))
            step(dve.tensor_tensor(self.w2, self.e2, self.w1, ALU.mult))
        step(dve.tensor_tensor(self.first, self.first, over(self.w1, EXPERTS), ALU.mult))
        step(dve.tensor_tensor(self.second, self.second, over(self.w2, EXPERTS), ALU.mult))
        if T == 1:
            step(dve.tensor_tensor(self.first, self.first, self.second, ALU.add))
            step(dve.tensor_copy(c.gates[:, :, :], along(self.first[:, 0, :], TILES)))
            step(dve.tensor_copy(c.chosen_weight[:, 0:1], self.w1))
            step(dve.tensor_copy(c.chosen_weight[:, 1:2], self.w2))
        else:
            step(dve.tensor_tensor(c.gates[:, :, :], self.first, self.second, ALU.add))


class BiasStart(Stage):

    def __init__(self, c, copies, diagonal, out, onto):
        self.c, self.copies, self.out, self.onto = c, copies, out, onto
        self.diagonal = diagonal.rearrange("p (a d) -> p a d", a=4)
        self.sizes = [P, TILES * EXPERTS - P]
        self.turned_gates = [c.arena[0:n, k * P:(k + 1) * P] for k, n in enumerate(self.sizes)]
        self.groups = -(-TILES // 4)
        self.turned = c.counter("gates_turned")
        self.t0 = self.turned.reserve(2)
        self.copied = c.counter("gates_copied")
        self.c0 = self.copied.reserve(2)
        self.laid = c.counter("bias_diagonal_ready")
        self.l0 = self.laid.reserve(4)
        self.product = c.counter("bias_products")
        self.p0 = self.product.reserve(-(-TILES // 2))
        self.taken = [c.counter(f"bias_taken_by_{e}") for e in ("vector", "scalar")]
        self.k0 = [self.taken[0].reserve(self.groups), self.taken[1].reserve(TILES // 4)]

    def bank(self, g, h):
        return self.c.bank[2 + (2 * g + h) % 6]

    def tensor(self, pe):
        c = self.c
        gates = c.gates[:, :, :].rearrange("p t e -> p (t e)")
        for k, n in enumerate(self.sizes):
            pe.transpose(c.bank[k][0:n, 0:P], gates[:, k * P:k * P + n], c.ident[:, :]).then_inc(self.turned.sem, 1)
        pe.wait_ge(self.laid.sem, self.l0 + 4)
        pe.wait_ge(self.copied.sem, self.c0 + 2)
        for g in range(self.groups):
            rows = min(4, TILES - 4 * g) * EXPERTS
            at = g % 4 * 32
            for h in range(2):
                if 4 * g + 2 * h >= TILES:
                    continue
                if g >= 3:
                    pe.wait_ge(self.taken[h].sem, self.k0[h] + g - 2)
                width = min(2, TILES - 4 * g - 2 * h) * D
                pe.matmul(self.bank(g, h)[:, 0:width], self.turned_gates[g // 4][at:at + rows, :],
                          self.diagonal[at:at + rows, 2 * h:2 * h + width // D, :], start=True, stop=True,
                          ).then_inc(self.product.sem, 1)

    def take(self, eng, g, h, use):
        first = 4 * g + 2 * h
        if first < TILES:
            n = min(2, TILES - first)
            eng.wait_ge(self.product.sem, self.p0 + 2 * g + h + 1)
            use(self.out[:, first:first + n, :],
                self.bank(g, h)[:, 0:n * D].rearrange("p (a d) -> p a d", a=n)).then_inc(self.taken[h].sem, 1)

    def vector(self, dve):
        for k in range(4):
            dve.tensor_scalar(self.diagonal[:, k, :], self.copies, self.c.quarter[:, k:k + 1], None, ALU.mult
                              ).then_inc(self.laid.sem, 1)
        for g in range(self.groups):
            if self.onto:
                for h in range(2):
                    self.take(dve, g, h, lambda out, product: dve.tensor_tensor(out, out, product, ALU.add))
            else:
                self.take(dve, g, 0, dve.tensor_copy)

    def scalar(self, act):
        for k, n in enumerate(self.sizes):
            act.wait_ge(self.turned.sem, self.t0 + k + 1)
            act.copy(self.turned_gates[k], self.c.bank[k][0:n, 0:P]).then_inc(self.copied.sem, 1)
        if not self.onto:
            for g in range(self.groups):
                self.take(act, g, 1, act.copy)


class Experts(Stage):

    def __init__(self, c, columns, out, W1, b1, W2, H, func, chosen=False):
        self.c, self.columns, self.out, self.H, self.func = c, columns, out, H, func
        self.W1, self.W2, self.b1, self.chosen = W1, W2, b1, chosen
        self.one_expert = H == 2 * UNIT
        self.trips = (2 if chosen else EXPERTS) // (1 if self.one_expert else 2)
        assert self.one_expert or not chosen
        self.MC, self.KC = UNIT // P, D // P
        self.width = BATCH * P
        self.half = self.width // 2
        size = self.KC * UNIT + self.MC * D

        def weights(area, at):
            return (area[:, at:at + self.KC * UNIT].rearrange("p (b n) -> p b n", n=UNIT),
                    area[:, at + self.KC * UNIT:at + size].rearrange("p (b n) -> p b n", n=D))

        self.plain = [weights(c.w_area, k * size) for k in range(2)]
        self.high = [weights(c.w_area_r, (2 + 2 * k) * size) for k in range(2)]
        self.low = [weights(c.w_area_r, (3 + 2 * k) * size) for k in range(2)]
        self.weights_masked = c.w_area[:, 6 * size:6 * size + self.KC * UNIT]
        assert 6 * size + self.KC * UNIT <= 7000
        n = self.MC * self.width
        self.hidden_high, self.hidden_low = (
            [c.arena_r[:, (2 * k + a) * n:(2 * k + a + 1) * n].rearrange("p (m n) -> p m n", m=self.MC)
             for k in range(2)] for a in range(2))
        self.hidden = [c.arena[:, 4 * n + m * self.width:4 * n + (m + 1) * self.width] for m in range(self.MC)]
        self.masked = c.arena[:, 4 * n + self.MC * self.width:4 * n + (self.MC + 1) * self.width]
        assert 4 * n + (self.MC + 1) * self.width <= RING_AT
        self.step_b1 = c.cols[:, 32:32 + 2 * self.MC]
        self.units = 2 * self.trips
        self.groups = self.units * BATCHES
        self.parts = 2 * self.MC
        self.bias = c.counter("step_bias_ready")
        self.b0 = self.bias.reserve(self.trips)
        self.landed = [c.counter(f"unit_weights{k}_landed") for k in range(2)]
        self.l0 = [s.reserve(32 * self.trips) for s in self.landed]
        self.split = c.counter("unit_weights_split")
        self.s0 = self.split.reserve(2 * self.units)
        self.up = c.counter("hidden_summed")
        self.u0 = self.up.reserve(self.groups * self.parts)
        self.active = c.counter("hidden_active")
        self.a0 = self.active.reserve(self.groups * self.parts)
        self.high_known = c.counter("hidden_masked")
        self.h0 = self.high_known.reserve(self.groups * self.MC)
        self.high_ready = c.counter("hidden_high_ready")
        self.i0 = self.high_ready.reserve(self.groups * self.MC)
        self.low_ready = c.counter("hidden_low_ready")
        self.r0 = self.low_ready.reserve(self.groups * self.MC)
        self.down = c.counter("expert_summed")
        self.d0 = self.down.reserve(self.groups * BATCH)
        self.added = c.counter("expert_added")
        self.g0 = self.added.reserve(self.groups * BATCH)

    def expert(self, eng, i, k):
        if self.chosen:
            return eng.value_load(self.c.chosen[0:1, bass.ds(i, 1)], min_val=0, max_val=EXPERTS - 1)
        return i if self.one_expert else 2 * i + k

    def sync(self, sp):
        with sp.Fori(0, self.trips) as i:
            for k in range(2):
                self.c.hold(sp, "sync", self.split.sem, self.s0 + 2 * (2 * i + k - 1))
                e = self.expert(sp, i, k)
                at = k * UNIT if self.one_expert else 0
                w1, w2 = self.plain[k]
                sp.dma_start(w1, self.W1[bass.ds(e, 1), :, at:at + UNIT].rearrange("a (b p) h -> p (a b) h", p=P)
                             ).then_inc(self.landed[k].sem, 16)
                sp.dma_start(w2, self.W2[bass.ds(e, 1), at:at + UNIT, :].rearrange("a (b p) h -> p (a b) h", p=P)
                             ).then_inc(self.landed[k].sem, 16)
        for k in range(2):
            sp.wait_ge(self.landed[k].sem, self.l0[k] + 32 * self.trips)

    def down_bank(self, n, u):
        return self.c.bank[4 + (BATCH * n + u) % 4][:, 0:D]

    def tensor(self, pe):
        c = self.c

        def product(out, pairs):
            terms = [(left[x], right[y]) for left, right in pairs for x, y in ((0, 0), (0, 1), (1, 0))]
            for n, (left, right) in enumerate(terms):
                ins = pe.matmul(out, left, right, start=n == 0,
                                stop=n == len(terms) - 1)
            return ins

        def up(i, n):
            k, g = divmod(n, BATCHES)
            if g == 0:
                pe.wait_ge(self.split.sem, self.s0 + 2 * (2 * i + k + 1))
            for q in range(self.parts):
                m, half = divmod(q, 2)
                count = self.parts * (2 * BATCHES * i + n) + q
                pe.wait_ge(self.active.sem, self.a0 + count - 3)
                at = g * self.width + half * self.half
                product(c.bank[q % 4][:, 0:self.half],
                        [([w[k][0][:, b, m * P:(m + 1) * P] for w in (self.high, self.low)],
                          [x[b][:, at:at + self.half] for x in self.columns]) for b in range(self.KC)]
                        ).then_inc(self.up.sem, 1)

        def down(i, n):
            k = n // BATCHES
            pe.wait_ge(self.high_ready.sem, self.i0 + self.MC * (2 * BATCHES * i + n + 1))
            pe.wait_ge(self.low_ready.sem, self.r0 + self.MC * (2 * BATCHES * i + n + 1))
            for u in range(BATCH):
                back = 2 if n == 0 and u < 2 else 4
                pe.wait_ge(self.added.sem, self.g0 + BATCH * (2 * BATCHES * i + n) + u + 1 - back)
                product(self.down_bank(n, u),
                        [([h[n % 2][:, m, u * P:(u + 1) * P] for h in (self.hidden_high, self.hidden_low)],
                          [w[k][1][:, m, :] for w in (self.high, self.low)]) for m in range(self.MC)]
                        ).then_inc(self.down.sem, 1)

        def step(i, last):
            for n in range(2 * BATCHES):
                if n + 1 < 2 * BATCHES:
                    up(i, n + 1)
                elif not last:
                    up(i + 1, 0)
                down(i, n)

        up(0, 0)
        with pe.Fori(0, self.trips - 1) as i:
            step(i, False)
        step(self.trips - 1, True)

    def scalar(self, act):
        c = self.c
        with act.Fori(0, self.trips) as i:
            c.hold(act, "scalar", self.active.sem, self.a0 + self.parts * 2 * BATCHES * i)
            columns = self.MC * 2
            first = self.expert(act, i, 0) * (columns if self.one_expert else columns // 2)
            act.copy(self.step_b1, self.b1[:, bass.ds(first, columns)]).then_inc(self.bias.sem, 1)
            act.wait_ge(self.bias.sem, self.b0 + i + 1)
            for n in range(2 * BATCHES):
                k, g = n // BATCHES, 2 * BATCHES * i + n

                def activate(q):
                    m, half = divmod(q, 2)
                    if half == 0:
                        act.wait_ge(self.low_ready.sem, self.r0 + self.MC * (g - 1) + m + 1)
                    act.wait_ge(self.up.sem, self.u0 + self.parts * g + q + 1)
                    act.activation(self.hidden[m][:, half * self.half:(half + 1) * self.half],
                                   c.bank[q % 4][:, 0:self.half], self.func,
                                   bias=self.step_b1[:, k * self.MC + m:k * self.MC + m + 1]
                                   ).then_inc(self.active.sem, 1)

                def round_high(m):
                    act.wait_ge(self.high_known.sem, self.h0 + self.MC * g + m + 1)
                    if m == 0:
                        act.wait_ge(self.down.sem, self.d0 + BATCH * (g - 1))
                    act.copy(self.hidden_high[n % 2][:, m, :], self.masked).then_inc(self.high_ready.sem, 1)

                activate(0)
                activate(1)
                activate(2)
                round_high(0)
                activate(3)
                round_high(1)

    def vector(self, dve):
        c, v = self.c, self.c.v

        def split_weights(i, k, which):
            if which == 0:
                dve.wait_ge(self.landed[k].sem, self.l0[k] + 32 * (i + 1))
                dve.wait_ge(self.down.sem, self.d0 + TILES * (2 * i + k - 1))
            plain, high, low = self.plain[k][which], self.high[k][which], self.low[k][which]
            masked = self.weights_masked.rearrange("p (b n) -> p b n", b=2)
            dve.wait_ge(self.split.sem, self.s0 + 2 * (2 * i + k) + which)
            v.mark(high_bits(dve, masked, plain))
            v.wait(dve)
            v.mark(dve.tensor_copy(high, masked))
            dve.tensor_tensor(low, plain, masked, ALU.subtract).then_inc(self.split.sem, 1)

        def split_hidden(i, n, m):
            g = 2 * BATCHES * i + n
            dve.wait_ge(self.active.sem, self.a0 + self.parts * g + 2 * (m + 1))
            dve.wait_ge(self.high_ready.sem, self.i0 + self.MC * g + m)
            dve.wait_ge(self.low_ready.sem, self.r0 + self.MC * g + m)
            if m == 0:
                dve.wait_ge(self.down.sem, self.d0 + BATCH * (g - 1))
            high_bits(dve, self.masked, self.hidden[m]).then_inc(self.high_known.sem, 1)
            dve.wait_ge(self.high_known.sem, self.h0 + self.MC * g + m + 1)
            dve.tensor_tensor(self.hidden_low[n % 2][:, m, :], self.hidden[m], self.masked, ALU.subtract
                              ).then_inc(self.low_ready.sem, 1)

        def add(i, n, u):
            k, g = divmod(n, BATCHES)
            t = g * BATCH + u
            count = BATCH * (2 * BATCHES * i + n) + u
            dve.wait_ge(self.down.sem, self.d0 + count + 1)
            if u == 0:
                dve.wait_ge(self.added.sem, self.g0 + count + BATCH - TILES)
            if self.chosen:
                gate = c.chosen_weight[:, bass.ds(i, 1)]
            else:
                gate = c.gates[:, t, bass.ds(self.expert(dve, i, k), 1)]
            dve.scalar_tensor_tensor(out=self.out[:, t, :], in0=self.down_bank(n, u), scalar=gate,
                                     in1=self.out[:, t, :], op0=ALU.mult, op1=ALU.add
                                     ).then_inc(self.added.sem, 1)

        def step(i, last):
            for n in range(2 * BATCHES):
                g = n % BATCHES
                if g in (1, 3) and not (last and n >= BATCHES):
                    split_weights(i + n // BATCHES, 1 - n // BATCHES, g // 2)
                after = (i, n + 1) if n + 1 < 2 * BATCHES else (i + 1, 0)
                more = not (last and n + 1 == 2 * BATCHES)
                if more:
                    split_hidden(*after, 0)
                add(i, n, 0)
                add(i, n, 1)
                if more:
                    split_hidden(*after, 1)
                for u in range(2, BATCH):
                    add(i, n, u)

        split_weights(0, 0, 0)
        split_weights(0, 0, 1)
        for m in range(self.MC):
            split_hidden(0, 0, m)
        with v.loop(dve, self.trips - 1, 8) as i:
            step(i, False)
        step(self.trips - 1, True)


class Finish(Stage):

    def __init__(self, c):
        self.c = c
        self.s0 = c.store.reserve(32)

    def sync(self, sp):
        c, whole = self.c, (TILES - 1) * P
        sp.dma_start(c.out[0:whole, :].rearrange("(t p) d -> p t d", p=P), c.x[:, 0:TILES - 1, :]
                     ).then_inc(c.store.sem, 16)
        sp.dma_start(c.out[whole:NODES, :], c.x[0:LAST, TILES - 1, :]).then_inc(c.store.sem, 16)
        sp.wait_ge(c.store.sem, self.s0 + 32)


def gnn_ffn_layers(nc, T, out, stages_of):
    with ExitStack() as ctx:
        c = Core(nc, ctx, T, out)
        stages = stages_of(c)
        number(stages, c.engines)
        block = ctx.enter_context(nc.Block())

        @block.sync
        def _(sp):
            for counter in c.counters.values():
                if counter.lead:
                    sp.sem_inc(counter.sem, counter.lead)
            c.run("sync", sp, stages)

        @block.tensor
        def _(pe):
            c.run("tensor", pe, stages)

        @block.vector
        def _(dve):
            c.run("vector", dve, stages)

        @block.scalar
        def _(act):
            c.run("scalar", act, stages)

        @block.gpsimd
        def _(pool):
            c.run("gpsimd", pool, stages)


class BetweenConvolutions:

    def __init__(self, c, rows, width, cuts=(0, BATCH)):
        self.c, self.rows, self.width = c, rows, width
        self.parts = list(zip(cuts[:-1], cuts[1:]))
        self.chunks = -(-width // 512)
        self.groups = 2 * self.chunks
        self.stats = c.stat_in[:, 0:BATCH * self.groups * 3]
        self.mean, self.rstd = c.batch_mean[:, 0:BATCH], c.batch_mean[:, BATCH:2 * BATCH]
        self.s = [Statistics(c, hi - lo, self.groups, width, uses=BATCHES, tag=f"part{lo}_")
                  for lo, hi in self.parts]
        self.steps = BATCH * self.chunks + sum(s.STEPS for s in self.s)

    def statistics(self, dve, i, tiles, ready, first_row=0):
        c, v = self.c, self.c.v
        for u in tiles:
            ready(u)
            for j in range(self.chunks):
                n = min(512, self.width)
                at = (u * self.chunks + j) * 6
                v.mark(dve.bn_stats(self.stats[:, at:at + 6], self.rows[:, first_row + u, j * n:(j + 1) * n]))
        v.wait(dve)
        part = self.parts.index((tiles[0], tiles[-1] + 1))
        lo, hi = self.parts[part]
        self.s[part].vector(dve, self.stats.rearrange("p (t g s) -> p t g s", g=self.groups, s=3)[:, lo:hi],
                            self.mean[:, lo:hi], self.rstd[:, lo:hi], use=i)

    def normalise(self, dve, u, rows):
        return dve.tensor_scalar(rows, rows, self.mean[:, u:u + 1], self.rstd[:, u:u + 1],
                                 ALU.subtract, ALU.mult)


class FirstConvolutions(Stage):

    def __init__(self, c, sums, own, W1, b1, W2, gain, shift, out, table):
        self.c = c
        hidden, width = 1024, 512

        def combine(dve, i, u, to):
            to3 = to.rearrange("p (a d) -> p a d", a=1)
            c.v.mark(dve.tensor_tensor(to3, sums[:, tiles5(i, u), :], own[:, tiles5(i, u), :], ALU.add))
            c.v.wait(dve)
            return dve.tensor_scalar(to, to, c.dinv[:, tiles5(i, u)], None, ALU.mult)

        def add_bias(dve, i, u, banks):
            dve.wait_ge(self.second.turned.sem, self.second.t0 + self.second.G * (BATCH * (i - 1) + u + 1))
            for j, bank in enumerate(banks):
                ins = dve.tensor_tensor(self.second.rows[:, u, j * 512:(j + 1) * 512], bank[:, :],
                                        b1[:, j * 512:(j + 1) * 512], ALU.add)
            return ins

        def scale(act, i, u, banks):
            return act.activation(out[:, tiles5(i, u), :], banks[0][:, :].rearrange("p (a d) -> p a d", a=1),
                                  ACT.Identity, scale=c.dinv[:, tiles5(i, u)])

        self.first = Project(c, D, hidden, W1, combine, add_bias, "vector", tag="first_",
                             rows=c.big_a[:, 6656:6656 + BATCH * D], columns=c.big_a[:, 8192:8192 + 2 * D])
        self.second = Project(c, hidden, width, W2, lambda dve, i, u, to: self.between.normalise(dve, u, to), scale,
                              "scalar", affine=(gain, shift), store=(out, table), first_bank=6)
        self.cut = 3
        self.between = BetweenConvolutions(c, self.second.rows, hidden, (0, self.cut, BATCH))
        self.relu_ready = c.counter("relu_ready")
        self.r0 = self.relu_ready.reserve(TILES)

    def tensor(self, pe):
        with pe.Fori(0, BATCHES) as i:
            self.first.tensor_batch(pe, i)
            self.second.tensor_batch(pe, i)

    def vector(self, dve):
        c = self.c

        def ready(u):
            dve.wait_ge(self.relu_ready.sem, self.r0 + BATCH * i + u + 1)

        with c.v.loop(dve, BATCHES, BATCH + self.between.steps) as i:
            for u in range(BATCH):
                self.first.prepare_one(dve, i, u)
            for u in range(self.cut):
                self.first.finish_one(dve, i, u)
            self.between.statistics(dve, i, range(self.cut), ready)
            for u in range(self.cut, BATCH):
                self.first.finish_one(dve, i, u)
            for u in range(self.cut):
                self.second.prepare_one(dve, i, u)
            self.between.statistics(dve, i, range(self.cut, BATCH), ready)
            for u in range(self.cut, BATCH):
                self.second.prepare_one(dve, i, u)

    def scalar(self, act):
        with act.Fori(0, BATCHES) as i:
            def relu(u):
                act.wait_ge(self.first.used.sem, self.first.u0 + BATCH * i + u + 1)
                rows = self.second.rows[:, u, :]
                act.activation(rows, rows, ACT.Relu).then_inc(self.relu_ready.sem, 1)

            for u in range(BATCH):
                self.first.copy_columns(act, i, u)
                if u >= 2:
                    relu(u - 2)
            self.between.s[0].scalar(act, use=i)
            for u in range(self.cut, BATCH):
                relu(u)
            self.second.scalar_batch(act, i, lambda: self.between.s[1].scalar(act, use=i))

    def sync(self, sp):
        self.second.sync(sp)


class PrepareSecond:

    def __init__(self, c, project_of, sums, own, bias, width):
        self.c, self.project_of, self.sums, self.own, self.bias = c, project_of, sums, own, bias
        rows = c.arena[:, 0:2 * BATCH * width].rearrange("p (u d) -> p u d", d=width)
        self.between = BetweenConvolutions(c, rows, width)
        self.steps = 3 * BATCH + self.between.steps

    def vector(self, dve, i, first_row):
        c, v, project = self.c, self.c.v, self.project_of()
        rows = self.between.rows[:, first_row:first_row + BATCH, :]
        for u in range(BATCH):
            dve.wait_ge(project.turned.sem, project.t0 + project.G * (BATCH * (i - 2) + u + 1))
            v.mark(dve.tensor_tensor(rows[:, u:u + 1, :], self.sums[:, tiles5(i, u), :],
                                     self.own[:, tiles5(i, u), :], ALU.add))
        v.wait(dve)
        for u in range(BATCH):
            v.mark(dve.scalar_tensor_tensor(out=rows[:, u, :], in0=rows[:, u, :], scalar=c.dinv[:, tiles5(i, u)],
                                            in1=self.bias, op0=ALU.mult, op1=ALU.add))
        v.wait(dve)
        for u in range(BATCH):
            v.mark(dve.tensor_scalar(rows[:, u, :], rows[:, u, :], 0.0, None, ALU.max))
        v.wait(dve)
        self.between.statistics(dve, i, range(BATCH), lambda u: None, first_row)

    def scalar(self, act, i):
        self.between.s[0].scalar(act, use=i)


class LastRows(Stage):

    background = True

    def __init__(self, c):
        self.c = c
        self.edge = c.last_number[:, :]
        self.ready = c.counter("last_edges_ready")
        self.r0 = self.ready.reserve(1)
        self.landed = c.counter("last_rows_landed", 0)
        self.l0 = self.landed.reserve(16 * TILES)

    def gpsimd(self, pool):
        c = self.c
        dst = c.T["dst"].rearrange("(e a) -> e a", a=1)
        pool.wait_ge(self.ready.sem, self.r0 + 1)
        for t in range(TILES):
            pool.indirect_dma_start(c.last_row[:, t:t + 1], None, dst,
                                    bass.IndirectOffsetOnAxis(ap=self.edge[:, t:t + 1], axis=0)
                                    ).then_inc(self.landed.sem, 16)
        pool.wait_ge(self.landed.sem, self.l0 + 16 * TILES)

    def vector(self, dve):
        dve.tensor_scalar(self.edge, self.c.last_edge[:, :], 1.0, 0.0, ALU.subtract, ALU.max
                          ).then_inc(self.ready.sem, 1)


class GatherLast(Stage):

    background = True

    def __init__(self, c, out):
        self.c, self.out = c, out
        self.landed = c.counter("last_features_landed", 0)
        self.n0 = self.landed.reserve(16 * TILES)

    def gpsimd(self, pool):
        c = self.c
        for t in range(TILES):
            pool.indirect_dma_start(self.out[:, t, :], None, c.table,
                                    bass.IndirectOffsetOnAxis(ap=c.last_row[:, t:t + 1], axis=0)
                                    ).then_inc(self.landed.sem, 16)
        pool.wait_ge(self.landed.sem, self.n0 + 16 * TILES)


def tiles_of(area, width=D, at=0):
    return area[:, at:at + TILES * width].rearrange("p (t d) -> p t d", d=width)


def network(c):
    T = c.T
    stages = []

    def do(stage, *join):
        stage.join += join
        stages.append(stage)
        return stage

    def everywhere(name, at, n, area=None):
        to = (c.vec if area is None else area)[:, at:at + n]
        return to, T[name].partition_broadcast(P)

    def by_partition(name, at, n):
        return c.cols[:, at:at + n // P], T[name].rearrange("(b p) -> p b", p=P)

    def normalise_from(src):
        def prepare(dve, i, u, to):
            return dve.tensor_scalar(to.rearrange("p (a d) -> p a d", a=1), src[:, tiles5(i, u), :],
                                     c.mean[:, tiles5(i, u)], c.rstd[:, tiles5(i, u)], ALU.subtract, ALU.mult)
        return prepare

    x = c.x[:, :, :]
    sums = tiles_of(c.big_a)

    def project_nodes(W, *join):
        do(RowStats(c, c.x), *join)
        out = tiles_of(c.big_b)

        def take(act, i, u, banks):
            return act.copy(out[:, tiles5(i, u), :], banks[0][:, 0:D].rearrange("p (a d) -> p a d", a=1))

        do(Project(c, D, D, W, normalise_from(c.x), take, "scalar", store=(out, c.table)))

    router_weights = c.w_area[:, 2048:2048 + 2 * EXPERTS].rearrange("p (b e) -> p b e", e=EXPERTS)
    b1_columns, b2_copies, b2_diagonal = c.w_area[:, 7000:7168], c.w_area[:, 3072:3328], c.w_area[:, 3328:4352]

    def load_ffn(H, router, bias_names, b1, b2, by_expert=False):
        pairs = [(b1_columns[:, 0:EXPERTS * H // P].rearrange("p (e m) -> p e m", e=EXPERTS),
                  T[b1].rearrange("e (m p) -> p e m", p=P))]
        pairs += [(b2_copies[k:k + EXPERTS, :], T[b2]) for k in range(0, P, EXPERTS)]
        if by_expert:
            pairs += [(router_weights[:, b, :], T[router][:, b * P:(b + 1) * P].rearrange("e p -> p e"))
                      for b in range(2)]
        else:
            pairs.append((router_weights, T[router].rearrange("(b p) e -> p b e", p=P)))
        biases = [c.w_area[:, 2112 + 16 * k:2112 + 16 * k + EXPERTS] for k in range(len(bias_names))]
        pairs += [(to, T[name].partition_broadcast(P)) for to, name in zip(biases, bias_names)]
        return do(Load(c, pairs)), biases

    def ffn(loaded, H, func, kind, src, affine, W1, W2, onto=True, own_too=False):
        out = x if onto else sums
        n = TILES * P
        columns = [[area[:, k * n:(k + 1) * n] for area, k in places] for places in
                   (((c.big_b_r, 0), (c.big_b_r, 1)), ((c.big_b_r, 2), (c.big_a_r, 2)))]
        load, biases = loaded
        br = biases[0] if biases else None
        if len(biases) == 2:
            do(Steps(c, lambda dve: iter([dve.tensor_tensor(br, biases[0], biases[1], ALU.add)])), load)

        def take(dve, i, u, banks):
            out = c.logits[:, tiles5(i, u), :]
            product = banks[0][:, 0:EXPERTS].rearrange("p (a e) -> p a e", a=1)
            if br is None:
                return dve.tensor_copy(out, product)
            return dve.tensor_tensor(out, product, br.rearrange("p (a e) -> p a e", a=1), ALU.add)

        do(Project(c, D, EXPERTS, router_weights, normalise_from(src), take, "vector", affine=affine,
                   keep_columns=columns), load)
        if own_too:
            do(AddOwnNormalised(c, x))
        do(Route(c, c.logits, kind))
        do(BiasStart(c, b2_copies, b2_diagonal, out, onto))
        do(Experts(c, columns, out, T[W1], b1_columns, T[W2], H, func, chosen=kind == "pooled"))

    do(Setup(c))
    by_src = do(SortPlan(c, "src", "src", "dst", "edge_weight", c.big_a[:, 10000:12800], 0))
    src_scatter = do(Scatter(c, by_src))
    do(ChunkTiles(c, by_src))
    whole = (TILES - 1) * P
    nodes = do(Load(c, [(c.x[:, 0:TILES - 1, :], T["x"][0:whole, :].rearrange("(t p) d -> p t d", p=P)),
                        (c.x[0:LAST, TILES - 1, :], T["x"][whole:NODES, :])]))
    by_dst = do(SortPlan(c, "dst", "dst", "src", None, c.big_b[:, 10000:12800], 32, made=by_src))
    do(ChunkTiles(c, by_dst))

    w0 = do(TurnWeights(c, T["L0_gnn_W"], D, D))
    project_nodes(w0.out, nodes)
    gain, shift = c.cols[:, 0:2], c.cols[:, 2:4]
    ffn0 = load_ffn(512, "L0_ffn_Wr", ["L0_ffn_br"], "L0_ffn_b1", "L0_ffn_b2")
    affine0 = do(Load(c, [by_partition("L0_ffn_gamma", 0, D), by_partition("L0_ffn_beta", 2, D)]))
    do(ReadSlots(c, by_src, src_scatter, c.big_a))
    do(GatherAdd(c, by_src, D, onto=x), affine0)
    dst_scatter = do(Scatter(c, by_dst))
    do(RowStats(c, c.x))
    do(Normalise(c, sums, x))
    do(RowStats(c, sums))
    ffn(ffn0, 512, ACT.Gelu, "softmax", sums, (gain, shift), "L0_ffn_W1", "L0_ffn_W2")

    w1 = do(TurnWeights(c, T["L1_gnn_W"].rearrange("h o k -> (h o) k"), D, D))
    affine1 = do(Load(c, [(c.vec[:, 0:D], T["L1_gnn_gamma"].rearrange("h o -> (h o)").partition_broadcast(P)),
                          (c.vec[:, D:2 * D], T["L1_gnn_beta"].rearrange("h o -> (h o)").partition_broadcast(P))]))
    project_nodes(w1.out)
    do(ReadSlots(c, by_dst, dst_scatter, c.big_a))
    last_in_chunk = c.last_in_chunk[:, :]

    def find_last(half):
        finder = LastEdge(c, by_src, c.big_b[:, 0:2000], c.big_b[:, 2000:6400], last_in_chunk,
                          half * CHUNKS // 2, CHUNKS // RING)
        return finder, do(Load(c, [(c.big_b[:, 0:CHUNKS * 4], by_src.slots[:, 0:CHUNKS * 4])]))

    last_edge, back = find_last(0)
    do(Steps(c, last_edge.prepare), back)
    ffn1 = load_ffn(512, "L1_ffn_Wr", ["L1_ffn_br"], "L1_ffn_b1", "L1_ffn_b2")
    gain1 = do(Load(c, [everywhere("L1_ffn_gamma", 2 * D, D), everywhere("L1_ffn_beta", 3 * D, D)]))
    with_degree = do(GatherAdd(c, by_dst, D, degree=True, beside=last_edge))
    do(BatchNorm(c, with_degree.sums, c.vec[:, 0:D], c.vec[:, D:2 * D]), affine1)
    do(RowStats(c, c.x))
    ffn(ffn1, 512, ACT.Gelu, "pooled", c.x, None, "L1_ffn_W1", "L1_ffn_W2", onto=False)
    other = tiles_of(c.big_b)
    do(Normalise(c, other, x))
    do(Steps(c, lambda dve: iter([dve.tensor_tensor(sums, sums, other, ALU.add)])))
    last_edge, back = find_last(1)
    do(RowStats(c, sums))
    do(AddNormed(c, x, sums, c.vec[:, 2 * D:3 * D], c.vec[:, 3 * D:4 * D]), gain1)

    do(RowStats(c, c.x))
    own = tiles_of(c.big_b, D, TILES * D)

    do(Steps(c, last_edge.prepare), back)
    do(Steps(c, lambda dve: iter([dve.tensor_tensor(c.rstd[:, :], c.rstd[:, :], c.dinv[:, :], ALU.mult)])))
    do(Normalise(c, own, x))
    do(StoreTable(c, own))
    conv1 = c.w_area[:, 0:2048].rearrange("p (b n) -> p b n", b=2)
    conv2 = c.w_area[:, 2048:6144].rearrange("p (b n) -> p b n", b=8)
    conv3 = c.w_area[:, 6144:7168].rearrange("p (b n) -> p b n", b=4)
    convs = do(Load(c, [(w, T[name].rearrange("(b p) n -> p b n", p=P)) for w, name in
                        ((conv1, "L2_gnn_W1"), (conv2, "L2_gnn_W2"), (conv3, "L2_gnn_W3"))]
                    + [everywhere("L2_gnn_b1", 0, 1024), everywhere("L2_gnn_b2", 1024, 512),
                       everywhere("L2_gnn_b3", 1536, D), everywhere("L2_gnn_g3", 1792, D),
                       everywhere("L2_gnn_beta3", 2048, D),
                       by_partition("L2_gnn_g1", 0, 1024), by_partition("L2_gnn_beta1", 8, 1024),
                       by_partition("L2_gnn_g2", 16, 512), by_partition("L2_gnn_beta2", 20, 512)]))
    do(Steps(c, lambda dve: iter([dve.tensor_copy(c.edge_value[:, :], by_src.tile_all)])))
    do(GatherAdd(c, by_dst, D, beside=last_edge))
    wide = tiles_of(c.big_b, 512)
    do(FirstConvolutions(c, sums, own, conv1, c.vec[:, 0:1024], conv2, c.cols[:, 0:8], c.cols[:, 8:16],
                         wide, c.wide_table), convs)
    wide_sums = do(GatherAdd(c, by_dst, 512)).sums
    third = tiles_of(c.big_b)

    def scale(act, i, u, banks):
        return act.activation(third[:, tiles5(i, u), :], banks[0][:, 0:D].rearrange("p (a d) -> p a d", a=1),
                              ACT.Identity, scale=c.dinv[:, tiles5(i, u)])

    holder = []
    prepare = PrepareSecond(c, lambda: holder[0], wide_sums, wide, c.vec[:, 1024:1536], 512)
    holder.append(do(Project(c, 512, D, conv3, lambda dve, i, u, to: prepare.between.normalise(dve, u, to), scale,
                             "scalar", affine=(c.cols[:, 16:20], c.cols[:, 20:24]), store=(third, c.table),
                             steps=prepare.steps, before_batch=prepare)))
    ffn2 = load_ffn(512, "L2_ffn_Wg", ["L2_ffn_bg", "L2_ffn_bias"], "L2_ffn_b1", "L2_ffn_b2")
    of_tiles = LastOfTiles(c, c.edge_value[:, :], c.big_b[:, 6400:6400 + CHUNKS])
    do(GatherAdd(c, by_dst, D, of_tiles=of_tiles, onto=third))
    last_rows = do(LastRows(c))

    do(EndConvolution(c, third, sums, c.vec[:, 1536:1792]))
    do(RowStats(c, sums))
    do(AddNormed(c, x, sums, c.vec[:, 1792:2048], c.vec[:, 2048:2304]))
    do(RowStats(c, c.x))
    ffn(ffn2, 512, ACT.Relu, "softmax", c.x, None, "L2_ffn_W1", "L2_ffn_W2")

    do(RowStats(c, c.x))
    do(Normalise(c, third, x))
    do(StoreTable(c, third))
    last_features = do(GatherLast(c, sums), last_rows)
    w3 = do(TurnWeights(c, T["L3_gnn_W"], D, 2 * D, [everywhere("L3_gnn_b", 0, D)]))
    ffn3 = load_ffn(256, "L3_ffn_router_w", [], "L3_ffn_b1", "L3_ffn_b2", by_expert=True)
    do(Steps(c, lambda dve: iter([dve.tensor_tensor(x, x, along(c.vec[:, 0:D], TILES), ALU.add)])))

    has_edge = c.stat_tmp[:, 0, 0:TILES]

    do(Steps(c, lambda dve: iter([dve.tensor_scalar(has_edge, c.last_edge[:, :], 0.0, None, ALU.is_gt)])))

    def beside(dve, i, u, to):
        to = to.rearrange("p (a d) -> p a d", a=1)
        dve.tensor_copy(to[:, :, 0:D], third[:, tiles5(i, u), :])
        return dve.tensor_scalar(to[:, :, D:2 * D], sums[:, tiles5(i, u), :], has_edge[:, tiles5(i, u)], None,
                                 ALU.mult)

    def add(dve, i, u, banks):
        tile = c.x[:, tiles5(i, u), :]
        return dve.tensor_tensor(tile, tile, banks[0][:, 0:D].rearrange("p (a d) -> p a d", a=1), ALU.add)

    do(Project(c, 2 * D, D, w3.out, beside, add, "vector"), last_features)
    do(RowStats(c, c.x))
    ffn(ffn3, 256, ACT.Gelu, "probs", c.x, None, "L3_ffn_w1", "L3_ffn_w2", own_too=True)
    do(Finish(c))
    return stages


_INS = [
    'x', 'src', 'dst', 'edge_weight', 'L0_gnn_W', 'L0_ffn_gamma', 'L0_ffn_beta', 'L0_ffn_Wr', 'L0_ffn_br',
    'L0_ffn_W1', 'L0_ffn_b1', 'L0_ffn_W2', 'L0_ffn_b2', 'L1_gnn_W', 'L1_gnn_gamma', 'L1_gnn_beta', 'L1_ffn_Wr',
    'L1_ffn_br', 'L1_ffn_W1', 'L1_ffn_b1', 'L1_ffn_W2', 'L1_ffn_b2', 'L1_ffn_gamma', 'L1_ffn_beta', 'L2_gnn_W1',
    'L2_gnn_b1', 'L2_gnn_g1', 'L2_gnn_beta1', 'L2_gnn_W2', 'L2_gnn_b2', 'L2_gnn_g2', 'L2_gnn_beta2', 'L2_gnn_W3',
    'L2_gnn_b3', 'L2_gnn_g3', 'L2_gnn_beta3', 'L2_ffn_Wg', 'L2_ffn_bg', 'L2_ffn_bias', 'L2_ffn_W1', 'L2_ffn_b1',
    'L2_ffn_W2', 'L2_ffn_b2', 'L3_gnn_W', 'L3_gnn_b', 'L3_ffn_router_w', 'L3_ffn_w1', 'L3_ffn_b1', 'L3_ffn_w2',
    'L3_ffn_b2',
]
_OUTS = [((NODES, D), 'float32')]


def kernel(**inputs):
    import numpy as _np
    import concourse.bacc as _bacc
    from concourse import mybir as _mybir
    from concourse.bass_utils import run_bass_kernel_spmd as _run

    nc = _bacc.Bacc("TRN2", target_bir_lowering=False, num_devices=1)
    arrays, T = {}, {}
    for name in _INS:
        a = _np.ascontiguousarray(inputs[name])
        arrays[f"in_{name}_dram"] = a
        T[name] = nc.dram_tensor(f"in_{name}_dram", a.shape, _mybir.dt.from_np(a.dtype), kind="ExternalInput").ap()
    outs = [nc.dram_tensor(f"out_{i}_dram", shape, _mybir.dt.from_np(_np.dtype(dtype)), kind="ExternalOutput").ap()
            for i, (shape, dtype) in enumerate(_OUTS)]
    gnn_ffn_layers(nc, T, outs[0], network)
    r = _run(nc, [arrays], core_ids=[0])
    return r.results[0]["out_0_dram"]
```
